# Optimizing a Trainium2 kernel written in Bass

```python
import numpy as np
import jax
import jax.numpy as jnp

def _softmax(x, axis=-1):
    return jax.nn.softmax(x, axis=axis)

def _gelu(x):
    return jax.nn.gelu(x, approximate=True)

def _silu(x):
    return jax.nn.silu(x)

def _sigmoid(x):
    return jax.nn.sigmoid(x)

def _layernorm(x, axis=-1, eps=1e-05):
    m = jnp.mean(x, axis=axis, keepdims=True)
    v = jnp.var(x, axis=axis, keepdims=True)
    return (x - m) / jnp.sqrt(v + eps)

def _scatter_add(tgt, idx, src, axis=0):
    return tgt.at[idx].add(src)

def _segment_sum(src, seg, n):
    return jax.ops.segment_sum(src, seg, n)
kernel_name = 'mk_macaron_d1_jaxref_r4_02c34a'

def setup_inputs(seed: int=0):
    np.random.seed(seed)
    _w = jnp.asarray

    def _L0_attn_setup():
        import jax, jax.numpy as jnp
        import numpy as np
        from jax.scipy.linalg import solve_triangular
        B, L, HID, NH = (2, 256, 256, 4)
        DK = DV = 64
        CONV_K, CHUNK, FIR_S_K, FIR_L_K = (4, 32, 3, 31)
        GATE_IN = HID + 3 * DV * 4 + DV * 4
        GATE_H = 2 * DV

        def _l2norm(x):
            return x * jax.lax.rsqrt(jnp.sum(x * x, -1, keepdims=True) + 1e-06)

        def _short_conv(x, w):
            c, k = w.shape
            y = jax.lax.conv_general_dilated(x.transpose(0, 2, 1), w[:, None, :], (1,), [(k - 1, 0)], feature_group_count=c)
            return jax.nn.silu(y.transpose(0, 2, 1))

        def _fir(x, f):
            b, l, h, d = x.shape
            k = f.shape[-1]
            xf = x.transpose(0, 2, 3, 1).reshape(b, h * d, l)
            y = jax.lax.conv_general_dilated(xf, f.reshape(h * d, 1, k), (1,), [(k - 1, 0)], feature_group_count=h * d)
            return y.reshape(b, h, d, l).transpose(0, 3, 1, 2)

        def _delta_rule(q, k, v, beta, chunk=CHUNK):
            b, h, l, dk = q.shape
            dv = v.shape[-1]
            n = l // chunk
            q = _l2norm(q)
            k = _l2norm(k)
            v = v * beta[..., None]
            kb = k * beta[..., None]
            rs = lambda t: t.reshape(b, h, n, chunk, -1)
            q, k, v, kb = map(rs, (q, k, v, kb))
            A = -jnp.tril(jnp.einsum('bhncd,bhned->bhnce', kb, k), -1)
            eye = jnp.eye(chunk, dtype=q.dtype)
            T = solve_triangular(eye - A, jnp.broadcast_to(eye, A.shape), lower=True)
            u = T @ v
            w = T @ kb
            mov = lambda t: jnp.moveaxis(t, 2, 0)

            def step(S, inp):
                qi, ki, ui, wi = inp
                attn = jnp.tril(qi @ ki.transpose(0, 1, 3, 2))
                u_i = ui - wi @ S
                o_i = qi @ S + attn @ u_i
                return (S + ki.transpose(0, 1, 3, 2) @ u_i, o_i)
            S0 = jnp.zeros((b, h, dk, dv), dtype=q.dtype)
            S, o = jax.lax.scan(step, S0, (mov(q), mov(k), mov(u), mov(w)))
            o = jnp.moveaxis(o, 0, 2).reshape(b, h, l, dv)
            return (o, S)

        def _gate(hidden, branches, W1, b1, W2, b2, temp, eps_floor):

            def stats(p):
                m = p.mean(-1, keepdims=True)
                r = jnp.sqrt(jnp.clip((p * p).mean(-1, keepdims=True), 1e-08))
                mx = p.max(-1, keepdims=True)
                return jnp.concatenate([jnp.broadcast_to(m, p.shape), jnp.broadcast_to(r, p.shape), jnp.broadcast_to(mx, p.shape)], -1)
            b, l, h, d = branches[0].shape
            hb = jnp.broadcast_to(hidden[:, :, None, :], (b, l, h, hidden.shape[-1]))
            head_in = jnp.concatenate([hb] + [stats(p) for p in branches] + list(branches), -1)
            hmid = jax.nn.gelu(head_in @ W1 + b1, approximate=False)
            logits = hmid @ W2 + b2
            t = jnp.clip(temp, 0.2, 10.0)[None, None, :, None]
            w = jax.nn.softmax(logits / t, -1)
            floor = jnp.clip(eps_floor, 1e-07, 0.1)[None, None]
            w = jnp.maximum(w, floor)
            return w / w.sum(-1, keepdims=True)
        key = jax.random.key(seed)
        ks = jax.random.split(key, 16)
        s = 0.02
        inp = {'x': jax.random.normal(ks[0], (B, L, HID), jnp.float32), 'Wq': jax.random.normal(ks[1], (HID, NH * DK), jnp.float32) * s, 'Wk': jax.random.normal(ks[2], (HID, NH * DK), jnp.float32) * s, 'Wv': jax.random.normal(ks[3], (HID, NH * DV), jnp.float32) * s, 'Wb': jax.random.normal(ks[4], (HID, NH), jnp.float32) * s, 'qc_w': jax.random.normal(ks[5], (NH * DK, CONV_K), jnp.float32) * 0.5, 'kc_w': jax.random.normal(ks[6], (NH * DK, CONV_K), jnp.float32) * 0.5, 'vc_w': jax.random.normal(ks[7], (NH * DV, CONV_K), jnp.float32) * 0.5, 'gW1': jax.random.normal(ks[10], (GATE_IN, GATE_H), jnp.float32) * s, 'gb1': jnp.zeros((GATE_H,), jnp.float32), 'gW2': jax.random.normal(ks[11], (GATE_H, 4), jnp.float32) * s, 'gb2': jnp.zeros((4,), jnp.float32), 'temp': jnp.ones((NH,), jnp.float32), 'eps_floor': jnp.full((NH, 4), 0.01, jnp.float32), 'onorm_w': jnp.ones((DV,), jnp.float32), 'Wo': jax.random.normal(ks[12], (NH * DV, HID), jnp.float32) * s}
        fs = jnp.zeros((NH, DV, FIR_S_K)).at[..., -1].set(1.0)
        fl = jnp.zeros((NH, DV, FIR_L_K)).at[..., -1].set(1.0)
        inp['fir_s'] = fs + s * jax.random.normal(ks[8], fs.shape, jnp.float32)
        inp['fir_l'] = fl + s * jax.random.normal(ks[9], fl.shape, jnp.float32)
        return inp
    _L0_attn_in = _L0_attn_setup()

    def _L0_ffn_setup():
        import jax, jax.numpy as jnp
        import numpy as np
        N_EMBD = 256
        N_STATE = 1024
        key = jax.random.key(seed)
        k_x, k_w1, k_b1, k_w2, k_b2 = jax.random.split(key, 5)
        x = jax.random.normal(k_x, (4, 512, N_EMBD), dtype=jnp.float32)
        w1 = jax.random.normal(k_w1, (N_EMBD, N_STATE), dtype=jnp.float32) * (1.0 / np.sqrt(N_EMBD))
        b1 = jax.random.normal(k_b1, (N_STATE,), dtype=jnp.float32) * 0.02
        w2 = jax.random.normal(k_w2, (N_STATE, N_EMBD), dtype=jnp.float32) * (1.0 / np.sqrt(N_STATE))
        b2 = jax.random.normal(k_b2, (N_EMBD,), dtype=jnp.float32) * 0.02
        return {'x': x, 'w1': w1, 'b1': b1, 'w2': w2, 'b2': b2}
    _L0_ffn_in = _L0_ffn_setup()
    _d = {'L0_attn_x': _L0_attn_in['x'], 'L0_attn_Wq': _L0_attn_in['Wq'], 'L0_attn_Wk': _L0_attn_in['Wk'], 'L0_attn_Wv': _L0_attn_in['Wv'], 'L0_attn_Wb': _L0_attn_in['Wb'], 'L0_attn_qc_w': _L0_attn_in['qc_w'], 'L0_attn_kc_w': _L0_attn_in['kc_w'], 'L0_attn_vc_w': _L0_attn_in['vc_w'], 'L0_attn_fir_s': _L0_attn_in['fir_s'], 'L0_attn_fir_l': _L0_attn_in['fir_l'], 'L0_attn_gW1': _L0_attn_in['gW1'], 'L0_attn_gb1': _L0_attn_in['gb1'], 'L0_attn_gW2': _L0_attn_in['gW2'], 'L0_attn_gb2': _L0_attn_in['gb2'], 'L0_attn_temp': _L0_attn_in['temp'], 'L0_attn_eps_floor': _L0_attn_in['eps_floor'], 'L0_attn_onorm_w': _L0_attn_in['onorm_w'], 'L0_attn_Wo': _L0_attn_in['Wo'], 'L0_ffn_w1': _L0_ffn_in['w1'], 'L0_ffn_b1': _L0_ffn_in['b1'], 'L0_ffn_w2': _L0_ffn_in['w2'], 'L0_ffn_b2': _L0_ffn_in['b2']}
    _x0 = _d['L0_attn_x']
    _d['L0_attn_x'] = jax.random.normal(jax.random.fold_in(jax.random.key(seed), 1), (8, 512, 256), dtype=_x0.dtype)
    del _x0
    return _d

def reference(L0_attn_x, L0_attn_Wq, L0_attn_Wk, L0_attn_Wv, L0_attn_Wb, L0_attn_qc_w, L0_attn_kc_w, L0_attn_vc_w, L0_attn_fir_s, L0_attn_fir_l, L0_attn_gW1, L0_attn_gb1, L0_attn_gW2, L0_attn_gb2, L0_attn_temp, L0_attn_eps_floor, L0_attn_onorm_w, L0_attn_Wo, L0_ffn_w1, L0_ffn_b1, L0_ffn_w2, L0_ffn_b2):

    def _L0_attn_ref(x, Wq, Wk, Wv, Wb, qc_w, kc_w, vc_w, fir_s, fir_l, gW1, gb1, gW2, gb2, temp, eps_floor, onorm_w, Wo):
        import jax, jax.numpy as jnp
        import numpy as np
        from jax.scipy.linalg import solve_triangular
        B, L, HID, NH = (2, 256, 256, 4)
        DK = DV = 64
        CONV_K, CHUNK, FIR_S_K, FIR_L_K = (4, 32, 3, 31)
        GATE_IN = HID + 3 * DV * 4 + DV * 4
        GATE_H = 2 * DV

        def _l2norm(x):
            return x * jax.lax.rsqrt(jnp.sum(x * x, -1, keepdims=True) + 1e-06)

        def _short_conv(x, w):
            c, k = w.shape
            y = jax.lax.conv_general_dilated(x.transpose(0, 2, 1), w[:, None, :], (1,), [(k - 1, 0)], feature_group_count=c)
            return jax.nn.silu(y.transpose(0, 2, 1))

        def _fir(x, f):
            b, l, h, d = x.shape
            k = f.shape[-1]
            xf = x.transpose(0, 2, 3, 1).reshape(b, h * d, l)
            y = jax.lax.conv_general_dilated(xf, f.reshape(h * d, 1, k), (1,), [(k - 1, 0)], feature_group_count=h * d)
            return y.reshape(b, h, d, l).transpose(0, 3, 1, 2)

        def _delta_rule(q, k, v, beta, chunk=CHUNK):
            b, h, l, dk = q.shape
            dv = v.shape[-1]
            n = l // chunk
            q = _l2norm(q)
            k = _l2norm(k)
            v = v * beta[..., None]
            kb = k * beta[..., None]
            rs = lambda t: t.reshape(b, h, n, chunk, -1)
            q, k, v, kb = map(rs, (q, k, v, kb))
            A = -jnp.tril(jnp.einsum('bhncd,bhned->bhnce', kb, k), -1)
            eye = jnp.eye(chunk, dtype=q.dtype)
            T = solve_triangular(eye - A, jnp.broadcast_to(eye, A.shape), lower=True)
            u = T @ v
            w = T @ kb
            mov = lambda t: jnp.moveaxis(t, 2, 0)

            def step(S, inp):
                qi, ki, ui, wi = inp
                attn = jnp.tril(qi @ ki.transpose(0, 1, 3, 2))
                u_i = ui - wi @ S
                o_i = qi @ S + attn @ u_i
                return (S + ki.transpose(0, 1, 3, 2) @ u_i, o_i)
            S0 = jnp.zeros((b, h, dk, dv), dtype=q.dtype)
            S, o = jax.lax.scan(step, S0, (mov(q), mov(k), mov(u), mov(w)))
            o = jnp.moveaxis(o, 0, 2).reshape(b, h, l, dv)
            return (o, S)

        def _gate(hidden, branches, W1, b1, W2, b2, temp, eps_floor):

            def stats(p):
                m = p.mean(-1, keepdims=True)
                r = jnp.sqrt(jnp.clip((p * p).mean(-1, keepdims=True), 1e-08))
                mx = p.max(-1, keepdims=True)
                return jnp.concatenate([jnp.broadcast_to(m, p.shape), jnp.broadcast_to(r, p.shape), jnp.broadcast_to(mx, p.shape)], -1)
            b, l, h, d = branches[0].shape
            hb = jnp.broadcast_to(hidden[:, :, None, :], (b, l, h, hidden.shape[-1]))
            head_in = jnp.concatenate([hb] + [stats(p) for p in branches] + list(branches), -1)
            hmid = jax.nn.gelu(head_in @ W1 + b1, approximate=False)
            logits = hmid @ W2 + b2
            t = jnp.clip(temp, 0.2, 10.0)[None, None, :, None]
            w = jax.nn.softmax(logits / t, -1)
            floor = jnp.clip(eps_floor, 1e-07, 0.1)[None, None]
            w = jnp.maximum(w, floor)
            return w / w.sum(-1, keepdims=True)
        b, l, _ = x.shape
        q = _short_conv(x @ Wq, qc_w).reshape(b, l, NH, DK)
        k = _short_conv(x @ Wk, kc_w).reshape(b, l, NH, DK)
        v = _short_conv(x @ Wv, vc_w).reshape(b, l, NH, DV)
        beta = jax.nn.sigmoid(x @ Wb)
        tr = lambda t: t.transpose(0, 2, 1, 3)
        delta_o, _ = _delta_rule(tr(q), tr(k), tr(v), beta.transpose(0, 2, 1))
        delta_o = tr(delta_o)
        branches = [_fir(v, fir_s), _fir(v, fir_l), delta_o, v]
        w = _gate(x, branches, gW1, gb1, gW2, gb2, temp, eps_floor)
        o = sum((w[..., i:i + 1] * branches[i] for i in range(4)))
        o = o * jax.lax.rsqrt((o * o).mean(-1, keepdims=True) + 1e-05) * onorm_w
        return o.reshape(b, l, NH * DV) @ Wo

    def _L0_ffn_ref(x, w1, b1, w2, b2):
        import jax, jax.numpy as jnp
        import numpy as np
        N_EMBD = 256
        N_STATE = 1024
        h = jax.nn.gelu(jnp.einsum('bse,eh->bsh', x, w1) + b1, approximate=False)
        return jnp.einsum('bsh,he->bse', h, w2) + b2
    x = L0_attn_x
    x = x + 0.5 * _L0_ffn_ref(_layernorm(x, axis=-1), L0_ffn_w1, L0_ffn_b1, L0_ffn_w2, L0_ffn_b2)
    x = x + _L0_attn_ref(_layernorm(x, axis=-1), L0_attn_Wq, L0_attn_Wk, L0_attn_Wv, L0_attn_Wb, L0_attn_qc_w, L0_attn_kc_w, L0_attn_vc_w, L0_attn_fir_s, L0_attn_fir_l, L0_attn_gW1, L0_attn_gb1, L0_attn_gW2, L0_attn_gb2, L0_attn_temp, L0_attn_eps_floor, L0_attn_onorm_w, L0_attn_Wo)
    x = x + 0.5 * _L0_ffn_ref(_layernorm(x, axis=-1), L0_ffn_w1, L0_ffn_b1, L0_ffn_w2, L0_ffn_b2)
    return x

_drawn_inputs = setup_inputs


def setup_inputs(seed=0):
    import zlib

    import numpy as np

    out = dict(_drawn_inputs(seed))
    spreads = {'L0_attn_gb1': (0.0, 0.8),
     'L0_attn_gb2': (0.0, 0.8),
     'L0_attn_temp': (1.0, 0.6),
     'L0_attn_eps_floor': (0.009999999776482582, 0.2),
     'L0_attn_onorm_w': (1.0, 0.2)}
    factors = {'L0_attn_Wb': 8.0,
     'L0_attn_gW1': 8.0,
     'L0_attn_gW2': 8.0,
     'L0_ffn_b1': 5.113,
     'L0_ffn_b2': 3.451}
    for name, (base, spread) in spreads.items():
        noise = np.random.default_rng([zlib.crc32(name.encode()), seed]).standard_normal(out[name].shape)
        drawn = base * np.exp(spread * noise) if base else spread * noise
        out[name] = jnp.asarray(drawn.astype(out[name].dtype))
    for name, factor in factors.items():
        out[name] = (out[name] * factor).astype(out[name].dtype)
    return out
```

```python
from contextlib import ExitStack

import concourse.bass as bass
from concourse import mybir

F32 = mybir.dt.float32
F32R = mybir.dt.float32r
ALU = mybir.AluOpType
ACT = mybir.ActivationFunctionType
AX = mybir.AxisListType

SEQS, T, C = 8, 512, 256
P = 128
TILES = T // P
HALVES = C // P
HEADS, D = 4, 64
HID = 1024
KT = HID // P
CHUNK = 32
CPT = P // CHUNK
UNITS = TILES * HEADS
BR = 4
CONV = 4
GROUPS = C // 32
LONG, SHORT = 31, 3
TAPG = 8
PAD = 4 * (TAPG - 1)
RAWS = 3
RING = 3


def macaron_kernel(nc, x, Wq, Wk, Wv, Wb, qc_w, kc_w, vc_w, fir_s, fir_l, gW1, gb1, gW2, gb2,
                   temp, eps_floor, onorm_w, Wo, w1, b1, w2, b2, out):
    ctx = ExitStack()
    with ctx:
        def sb(name, shape, dt=F32):
            return ctx.enter_context(nc.sbuf_tensor(name, shape, dt))

        def sem(name):
            return ctx.enter_context(nc.semaphore(name))

        l_dram = nc.dram_tensor("l_dram", [CPT, CHUNK, UNITS, CHUNK], F32, kind="Internal").ap()
        t_dram = nc.dram_tensor("t_dram", [CPT, UNITS, CHUNK, CHUNK], F32, kind="Internal").ap()
        v_dram = nc.dram_tensor("v_dram", [HALVES, P, T], F32, kind="Internal").ap()

        ident = sb("ident", [P, P])
        low_strict = sb("low_strict", [P, CHUNK])
        up_incl = sb("up_incl", [P, CHUNK])
        eye32 = sb("eye32", [P, CHUNK])
        w1_hi, w1_lo = sb("w1_hi", [P, HALVES, HID], F32R), sb("w1_lo", [P, HALVES, HID], F32R)
        w2_hi, w2_lo = sb("w2_hi", [P, KT, C], F32R), sb("w2_lo", [P, KT, C], F32R)
        wqkv_hi, wqkv_lo = sb("wqkv_hi", [P, 3, HALVES, C], F32R), sb("wqkv_lo", [P, 3, HALVES, C], F32R)
        wo_hi, wo_lo = sb("wo_hi", [P, HALVES, C], F32R), sb("wo_lo", [P, HALVES, C], F32R)
        wh_hi, wh_lo = sb("wh_hi", [P, HALVES, P], F32R), sb("wh_lo", [P, HALVES, P], F32R)
        b1_col = sb("b1_col", [P, KT])
        b2_half = sb("b2_half", [P, C])
        wb_pad = sb("wb_pad", [P, HALVES, 32])
        conv_col = sb("conv_col", [P, 3, HALVES, CONV])
        taps_l, taps_s = sb("taps_l", [P, GROUPS, LONG + 1]), sb("taps_s", [P, GROUPS, CONV])
        fir_w = sb("fir_w", [P, GROUPS, TAPG + 1, 32])
        gate_br = sb("gate_br", [P, BR, P])
        stat_sel = sb("stat_sel", [D, 2 * BR, 32])
        mean_ones = sb("mean_ones", [D, P])
        stat_all = sb("stat_all", [32, P])
        head_mask = sb("head_mask", [32, HEADS])
        gate_st = sb("gate_st", [32, HEADS, P])
        gb1_col = sb("gb1_col", [P, 1])
        w2g_pad = sb("w2g_pad", [P, 32])
        temp_col, tinv_col, gb2_col, gbt_col = (sb(n, [P, 1]) for n in ("temp_col", "tinv_col", "gb2_col", "gbt_col"))
        floor_b = sb("floor_b", [P, HEADS, BR])
        onorm_col = sb("onorm_col", [P, 1])

        arena = sb("arena", [P, 8, TILES * C])

        def tok(n):
            return arena[:, n, :].rearrange("p (t c) -> p t c", t=TILES)

        def heads(n):
            return arena[:, n, :].rearrange("p (u d) -> p u d", u=UNITS)

        K_TOK, V_TOK, FS_TOK, FL_TOK, DL_TOK, MIX, TMP, SQ = range(8)
        flat = arena[:, :, :].rearrange("p a b -> p (a b)")
        w1_st = flat[:, 0:2048].rearrange("p (k n) -> p k n", k=HALVES)
        w2_st = flat[:, 2048:4096].rearrange("p (k n) -> p k n", k=KT)
        wqkv_st = flat[:, 4096:5632].rearrange("p (w k n) -> p w k n", w=3, k=HALVES)
        wo_st = flat[:, 5632:6144].rearrange("p (k n) -> p k n", k=HALVES)
        wh_st = flat[:, 6144:6400].rearrange("p (k n) -> p k n", k=HALVES)
        b2_st = flat[:, 6400:6656]
        stat_rows = flat[0:D, 6656:8192].rearrange("d (s n) -> d s n", s=3 * BR)

        x_tok = sb("x_tok", [P, TILES, C])
        xb_tok = sb("xb_tok", [P, TILES, C])
        x1_tok = sb("x1_tok", [P, TILES, C])
        xn_tok = tok(SQ)
        xt_hi, xt_lo = sb("xt_hi", [P, HALVES, T], F32R), sb("xt_lo", [P, HALVES, T], F32R)
        bn = sb("bn", [P, TILES, 6])
        mv = sb("mv", [P, TILES, 2])
        std = sb("std", [P, TILES])
        rstd = sb("rstd", [P, TILES])
        h_f = sb("h_f", [P, 2, T])
        h_hi, h_lo = sb("h_hi", [P, RING, T], F32R), sb("h_lo", [P, RING, T], F32R)
        raw = sb("raw", [P, RAWS, CONV - 1 + T])
        conv_acc = sb("conv_acc", [P, 2, T])
        qk_fm = sb("qk_fm", [P, HALVES, 2, T])
        v_fm = sb("v_fm", [P, HALVES, T])
        v_shift = sb("v_shift", [P, GROUPS, PAD + T])
        fs_fm, fl_fm = (sb(n, [P, HALVES, T]) for n in ("fs_fm", "fl_fm"))
        lg_fm = sb("lg_fm", [P, T])
        beta_rows = lg_fm[0:32, :]
        beta_tok = sb("beta_tok", [P, TILES, HEADS])
        ssq = sb("ssq", [P, 2, UNITS])
        nrm = sb("nrm", [P, 2, UNITS])
        inv = sb("inv", [P, 2, UNITS])
        c1, c2n = sb("c1", [P, UNITS]), sb("c2n", [P, UNITS])
        l_tok = sb("l_tok", [P, UNITS, CHUNK])
        at_tok = sb("at_tok", [P, UNITS, CHUNK])
        l_inv, l_prod = (arena[0:CPT * UNITS, n, :].rearrange("p (i j) -> p i j", i=CHUNK) for n in (MIX, TMP))
        t_tok = sb("t_tok", [P, UNITS, CHUNK])
        u_t = l_tok
        u1, u2n = sb("u1", [P, UNITS, CHUNK]), sb("u2n", [P, UNITS, CHUNK])
        w_fm = sb("w_fm", [P, HALVES, T])
        dl_fm = w_fm
        s_sb = sb("s_sb", [P, HALVES, D])
        du = sb("du", [P, 2, HALVES, D])
        stats = sb("stats", [P, TILES, 2, BR, HEADS])
        stat_fm = sb("stat_fm", [32, T])
        hid_fm = sb("hid_fm", [P, T])
        pre, hm = h_f, conv_acc
        lg = sb("lg", [P, UNITS, BR])
        lmax, lsum, linv = (sb(n, [P, UNITS]) for n in ("lmax", "lsum", "linv"))
        mix_w = sb("mix_w", [P, UNITS, BR])
        oss, onrm, oinv = (sb(n, [P, UNITS]) for n in ("oss", "onrm", "oinv"))

        psum = ctx.enter_context(nc.psum_tensor("psum", [P, 8, 512], F32))
        BANKS = [psum[:, n, :] for n in range(8)]
        TR0, TR1, AC0, AC1, AC2, OW0, OW1, ST = range(8)
        filled = [sem(f"filled{n}") for n in range(8)]
        emptied = [sem(f"emptied{n}") for n in range(8)]

        USES = []
        for f in range(2):
            if f == 1:
                USES += [("ln2", TR0, 2), ("ln2", TR1, 2)]
                USES += [("qkv", (AC0, AC1, AC2)[m % 3], 1) for m in range(6)]
                USES += [("beta", TR0, 1), ("hidden", AC0, 1)]
                USES += [("beta_t", TR1, 1)]
                USES += [("k_t", TR0, 1), ("k_t", TR1, 1), ("q_t", TR0, 1), ("q_t", TR1, 1)]
                USES += [("gram", AC1, 1), ("gram", AC2, 1)]
                USES += [("v_t", TR0, 1), ("v_t", TR1, 1)]
                USES += [("fir_s", AC0, 1), ("fir_s", AC1, 1), ("fir_l", AC2, 1), ("fir_l", AC0, 1)]
                USES += [("fs_t", TR0, 1), ("fs_t", TR1, 1), ("fl_t", TR0, 1), ("fl_t", TR1, 1)]
                USES += [("w", b, 1) for b in (AC1, AC2, OW0, OW1)]
                USES += [("du", OW0, 1), ("du", OW1, 1)]
                USES += [("o", b, 1) for b in (AC0, AC1, TR0, TR1) * 2]
                USES += [("dl_t", TR0, 1), ("dl_t", TR1, 1), ("stat_t", TR0, 1)]
                USES += [("gate", (AC0, AC1)[h % 2], 1) for h in range(HEADS)]
                USES += [("logit", AC2, 1), ("logit_t", TR1, 1)]
                USES += [("mix_t", TR0, 2), ("mix_t", TR1, 2)]
                USES += [("wo", OW0, 1), ("wo", OW1, 1)]
            USES += [(f"lnf{f}", TR0, 2), (f"lnf{f}", TR1, 2)]
            USES += [(f"ffn{f}", (AC0, AC1, AC2)[m % 3], 1) for m in range(KT)]
            USES += [(f"ffo{f}", OW0, 1), (f"ffo{f}", OW1, 1)]
        FILLS = [sum(b == n and w != "du" for w, b, _ in USES) for n in range(8)]
        READS = [sum(r for _, b, r in USES if b == n) for n in range(8)]

        def use(what, k):
            n = [n for n, u in enumerate(USES) if u[0] == what][k]
            b = USES[n][1]
            return b, sum(u[1] == b and u[0] != "du" for u in USES[:n]), sum(u[2] for u in USES[:n] if u[1] == b)

        def claim(pe, i, what, k=0):
            b, _, reads = use(what, k)
            pe.wait_ge(emptied[b], i * READS[b] + reads + 1)
            return BANKS[b], filled[b]

        def arrive(eng, i, what, k=0):
            b, fills, _ = use(what, k)
            eng.wait_ge(filled[b], i * FILLS[b] + fills + 1)
            return BANKS[b], emptied[b]

        w_loaded = sem("w_loaded")
        c_loaded = sem("c_loaded")
        const_made = sem("const_made")
        setup_pe = sem("setup_pe")
        setup_dve = sem("setup_dve")
        x_loaded = sem("x_loaded")
        y_stored = sem("y_stored")
        xb_made = sem("xb_made")
        var_made = sem("var_made")
        std_made = sem("std_made")
        xn_made = sem("xn_made")
        xhi_made = sem("xhi_made")
        xt_made = sem("xt_made")
        gelu_made = sem("gelu_made")
        h_split = sem("h_split")
        h_used = sem("h_used")
        res_made = sem("res_made")
        raw_made = sem("raw_made")
        conv_made = sem("conv_made")
        silu_made = sem("silu_made")
        v_stored = sem("v_stored")
        v_shifted = sem("v_shifted")
        beta_made = sem("beta_made")
        tok_made = sem("tok_made")
        hid_made = sem("hid_made")
        sq_made = sem("sq_made")
        sq_used = sem("sq_used")
        ssq_made = sem("ssq_made")
        root_made = sem("root_made")
        l_made = sem("l_made")
        at_made = sem("at_made")
        l_stored = sem("l_stored")
        l_loaded = sem("l_loaded")
        t_stored = sem("t_stored")
        t_loaded = sem("t_loaded")
        u_made = sem("u_made")
        fir_made = sem("fir_made")
        w_made = sem("w_made")
        du_ready = sem("du_ready")
        du_made = sem("du_made")
        s_ready = sem("s_ready")
        s_made = sem("s_made")
        dl_made = sem("dl_made")
        dlt_made = sem("dlt_made")
        stats_made = sem("stats_made")
        statt_made = sem("statt_made")
        pre_made = sem("pre_made")
        hm_made = sem("hm_made")
        hm_used = sem("hm_used")
        lg_made = sem("lg_made")
        lshift_made = sem("lshift_made")
        exp_made = sem("exp_made")
        mix_made = sem("mix_made")
        norm_made = sem("norm_made")
        omix_hi = sem("omix_hi")
        omix_lo = sem("omix_lo")
        passed = sem("passed")
        dve_step = sem("dve_step")
        pool_step = sem("pool_step")
        DVE_STEPS, POOL_STEPS = 68, 60
        CONST_MADE, C_LOADED, SETUP_DVE = 43, 29, 30

        x_v = x.rearrange("b (t p) c -> b p t c", p=P)
        out_v = out.rearrange("b (t p) c -> b p t c", p=P)

        block = ctx.enter_context(nc.Block())

        def row_bcast(ap, n=P):
            return ap.partition_broadcast(n)

        @block.sync
        def _(sp):
            sp.dma_start(w1_st, w1.rearrange("(k p) n -> p k n", p=P)).then_inc(w_loaded, 16)
            sp.dma_start(w2_st, w2.rearrange("(k p) n -> p k n", p=P)).then_inc(w_loaded, 16)
            for n, w in enumerate((Wk, Wq, Wv)):
                sp.dma_start(wqkv_st[:, n], w.rearrange("(k p) n -> p k n", p=P)).then_inc(w_loaded, 16)
            sp.dma_start(wo_st, Wo.rearrange("(k p) n -> p k n", p=P)).then_inc(w_loaded, 16)
            sp.dma_start(wh_st, gW1[0:C, :].rearrange("(k p) n -> p k n", p=P)).then_inc(w_loaded, 16)
            sp.dma_start(b2_st, row_bcast(b2)).then_inc(w_loaded, 16)
            sp.sem_inc(y_stored, 1)
            with sp.Fori(0, SEQS) as i:
                sp.wait_ge(y_stored, i * 16 + 1)
                sp.dma_start(x_tok[:, :, :], x_v[bass.ds(i, 1)].rearrange("a p t c -> (a p) t c")).then_inc(x_loaded, 16)
                sp.wait_ge(silu_made, i * 6 + 6)
                sp.dma_start(v_dram.rearrange("h p t -> p h t"), v_fm[:, :, :]).then_inc(v_stored, 16)
                sp.wait_ge(v_stored, i * 16 + 16)
                for s in range(CONV):
                    sp.dma_start(v_shift[32 * s:32 * s + 32, :, PAD + s:PAD + T],
                                 v_dram.rearrange("h (g c) t -> c (h g) t", c=32)[:, :, 0:T - s]).then_inc(v_shifted, 16)
                sp.wait_ge(l_made, i + 1)
                sp.dma_start(l_dram.rearrange("c i u j -> (c i) u j"), l_tok[:, :, :]).then_inc(l_stored, 16)
                sp.wait_ge(l_stored, i * 16 + 16)
                for c in range(CPT):
                    sp.dma_start(l_inv[UNITS * c:UNITS * c + UNITS, :, :],
                                 l_dram[c].rearrange("i u j -> u i j")).then_inc(l_loaded, 16)
                sp.wait_ge(pool_step, i * POOL_STEPS + POOL_STEPS)
                sp.dma_start(t_dram.rearrange("c u i j -> (c u) i j"), l_inv[:, :, :]).then_inc(t_stored, 16)
                sp.wait_ge(t_stored, i * 16 + 16)
                for c in range(CPT):
                    sp.dma_start(t_tok[32 * c:32 * c + 32, :, :], t_dram[c].rearrange("u i j -> i u j")).then_inc(t_loaded, 16)
                sp.wait_ge(res_made, i * 6 + 6)
                sp.dma_start(out_v[bass.ds(i, 1)].rearrange("a p t c -> (a p) t c"), x_tok[:, :, :]).then_inc(y_stored, 16)
            sp.wait_ge(y_stored, SEQS * 16 + 1)

        @block.gpsimd
        def _(pool):
            pool.memset(taps_l[:, :, :], 0.0).then_inc(const_made, 1)
            pool.memset(taps_s[:, :, :], 0.0).then_inc(const_made, 1)
            pool.wait_ge(const_made, 2)
            pool.dma_start(b1_col[:, :], b1.rearrange("(k p) -> p k", p=P), allow_slow_non_contiguous=True).then_inc(c_loaded, 16)
            pool.dma_start(gb1_col[:, :], gb1.rearrange("(p a) -> p a", a=1)).then_inc(c_loaded, 16)
            for n, w in enumerate((kc_w, qc_w, vc_w)):
                pool.dma_start(conv_col[:, n], w.rearrange("(h p) j -> p h j", p=P)).then_inc(c_loaded, 16)
            for s in range(CONV):
                pool.dma_start(taps_l[32 * s:32 * s + 32, :, 1:LONG + 1],
                               fir_l.rearrange("h d j -> (h d) j").rearrange("(g c) j -> c g j", c=32)).then_inc(c_loaded, 16)
                pool.dma_start(taps_s[32 * s:32 * s + 32, :, 1:SHORT + 1],
                               fir_s.rearrange("h d j -> (h d) j").rearrange("(g c) j -> c g j", c=32)).then_inc(c_loaded, 16)
            pool.dma_start(stat_rows[:, :, :], gW1[C:C + 3 * BR * D, :].rearrange("(s d) n -> d s n", d=D)).then_inc(c_loaded, 16)
            for h in range(2):
                pool.dma_start(gate_br[D * h:D * h + D, :, :],
                               gW1[C + 3 * BR * D:, :].rearrange("(s d) n -> d s n", d=D)).then_inc(c_loaded, 16)
            for h in range(HEADS):
                pool.dma_start(temp_col[32 * h:32 * h + 32, :],
                               temp[h:h + 1].partition_broadcast(32)).then_inc(c_loaded, 16)
            pool.dma_start(floor_b[:, :, :].rearrange("p h b -> p (h b)"),
                           row_bcast(eps_floor.rearrange("h b -> (h b)"))).then_inc(c_loaded, 16)
            for h in range(2):
                pool.dma_start(onorm_col[D * h:D * h + D, :], onorm_w.rearrange("(p a) -> p a", a=1)).then_inc(c_loaded, 16)

            made = 2

            def make(ins):
                nonlocal made
                made += 1
                ins.then_inc(const_made, 1)
                pool.wait_ge(const_made, made)

            for t, v in ((ident, 0.0), (low_strict, 1.0), (up_incl, 1.0), (eye32, 0.0), (wb_pad, 0.0), (w2g_pad, 0.0),
                         (gb2_col, 0.0), (stat_sel, 0.0), (mean_ones, 1.0 / D), (head_mask, 0.0), (v_shift, 0.0),
                         (raw, 0.0)):
                make(pool.memset(t[(slice(None),) * len(t.shape)], v))
            make(pool.affine_select(out=ident[:, :], in_=ident[:, :], compare_op=ALU.not_equal, fill=1.0, base=0,
                                    pattern=[[-1, P]], channel_multiplier=1))
            for c in range(CPT):
                rows = slice(32 * c, 32 * c + 32)
                make(pool.affine_select(out=low_strict[rows, :], in_=low_strict[rows, :], compare_op=ALU.is_gt, fill=0.0,
                                        base=0, pattern=[[-1, CHUNK]], channel_multiplier=1))
                make(pool.affine_select(out=up_incl[rows, :], in_=up_incl[rows, :], compare_op=ALU.is_ge, fill=0.0,
                                        base=0, pattern=[[1, CHUNK]], channel_multiplier=-1))
                make(pool.affine_select(out=eye32[rows, :], in_=eye32[rows, :], compare_op=ALU.not_equal, fill=1.0,
                                        base=0, pattern=[[-1, CHUNK]], channel_multiplier=1))
            for s in range(2 * BR):
                make(pool.memset(stat_sel[:, s, HEADS * s:HEADS * s + HEADS], 1.0))
            for s in range(2 * BR):
                make(pool.affine_select(out=head_mask[:, :], in_=head_mask[:, :], compare_op=ALU.not_equal, fill=1.0,
                                        base=-HEADS * s, pattern=[[-1, HEADS]], channel_multiplier=1))
            assert made == CONST_MADE, made
            pool.dma_start(wb_pad[:, :, 0:HEADS], Wb.rearrange("(k p) n -> p k n", p=P)).then_inc(c_loaded, 16)
            pool.dma_start(w2g_pad[:, 0:BR], gW2).then_inc(c_loaded, 16)
            for h in range(HEADS):
                pool.dma_start(gb2_col[32 * h:32 * h + BR, :], gb2.rearrange("(p a) -> p a", a=1)).then_inc(c_loaded, 16)

            with pool.Fori(0, SEQS) as i:
                n = 0
                pool.wait_ge(x_loaded, i * 16 + 16)
                if True:
                    pool.wait_ge(setup_dve, SETUP_DVE)
                    pool.tensor_tensor(xb_tok[:, :, :], x_tok[:, :, :], b2_half[:, :].unsqueeze(1).broadcast_to([P, TILES, C]),
                                       ALU.add).then_inc(xb_made, 1)
                pool.wait_ge(l_loaded, i * 64 + 64)
                for k in range(1, CHUNK - 1):
                    below = CHUNK - 1 - k
                    shape = [CPT * UNITS, below, k]
                    pool.tensor_tensor(l_prod[:, k + 1:, 0:k], l_inv[:, k + 1:, k:k + 1].broadcast_to(shape),
                                       l_inv[:, k:k + 1, 0:k].broadcast_to(shape), ALU.mult).then_inc(pool_step, 1)
                    n += 1
                    pool.wait_ge(pool_step, i * POOL_STEPS + n)
                    pool.tensor_tensor(l_inv[:, k + 1:, 0:k], l_inv[:, k + 1:, 0:k], l_prod[:, k + 1:, 0:k],
                                       ALU.add).then_inc(pool_step, 1)
                    n += 1
                    pool.wait_ge(pool_step, i * POOL_STEPS + n)
                assert n == POOL_STEPS
                pool.wait_ge(res_made, i * 6 + 4)
                pool.tensor_tensor(xb_tok[:, :, :], x1_tok[:, :, :], b2_half[:, :].unsqueeze(1).broadcast_to([P, TILES, C]),
                                   ALU.add).then_inc(xb_made, 1)

        @block.scalar
        def _(act):
            act.wait_ge(c_loaded, C_LOADED * 16)

            def layernorm(i, n, name):
                act.wait_ge(var_made, 3 * i + n + 1)
                act.activation(std[:, :], std[:, :], ACT.Sqrt).then_inc(std_made, 1)
                for h in range(HALVES):
                    bank, read = arrive(act, i, name, h)
                    act.activation(xt_hi[:, h, :], bank[:, :], ACT.Copy).then_inc(xhi_made, 1)
                    act.wait_ge(xhi_made, 6 * i + 2 * n + h + 1)
                    act.nop().then_inc(read, 1)

            def ffn(i, f):
                for m in range(KT):
                    bank, read = arrive(act, i, f"ffn{f}", m)
                    if m >= 2:
                        act.wait_ge(h_split, 2 * KT * i + KT * f + m - 1)
                    act.activation(h_f[:, m % 2, :], bank[:, :], ACT.Gelu, bias=b1_col[:, m:m + 1]).then_inc(gelu_made, 1)
                    act.wait_ge(gelu_made, 2 * KT * i + KT * f + m + 1)
                    act.nop().then_inc(read, 1)

            def copy_out(i, what, k, dst, made, count, func=ACT.Copy, **kw):
                bank, read = arrive(act, i, what, k)
                act.activation(dst, bank[0:dst.shape[0], :], func, **kw).then_inc(made, 1)
                act.wait_ge(made, count)
                act.nop().then_inc(read, 1)

            with act.Fori(0, SEQS) as i:
                layernorm(i, 0, "lnf0")
                ffn(i, 0)
                layernorm(i, 1, "ln2")
                def raw_out(m):
                    if m >= RAWS:
                        act.wait_ge(conv_made, 6 * i + m - RAWS + 1)
                    copy_out(i, "qkv", m, raw[:, m % RAWS, CONV - 1:], raw_made, 6 * i + m + 1)

                for m in range(RAWS):
                    raw_out(m)
                for m in range(6):
                    if m + RAWS < 6:
                        raw_out(m + RAWS)
                    act.wait_ge(conv_made, 6 * i + m + 1)
                    dst = qk_fm[:, m % 2, m // 2, :] if m < 4 else v_fm[:, m % 2, :]
                    act.activation(dst, conv_acc[:, m % 2, :], ACT.Silu).then_inc(silu_made, 1)
                copy_out(i, "beta", 0, beta_rows[:, :], beta_made, i + 1, ACT.Sigmoid)
                copy_out(i, "hidden", 0, hid_fm[:, :], hid_made, i + 1)
                for t in range(2):
                    copy_out(i, "k_t", t, arena[:, K_TOK, 512 * t:512 * t + 512], tok_made, 8 * i + t + 1)
                act.activation(arena[:, SQ, :], arena[:, K_TOK, :], ACT.Square).then_inc(sq_made, 1)
                for t in range(2):
                    bank, read = arrive(act, i, "q_t", t)
                    act.activation(arena[:, TMP, 512 * t:512 * t + 512], bank[:, :], ACT.Square).then_inc(sq_made, 1)
                    act.wait_ge(sq_made, 8 * i + t + 2)
                    act.nop().then_inc(read, 1)
                act.wait_ge(ssq_made, 3 * i + 1)
                act.activation(nrm[:, :, :], nrm[:, :, :], ACT.Sqrt).then_inc(root_made, 1)
                for n, (what, dst) in enumerate((("v_t", V_TOK), ("fs_t", FS_TOK), ("fl_t", FL_TOK))):
                    for t in range(2):
                        copy_out(i, what, t, arena[:, dst, 512 * t:512 * t + 512], tok_made, 8 * i + 2 * n + t + 3)
                    act.wait_ge(sq_used, 7 * i + 2 + n)
                    act.activation(arena[:, SQ, :], arena[:, dst, :], ACT.Square).then_inc(sq_made, 1)
                for n in range(TILES * CPT):
                    act.wait_ge(s_ready, 16 * i + n + 1)
                    act.activation(s_sb[:, :, :], BANKS[ST][:, 0:HALVES * D].rearrange("p (h d) -> p h d", h=HALVES),
                                   ACT.Copy).then_inc(s_made, 1)
                act.wait_ge(dl_made, 4 * i + 4)
                act.wait_ge(sq_used, 7 * i + 5)
                act.activation(arena[:, SQ, :], arena[:, DL_TOK, :], ACT.Square).then_inc(sq_made, 1)
                for h in range(HALVES):
                    copy_out(i, "dl_t", h, dl_fm[:, h, :], dlt_made, 2 * i + h + 1)
                act.wait_ge(ssq_made, 3 * i + 2)
                act.activation(stats[:, :, 0], stats[:, :, 0], ACT.Sqrt).then_inc(root_made, 1)
                copy_out(i, "stat_t", 0, stat_fm[:, :], statt_made, i + 1)
                for h in range(HEADS):
                    act.wait_ge(pre_made, 4 * i + h + 1)
                    if h >= 2:
                        act.wait_ge(hm_used, 4 * i + h - 1)
                    act.activation(hm[:, h % 2, :], pre[:, h % 2, :], ACT.Gelu, bias=gb1_col[:, 0:1]).then_inc(hm_made, 1)
                if True:
                    act.wait_ge(setup_dve, SETUP_DVE)
                copy_out(i, "logit", 0, lg_fm[:, :], lg_made, i + 1, ACT.Identity, bias=gbt_col[:, 0:1],
                         scale=tinv_col[:, 0:1])
                act.wait_ge(lshift_made, i + 1)
                act.activation(lg[:, :, :], lg[:, :, :], ACT.Exp).then_inc(exp_made, 1)
                act.wait_ge(mix_made, i + 1)
                act.wait_ge(sq_used, 7 * i + 6)
                act.activation(arena[:, SQ, :], arena[:, MIX, :], ACT.Square).then_inc(sq_made, 1)
                act.wait_ge(ssq_made, 3 * i + 3)
                act.activation(onrm[:, :], onrm[:, :], ACT.Sqrt).then_inc(root_made, 1)
                for h in range(HALVES):
                    bank, read = arrive(act, i, "mix_t", h)
                    act.activation(xt_hi[:, h, :], bank[:, :], ACT.Copy).then_inc(omix_hi, 1)
                    act.wait_ge(omix_hi, 2 * i + h + 1)
                    act.nop().then_inc(read, 1)
                layernorm(i, 2, "lnf1")
                ffn(i, 1)

        def product3(pe, dst, a_hi, a_lo, b_hi, b_lo, first, last, **kw):
            pe.matmul(dst, a_hi, b_hi, start=first, stop=False, **kw)
            pe.matmul(dst, a_hi, b_lo, start=False, stop=False, **kw)
            return pe.matmul(dst, a_lo, b_hi, start=False, stop=last, **kw)

        @block.tensor
        def _(pe):
            pe.wait_ge(const_made, CONST_MADE)
            pe.wait_ge(c_loaded, C_LOADED * 16)
            for b in range(BR):
                pe.matmul(BANKS[AC0][:, P * b:P * b + P], mean_ones[:, :], stat_rows[:, 3 * b, :],
                          start=True, stop=True)
            for s in range(2 * BR):
                last = pe.matmul(BANKS[AC1][0:32, 0:P], stat_sel[:, s, :], stat_rows[:, 3 * (s % BR) + 1 + s // BR, :],
                                 start=(s == 0), stop=(s == 2 * BR - 1))
            last.then_inc(setup_pe, 1)
            pe.wait_ge(setup_dve, SETUP_DVE)

            def turn(i, what, k, src, made, count):
                bank, full = claim(pe, i, what, k)
                pe.wait_ge(made, count)
                for n in range(4):
                    last = pe.transpose(bank[:, P * n:P * n + P], src(n), ident[:, :])
                last.then_inc(full, 1)

            def turn_rows(i, name, n):
                for h in range(HALVES):
                    turn(i, name, h, lambda t: xn_tok[:, t, P * h:P * h + P], xn_made, 3 * i + n + 1)

            def to_tok(i, what, src, made, count):
                for t in range(2):
                    turn(i, what, t, lambda n: src(n % 2)[:, P * (2 * t + n // 2):P * (2 * t + n // 2) + P], made, count)

            def ffn(i, f):
                seen = 2 * KT * i + KT * f
                ow = [claim(pe, i, f"ffo{f}", b) for b in range(2)]

                def down(m):
                    pe.wait_ge(h_split, seen + m + 1)
                    for t in range(TILES):
                        cols = slice(C * (t % 2), C * (t % 2) + C)
                        last = product3(pe, ow[t // 2][0][:, cols], h_hi[:, m % RING, P * t:P * t + P],
                                        h_lo[:, m % RING, P * t:P * t + P], w2_hi[:, m, :], w2_lo[:, m, :],
                                        m == 0 and t % 2 == 0, m == KT - 1, skip_group_check=True)
                    last.then_inc(h_used, 1)

                for m in range(KT):
                    bank, full = claim(pe, i, f"ffn{f}", m)
                    if m == 0:
                        pe.wait_ge(xt_made, 6 * i + 2 + 4 * f)
                    for k in range(HALVES):
                        cols = slice(P * m, P * m + P)
                        last = product3(pe, bank[:, :], w1_hi[:, k, cols], w1_lo[:, k, cols], xt_hi[:, k, :],
                                        xt_lo[:, k, :], k == 0, k == HALVES - 1)
                    last.then_inc(full, 1)
                    if m >= 2:
                        down(m - 2)
                down(KT - 2)
                pe.wait_ge(h_split, seen + KT)
                down(KT - 1)
                for b in range(2):
                    pe.wait_ge(h_used, seen + KT)
                    pe.nop().then_inc(ow[b][1], 1)

            with pe.Fori(0, SEQS) as i:
                turn_rows(i, "lnf0", 0)
                ffn(i, 0)
                turn_rows(i, "ln2", 1)
                pe.wait_ge(xt_made, 6 * i + 4)
                for m in range(6):
                    bank, full = claim(pe, i, "qkv", m)
                    cols = slice(P * (m % 2), P * (m % 2) + P)
                    for k in range(HALVES):
                        last = product3(pe, bank[:, :], wqkv_hi[:, m // 2, k, cols], wqkv_lo[:, m // 2, k, cols],
                                        xt_hi[:, k, :], xt_lo[:, k, :], k == 0, k == HALVES - 1)
                    last.then_inc(full, 1)
                bank, full = claim(pe, i, "beta")
                for k in range(HALVES):
                    for n, part in enumerate((xt_hi, xt_lo)):
                        last = pe.matmul(bank[0:32, :], wb_pad[:, k, :], part[:, k, :].bitcast(F32),
                                         start=(k + n == 0), stop=(k + n == 2))
                last.then_inc(full, 1)
                bank, full = claim(pe, i, "hidden")
                for k in range(HALVES):
                    last = product3(pe, bank[:, :], wh_hi[:, k, :], wh_lo[:, k, :], xt_hi[:, k, :], xt_lo[:, k, :],
                                    k == 0, k == HALVES - 1)
                last.then_inc(full, 1)
                bank, full = claim(pe, i, "beta_t")
                pe.wait_ge(beta_made, i + 1)
                pe.sem_inc(passed, 1)
                for t in range(TILES):
                    last = pe.transpose(bank[:, 32 * t:32 * t + 32], beta_rows[:, P * t:P * t + P], ident[0:32, 0:32])
                last.then_inc(full, 1)
                to_tok(i, "k_t", lambda h: qk_fm[:, h, 0, :], silu_made, 6 * i + 2)
                to_tok(i, "q_t", lambda h: qk_fm[:, h, 1, :], silu_made, 6 * i + 4)
                for b in range(2):
                    bank, full = claim(pe, i, "gram", b)
                    pe.sem_inc(passed, 1)
                    rows = slice(D * b, D * b + D)
                    for u in range(UNITS // 2):
                        t, h = u // HALVES, 2 * (u % HALVES) + b
                        for c in range(CPT):
                            at = P * t + CHUNK * c
                            last = pe.matmul(bank[32 * c:32 * c + 32, D * u:D * u + D],
                                             qk_fm[rows, h // 2, 0, at:at + CHUNK], qk_fm[rows, h // 2, :, at:at + CHUNK],
                                             start=True, stop=True)
                    last.then_inc(full, 1)
                to_tok(i, "v_t", lambda h: v_fm[:, h, :], silu_made, 6 * i + 6)
                pe.wait_ge(v_shifted, 64 * i + 64)
                for what in ("fir_s", "fir_l"):
                    for h in range(HALVES):
                        bank, full = claim(pe, i, what, h)
                        steps = [TAPG] if what == "fir_s" else range(TAPG)
                        for n in steps:
                            at = PAD if what == "fir_s" else 4 * n
                            for g in range(4):
                                last = pe.matmul(bank[32 * g:32 * g + 32, :], fir_w[:, 4 * h + g, n, :],
                                                 v_shift[:, 4 * h + g, at:at + T], start=(n == steps[0]),
                                                 stop=(n == steps[-1]))
                        last.then_inc(full, 1)
                to_tok(i, "fs_t", lambda h: fs_fm[:, h, :], fir_made, 4 * i + 2)
                to_tok(i, "fl_t", lambda h: fl_fm[:, h, :], fir_made, 4 * i + 4)
                pe.wait_ge(u_made, i + 1)
                for c in range(CPT):
                    bank, full = claim(pe, i, "w", c)
                    rows = slice(32 * c, 32 * c + 32)
                    for t in range(TILES):
                        for h in range(HEADS):
                            at = P * (h // 2) + CHUNK * t
                            last = pe.matmul(bank[D * (h % 2):D * (h % 2) + D, at:at + CHUNK],
                                             tok(K_TOK)[rows, t, D * h:D * h + D], u2n[rows, HEADS * t + h, :],
                                             start=True, stop=True)
                    last.then_inc(full, 1)
                pe.wait_ge(w_made, CPT * i + CPT)
                pe.wait_ge(at_made, i + 1)
                pe.wait_ge(tok_made, 8 * i + 4)
                pu = [claim(pe, i, "du", p)[0] for p in range(2)]
                for t in range(TILES):
                    po, o_full = zip(*[claim(pe, i, "o", 2 * t + p) for p in range(2)])
                    for c in range(CPT):
                        rows = slice(32 * c, 32 * c + 32)
                        at = P * t + CHUNK * c
                        n = CPT * t + c
                        by_head = [(2 * half + p, p, half, slice(D * p, D * p + D), slice(D * half, D * half + D))
                                   for p in range(2) for half in range(HALVES)]
                        pe.sem_inc(passed, 1)
                        for h, p, half, part, cols in by_head:
                            last = pe.matmul(pu[p][rows, cols], u1[rows, HEADS * t + h, :],
                                             tok(V_TOK)[rows, t, D * h:D * h + D], start=(half == 0), stop=(n == 0),
                                             skip_group_check=True)
                        if n > 0:
                            pe.wait_ge(s_made, 16 * i + n)
                            pe.sem_inc(passed, 1)
                            for h, p, half, part, cols in by_head:
                                last = pe.matmul(pu[p][rows, cols], w_fm[part, half, at:at + CHUNK],
                                                 s_sb[part, half, :], start=False, stop=True, skip_group_check=True)
                        last.then_inc(du_ready, 1)
                        if n > 0:
                            for h, p, half, part, cols in by_head:
                                pe.matmul(po[p][rows, cols], qk_fm[part, half, 1, at:at + CHUNK],
                                          s_sb[part, half, :], start=(half == 0), stop=False, skip_group_check=True)
                        pe.wait_ge(du_made, 16 * i + n + 1)
                        for h, p, half, part, cols in by_head:
                            last = pe.matmul(BANKS[ST][part, cols], tok(K_TOK)[rows, t, D * h:D * h + D],
                                             du[rows, p, half, :], start=(n == 0 and half == 0), stop=(n == 15),
                                             skip_group_check=True)
                        last.then_inc(s_ready, 1)
                        for h, p, half, part, cols in by_head:
                            last = pe.matmul(po[p][rows, cols], at_tok[rows, HEADS * t + h, :], du[rows, p, half, :],
                                             start=(n == 0 and half == 0), stop=True, skip_group_check=True)
                            if c == CPT - 1 and half == HALVES - 1:
                                last.then_inc(o_full[p], 1)
                for h in range(HALVES):
                    turn(i, "dl_t", h, lambda t: tok(DL_TOK)[:, t, P * h:P * h + P], dl_made, 4 * i + 4)
                bank, full = claim(pe, i, "stat_t")
                pe.wait_ge(stats_made, i + 1)
                pe.wait_ge(root_made, 3 * i + 2)
                for t in range(TILES):
                    last = pe.transpose(bank[0:32, P * t:P * t + P], stats[:, t].rearrange("p a b h -> p (a b h)"), ident[:, :])
                last.then_inc(full, 1)
                lbank, lfull = claim(pe, i, "logit")

                def logits(h):
                    pe.wait_ge(hm_made, 4 * i + h + 1)
                    last = pe.matmul(lbank[32 * h:32 * h + 32, :], w2g_pad[:, :], hm[:, h % 2, :], start=True, stop=True)
                    last.then_inc(hm_used, 1)

                pe.wait_ge(dlt_made, 2 * i + 2)
                pe.wait_ge(statt_made, i + 1)
                for h in range(HEADS):
                    bank, full = claim(pe, i, "gate", h)
                    part = slice(D * (h % 2), D * (h % 2) + D)
                    for b, src in enumerate((fs_fm, fl_fm, dl_fm, v_fm)):
                        pe.matmul(bank[:, :], gate_br[part, b, :], src[part, h // 2, :], start=(b == 0), stop=False)
                    pe.matmul(bank[:, :], gate_st[:, h, :], stat_fm[:, :], start=False, stop=True).then_inc(full, 1)
                    if h >= 1:
                        logits(h - 1)
                logits(HEADS - 1)
                pe.wait_ge(hm_used, 4 * i + 4)
                pe.nop().then_inc(lfull, 1)
                turn(i, "logit_t", 0, lambda t: lg_fm[:, P * t:P * t + P], lg_made, i + 1)
                for h in range(HALVES):
                    turn(i, "mix_t", h, lambda t: tok(TMP)[:, t, P * h:P * h + P], norm_made, i + 1)
                pe.wait_ge(omix_lo, 2 * i + 2)
                for b in range(2):
                    bank, full = claim(pe, i, "wo", b)
                    for t in (2 * b, 2 * b + 1):
                        for k in range(HALVES):
                            rows = slice(P * t, P * t + P)
                            last = product3(pe, bank[:, C * (t % 2):C * (t % 2) + C], xt_hi[:, k, rows], xt_lo[:, k, rows],
                                            wo_hi[:, k, :], wo_lo[:, k, :], k == 0, k == HALVES - 1)
                    last.then_inc(full, 1)
                turn_rows(i, "lnf1", 2)
                ffn(i, 1)

        @block.vector
        def _(dve):
            n = 0

            def step(ins):
                nonlocal n
                n += 1
                ins.then_inc(setup_dve, 1)

            def settle():
                dve.wait_ge(setup_dve, n)

            dve.wait_ge(w_loaded, 8 * 16)
            dve.wait_ge(const_made, CONST_MADE)
            dve.wait_ge(c_loaded, C_LOADED * 16)
            for s in range(CONV):
                rows = slice(32 * s, 32 * s + 32)
                shape = [32, GROUPS, TAPG, 32]
                e = eye32[rows, :].unsqueeze(1).broadcast_to([32, GROUPS * TAPG, 32]).rearrange("p (g n) c -> p g n c", g=GROUPS)
                tap = taps_l[rows, :, 3 - s:3 - s + 4 * (TAPG - 1) + 1:4]
                step(dve.tensor_tensor(fir_w[rows, :, 0:TAPG, :], e, tap.unsqueeze(3).broadcast_to(shape), ALU.mult))
                step(dve.tensor_tensor(fir_w[rows, :, TAPG, :], eye32[rows, :].unsqueeze(1).broadcast_to([32, GROUPS, 32]),
                                       taps_s[rows, :, 3 - s:4 - s].broadcast_to([32, GROUPS, 32]), ALU.mult))
            step(dve.tensor_scalar(b2_half[:, :], b2_st, 0.5, None, ALU.mult))
            step(dve.tensor_scalar(temp_col[:, :], temp_col[:, :], 0.2, 10.0, ALU.max, ALU.min))
            settle()
            step(dve.reciprocal(tinv_col[:, :], temp_col[:, :]))
            settle()
            step(dve.tensor_tensor(gbt_col[:, :], gb2_col[:, :], tinv_col[:, :], ALU.mult))
            step(dve.tensor_scalar(floor_b[:, :, :], floor_b[:, :, :], 1e-7, 0.1, ALU.max, ALU.min))
            step(dve.tensor_scalar(wo_st, wo_st, onorm_col[:, 0:1], None, ALU.mult))
            settle()
            for hi, lo, st in ((w1_hi, w1_lo, w1_st), (w2_hi, w2_lo, w2_st), (wqkv_hi, wqkv_lo, wqkv_st),
                               (wo_hi, wo_lo, wo_st), (wh_hi, wh_lo, wh_st)):
                dims = (slice(None),) * len(hi.shape)
                step(dve.tensor_copy(hi[dims], st))
                settle()
                step(dve.tensor_tensor(lo[dims], st, hi[dims].bitcast(F32), ALU.subtract))
            dve.wait_ge(setup_pe, 1)
            step(dve.tensor_tensor(gate_br[:, :, :], gate_br[:, :, :],
                                   BANKS[AC0][:, :].rearrange("p (b n) -> p b n", b=BR), ALU.add))
            step(dve.tensor_copy(stat_all[:, :], BANKS[AC1][0:32, 0:P]))
            settle()
            for h in range(HEADS):
                step(dve.tensor_scalar(gate_st[:, h, :], stat_all[:, :], head_mask[:, h:h + 1], None, ALU.mult))
            settle()
            assert n == SETUP_DVE, n
            for bank in emptied:
                dve.sem_inc(bank, 1)

            with dve.Fori(0, SEQS) as i:
                n = 0

                def link(ins):
                    nonlocal n
                    n += 1
                    ins.then_inc(dve_step, 1)
                    dve.wait_ge(dve_step, i * DVE_STEPS + n)

                def layernorm(k, src, name):
                    for t in range(TILES):
                        last = dve.bn_stats(bn[:, t, :], src[:, t, :])
                    link(last)
                    dve.sem_inc(passed, 1)
                    for t in range(TILES):
                        last = dve.bn_aggr(mv[:, t, :], bn[:, t, :])
                    link(last)
                    dve.tensor_scalar(std[:, :], mv[:, :, 1], 1e-5, None, ALU.add).then_inc(var_made, 1)
                    dve.wait_ge(std_made, 3 * i + k + 1)
                    link(dve.reciprocal(rstd[:, :], std[:, :]))
                    for t in range(TILES):
                        last = dve.tensor_scalar(xn_tok[:, t, :], src[:, t, :], mv[:, t, 0:1], rstd[:, t:t + 1],
                                                 ALU.subtract, ALU.mult)
                    last.then_inc(xn_made, 1)
                    low_part(name, xhi_made, 6 * i + 2 * k, xt_made)

                def low_part(name, hi_made, seen, made):
                    for h in range(HALVES):
                        bank, read = arrive(dve, i, name, h)
                        dve.wait_ge(hi_made, seen + h + 1)
                        dve.tensor_tensor(xt_lo[:, h, :], bank[:, :], xt_hi[:, h, :].bitcast(F32),
                                          ALU.subtract).then_inc(made, 1)
                        dve.wait_ge(made, (seen if made is xt_made else 2 * i) + h + 1)
                        dve.nop().then_inc(read, 1)

                def ffn(f):
                    seen = 2 * KT * i + KT * f
                    for m in range(KT):
                        dve.wait_ge(gelu_made, seen + m + 1)
                        if m >= RING:
                            dve.wait_ge(h_used, seen + m - RING + 1)
                        link(dve.tensor_copy(h_hi[:, m % RING, :], h_f[:, m % 2, :]))
                        dve.tensor_tensor(h_lo[:, m % RING, :], h_f[:, m % 2, :], h_hi[:, m % RING, :].bitcast(F32),
                                          ALU.subtract).then_inc(h_split, 1)

                def residual(what, dst, base, half, k):
                    for b in range(2):
                        bank, read = arrive(dve, i, what, b)
                        src = bank[:, :].rearrange("p (t c) -> p t c", t=2)
                        two = slice(2 * b, 2 * b + 2)
                        if half:
                            ins = dve.scalar_tensor_tensor(out=dst[:, two, :], in0=src, scalar=0.5, in1=base[:, two, :],
                                                           op0=ALU.mult, op1=ALU.add)
                        else:
                            ins = dve.tensor_tensor(dst[:, two, :], src, base[:, two, :], ALU.add)
                        ins.then_inc(res_made, 1)
                        dve.wait_ge(res_made, 6 * i + 2 * k + b + 1)
                        dve.nop().then_inc(read, 1)

                def per_head(v):
                    return v.unsqueeze(2).broadcast_to([P, UNITS, D])

                def per_row(v):
                    return v.unsqueeze(2).broadcast_to([P, UNITS, CHUNK])

                def copy_out(what, k, dst, src=None, ins=None, made=None, count=None):
                    bank, read = arrive(dve, i, what, k)
                    dve.tensor_copy(dst, bank[:, :]).then_inc(made, 1)
                    dve.wait_ge(made, count)
                    dve.nop().then_inc(read, 1)

                dve.wait_ge(x_loaded, i * 16 + 16)
                layernorm(0, x_tok, "lnf0")
                ffn(0)
                dve.wait_ge(xb_made, 2 * i + 1)
                residual("ffo0", x1_tok, xb_tok, True, 0)
                layernorm(1, x1_tok, "ln2")
                for m in range(6):
                    src = raw[:, m % RAWS, :]
                    w = conv_col[:, m // 2, m % 2, :]
                    acc = conv_acc[:, m % 2, :]
                    dve.wait_ge(raw_made, 6 * i + m + 1)
                    if m >= 2:
                        dve.wait_ge(silu_made, 6 * i + m - 1)
                    link(dve.tensor_scalar(acc, src[:, 0:T], w[:, 0:1], None, ALU.mult))
                    for j in range(1, CONV):
                        ins = dve.scalar_tensor_tensor(out=acc, in0=src[:, j:j + T], scalar=w[:, j:j + 1], in1=acc,
                                                       op0=ALU.mult, op1=ALU.add)
                        if j < CONV - 1:
                            link(ins)
                    ins.then_inc(conv_made, 1)
                bank, read = arrive(dve, i, "beta_t")
                link(dve.tensor_copy(beta_tok[:, :, :], bank[:, 0:P].rearrange("p (t n) -> p t n", t=TILES)[:, :, 0:HEADS]))
                dve.nop().then_inc(read, 1)
                dve.wait_ge(sq_made, 8 * i + 1)
                dve.tensor_reduce(ssq[:, 0, :], heads(SQ), AX.X, ALU.add).then_inc(sq_used, 1)
                dve.wait_ge(sq_made, 8 * i + 3)
                dve.wait_ge(sq_used, 7 * i + 1)
                dve.tensor_reduce(ssq[:, 1, :], heads(TMP), AX.X, ALU.add).then_inc(sq_used, 1)
                dve.wait_ge(sq_used, 7 * i + 2)
                dve.tensor_scalar(nrm[:, :, :], ssq[:, :, :], 1e-6, None, ALU.add).then_inc(ssq_made, 1)
                dve.wait_ge(root_made, 3 * i + 1)
                link(dve.reciprocal(inv[:, :, :], nrm[:, :, :]))
                link(dve.tensor_tensor(c1[:, :], beta_tok[:, :, :].rearrange("p t h -> p (t h)"), inv[:, 0, :], ALU.mult))
                link(dve.scalar_tensor_tensor(out=c2n[:, :], in0=c1[:, :], scalar=-1.0, in1=inv[:, 0, :],
                                              op0=ALU.mult, op1=ALU.mult))
                for b in range(2):
                    bank, read = arrive(dve, i, "gram", b)
                    g = bank.rearrange("p (u a j) -> p u a j", u=UNITS // 2, a=2)
                    shape = [P, UNITS // 2, CHUNK]
                    dve.tensor_tensor(l_tok[:, b::2, :], g[:, :, 0, :], c2n[:, b::2].unsqueeze(2).broadcast_to(shape), ALU.mult)
                    link(dve.tensor_tensor(at_tok[:, b::2, :], g[:, :, 1, :], up_incl[:, :].unsqueeze(1).broadcast_to(shape),
                                           ALU.mult))
                    dve.nop().then_inc(read, 1)
                dve.tensor_tensor(l_tok[:, :, :], l_tok[:, :, :],
                                  low_strict[:, :].unsqueeze(1).broadcast_to([P, UNITS, CHUNK]), ALU.mult).then_inc(l_made, 1)
                dve.nop().then_inc(at_made, 1)
                for n2, (what, dst) in enumerate((("fir_s", fs_fm), ("fir_l", fl_fm))):
                    for h in range(HALVES):
                        copy_out(what, h, dst[:, h, :], made=fir_made, count=4 * i + 2 * n2 + h + 1)
                for b, src, seen in ((3, V_TOK, 0), (0, FS_TOK, 1), (1, FL_TOK, 2)):
                    dve.wait_ge(tok_made, 8 * i + 2 * seen + 4)
                    dve.tensor_reduce(stats[:, :, 1, b, :], heads(src), AX.X, ALU.max)
                    dve.wait_ge(sq_made, 8 * i + 4 + seen)
                    dve.tensor_reduce(stats[:, :, 0, b, :], heads(SQ), AX.X, ALU.add).then_inc(sq_used, 1)
                dve.wait_ge(t_loaded, 64 * i + 64)
                link(dve.transpose(u_t[:, :, :].rearrange("p u j -> p (u j)"), t_tok[:, :, :].rearrange("p u j -> p (u j)")))
                link(dve.tensor_tensor(u_t[:, :, :], u_t[:, :, :], eye32[:, :].unsqueeze(1).broadcast_to([P, UNITS, CHUNK]),
                                       ALU.add))
                dve.tensor_tensor(u1[:, :, :], u_t[:, :, :], per_row(c1[:, :]), ALU.mult)
                dve.tensor_tensor(u2n[:, :, :], u_t[:, :, :], per_row(c2n[:, :]), ALU.mult).then_inc(u_made, 1)
                for c in range(CPT):
                    bank, read = arrive(dve, i, "w", c)
                    dve.tensor_copy(w_fm[:, :, :].rearrange("p h (t c j) -> p h t c j", t=TILES, c=CPT)[:, :, :, c, :],
                                    bank[:, 0:HALVES * P].rearrange("p (h t j) -> p h t j", h=HALVES, t=TILES)).then_inc(w_made, 1)
                    dve.wait_ge(w_made, CPT * i + c + 1)
                    dve.nop().then_inc(read, 1)
                for t in range(TILES):
                    for c in range(CPT):
                        rows = slice(32 * c, 32 * c + 32)
                        dve.wait_ge(du_ready, 16 * i + CPT * t + c + 1)
                        dve.tensor_copy(du[rows, :, :, :], psum[rows, OW0:OW1 + 1, 0:HALVES * D]
                                        .rearrange("p a (h d) -> p a h d", h=HALVES)).then_inc(du_made, 1)
                    first = use("o", 2 * t)[0]
                    reads = [arrive(dve, i, "o", 2 * t + p)[1] for p in range(2)]
                    us = slice(HEADS * t, HEADS * t + HEADS)
                    for p in range(2):
                        ins = dve.tensor_tensor(
                            heads(DL_TOK)[:, us, :][:, p::2, :],
                            psum[:, first + p, 0:HALVES * D].rearrange("p (h d) -> p h d", h=HALVES),
                            inv[:, 1, us][:, p::2].unsqueeze(2).broadcast_to([P, HALVES, D]), ALU.mult)
                    ins.then_inc(dl_made, 1)
                    dve.wait_ge(dl_made, 4 * i + t + 1)
                    for read in reads:
                        dve.nop().then_inc(read, 1)
                dve.wait_ge(du_made, 16 * i + 16)
                for p in range(2):
                    dve.nop().then_inc(emptied[use("du", p)[0]], 1)
                dve.tensor_reduce(stats[:, :, 1, 2, :], heads(DL_TOK), AX.X, ALU.max).then_inc(stats_made, 1)
                dve.wait_ge(sq_made, 8 * i + 7)
                dve.tensor_reduce(stats[:, :, 0, 2, :], heads(SQ), AX.X, ALU.add).then_inc(sq_used, 1)
                dve.wait_ge(sq_used, 7 * i + 6)
                link(dve.tensor_scalar(stats[:, :, 0], stats[:, :, 0], 1.0 / D, 1e-8, ALU.mult, ALU.max))
                dve.nop().then_inc(ssq_made, 1)
                for h in range(HEADS):
                    bank, read = arrive(dve, i, "gate", h)
                    dve.wait_ge(hid_made, i + 1)
                    if h >= 2:
                        dve.wait_ge(hm_made, 4 * i + h - 1)
                    dve.tensor_tensor(pre[:, h % 2, :], bank[:, :], hid_fm[:, :], ALU.add).then_inc(pre_made, 1)
                    dve.wait_ge(pre_made, 4 * i + h + 1)
                    dve.nop().then_inc(read, 1)
                bank, read = arrive(dve, i, "logit_t")
                lt = bank[:, :].rearrange("p (t h b) -> p t h b", t=TILES, h=HEADS)[:, :, :, 0:BR]
                link(dve.tensor_copy(lg[:, :, :].rearrange("p (t h) b -> p t h b", t=TILES), lt))
                dve.nop().then_inc(read, 1)

                def per_branch(v):
                    return v.unsqueeze(2).broadcast_to([P, UNITS, BR])

                link(dve.tensor_reduce(lmax[:, :], lg[:, :, :], AX.X, ALU.max))
                dve.tensor_tensor(lg[:, :, :], lg[:, :, :], per_branch(lmax[:, :]), ALU.subtract).then_inc(lshift_made, 1)
                dve.wait_ge(exp_made, i + 1)
                link(dve.tensor_reduce(lsum[:, :], lg[:, :, :], AX.X, ALU.add))
                link(dve.reciprocal(linv[:, :], lsum[:, :]))
                link(dve.tensor_tensor(lg[:, :, :], lg[:, :, :], per_branch(linv[:, :]), ALU.mult))
                link(dve.tensor_tensor(lg[:, :, :].rearrange("p (t h) b -> p t (h b)", t=TILES),
                                       lg[:, :, :].rearrange("p (t h) b -> p t (h b)", t=TILES),
                                       floor_b[:, :, :].rearrange("p h b -> p (h b)").unsqueeze(1).broadcast_to([P, TILES, HEADS * BR]), ALU.max))
                link(dve.tensor_reduce(lsum[:, :], lg[:, :, :], AX.X, ALU.add))
                link(dve.reciprocal(linv[:, :], lsum[:, :]))
                link(dve.tensor_tensor(mix_w[:, :, :], lg[:, :, :], per_branch(linv[:, :]), ALU.mult))
                for b, src in enumerate((FS_TOK, FL_TOK, DL_TOK, V_TOK)):
                    w = mix_w[:, :, b:b + 1].broadcast_to([P, UNITS, D])
                    if b == 0:
                        link(dve.tensor_tensor(heads(MIX), heads(src), w, ALU.mult))
                        continue
                    link(dve.tensor_tensor(heads(TMP), heads(src), w, ALU.mult))
                    ins = dve.tensor_tensor(heads(MIX), heads(MIX), heads(TMP), ALU.add)
                    if b < BR - 1:
                        link(ins)
                ins.then_inc(mix_made, 1)
                dve.wait_ge(sq_made, 8 * i + 8)
                dve.tensor_reduce(oss[:, :], heads(SQ), AX.X, ALU.add).then_inc(sq_used, 1)
                dve.wait_ge(sq_used, 7 * i + 7)
                dve.tensor_scalar(onrm[:, :], oss[:, :], 1.0 / D, 1e-5, ALU.mult, ALU.add).then_inc(ssq_made, 1)
                dve.wait_ge(root_made, 3 * i + 3)
                link(dve.reciprocal(oinv[:, :], onrm[:, :]))
                dve.tensor_tensor(heads(TMP), heads(MIX), per_head(oinv[:, :]), ALU.mult).then_inc(norm_made, 1)
                low_part("mix_t", omix_hi, 2 * i, omix_lo)
                residual("wo", x1_tok, x1_tok, False, 1)
                layernorm(2, x1_tok, "lnf1")
                ffn(1)
                dve.wait_ge(xb_made, 2 * i + 2)
                residual("ffo1", x_tok, xb_tok, True, 2)
                assert n == DVE_STEPS, n


_INS = ["x", "Wq", "Wk", "Wv", "Wb", "qc_w", "kc_w", "vc_w", "fir_s", "fir_l", "gW1", "gb1", "gW2", "gb2", "temp",
        "eps_floor", "onorm_w", "Wo"]
_FFN = ["w1", "b1", "w2", "b2"]


def kernel(**inputs):
    import numpy as _np
    import concourse.bacc as _bacc
    from concourse import mybir as _mybir
    from concourse.bass_utils import run_bass_kernel_spmd as _run

    nc = _bacc.Bacc("TRN2", target_bir_lowering=False, num_devices=1)
    arrays, args = {}, []
    for name in [f"L0_attn_{n}" for n in _INS] + [f"L0_ffn_{n}" for n in _FFN]:
        a = _np.ascontiguousarray(inputs[name])
        arrays[f"in_{name}"] = a
        args.append(nc.dram_tensor(f"in_{name}", a.shape, _mybir.dt.from_np(a.dtype), kind="ExternalInput").ap())
    args.append(nc.dram_tensor("out_0", (SEQS, T, C), _mybir.dt.float32, kind="ExternalOutput").ap())
    macaron_kernel(nc, *args)
    r = _run(nc, [arrays], core_ids=[0])
    return r.results[0]["out_0"]
```

```python
from contextlib import ExitStack

import concourse.bass as bass
from concourse import mybir

F32 = mybir.dt.float32
F32R = mybir.dt.float32r
ALU = mybir.AluOpType
ACT = mybir.ActivationFunctionType
AX = mybir.AxisListType

SEQS, T, C = 8, 512, 256
P = 128
TILES = T // P
HALVES = C // P
HEADS, D = 4, 64
HID = 1024
KT = HID // P
CHUNK = 32
CPT = P // CHUNK
UNITS = TILES * HEADS
BR = 4
CONV = 4
GROUPS = C // 32
LONG, SHORT = 31, 3
TAPG = 8
PAD = 4 * (TAPG - 1)
RING = 2


def macaron_kernel(nc, x, Wq, Wk, Wv, Wb, qc_w, kc_w, vc_w, fir_s, fir_l, gW1, gb1, gW2, gb2,
                   temp, eps_floor, onorm_w, Wo, w1, b1, w2, b2, out):
    ctx = ExitStack()
    with ctx:
        def sb(name, shape, dt=F32):
            return ctx.enter_context(nc.sbuf_tensor(name, shape, dt))

        def sem(name):
            return ctx.enter_context(nc.semaphore(name))

        l_dram = nc.dram_tensor("l_dram", [CPT, CHUNK, UNITS, CHUNK], F32, kind="Internal").ap()
        t_dram = nc.dram_tensor("t_dram", [CPT, UNITS, CHUNK, CHUNK], F32, kind="Internal").ap()
        v_dram = nc.dram_tensor("v_dram", [HALVES, P, T], F32, kind="Internal").ap()

        ident = sb("ident", [P, P])
        low_strict = sb("low_strict", [P, CHUNK])
        up_incl = sb("up_incl", [P, CHUNK])
        eye32 = sb("eye32", [P, CHUNK])
        w1_hi, w1_lo = sb("w1_hi", [P, HALVES, HID], F32R), sb("w1_lo", [P, HALVES, HID], F32R)
        w2_hi, w2_lo = sb("w2_hi", [P, KT, C], F32R), sb("w2_lo", [P, KT, C], F32R)
        wqkv_hi, wqkv_lo = sb("wqkv_hi", [P, 3, HALVES, C], F32R), sb("wqkv_lo", [P, 3, HALVES, C], F32R)
        wo_hi, wo_lo = sb("wo_hi", [P, HALVES, C], F32R), sb("wo_lo", [P, HALVES, C], F32R)
        wh_hi, wh_lo = sb("wh_hi", [P, HALVES, P], F32R), sb("wh_lo", [P, HALVES, P], F32R)
        b1_col = sb("b1_col", [P, KT])
        b2_half = sb("b2_half", [P, C])
        wb_pad = sb("wb_pad", [P, HALVES, 32])
        conv_col = sb("conv_col", [P, 3, HALVES, CONV])
        fir_w = sb("fir_w", [P, GROUPS, TAPG + 1, 32])
        gate_w = sb("gate_w", [P, 3, P])
        gate_st = sb("gate_st", [3 * 32, HEADS, P])
        sq_sel = sb("sq_sel", [P, 2, HEADS, 32])
        kq_sel = sb("kq_sel", [P, HALVES, 32])
        gb1_col = sb("gb1_col", [P, 1])
        w2g_pad = sb("w2g_pad", [P, 2, 32])
        temp_col, tinv_col, gb2_col, gbt_col = (sb(n, [P, 1]) for n in ("temp_col", "tinv_col", "gb2_col", "gbt_col"))
        floor_b = sb("floor_b", [P, HEADS, BR])
        onorm_col = sb("onorm_col", [P, 1])

        arena = sb("arena", [P, 8, TILES * C])
        flat = arena[:, :, :].rearrange("p a b -> p (a b)")
        w1_st = flat[:, 0:2048].rearrange("p (k n) -> p k n", k=HALVES)
        w2_st = flat[:, 2048:4096].rearrange("p (k n) -> p k n", k=KT)
        wqkv_st = flat[:, 4096:5632].rearrange("p (w k n) -> p w k n", w=3, k=HALVES)
        wo_st = flat[:, 5632:6144].rearrange("p (k n) -> p k n", k=HALVES)
        wh_st = flat[:, 6144:6400].rearrange("p (k n) -> p k n", k=HALVES)
        b2_st = flat[:, 6400:6656]
        stat_rows = flat[0:D, 6656:8192].rearrange("d (s n) -> d s n", s=3 * BR)

        def units(n, slots):
            return arena[:, n:n + slots, :].rearrange("p a (b d) -> p (a b) d", d=D)

        k_tok = arena[:, 0, :].rearrange("p (t c) -> p t c", t=TILES)
        dv_tok = flat[:, 1024:3072].rearrange("p (u s d) -> p u s d", u=UNITS, s=2)
        f_tok = flat[:, 3072:5120].rearrange("p (u s d) -> p u s d", u=UNITS, s=2)
        sq = arena[:, 5, :].rearrange("p (n t) -> p n t", n=2)
        sq_u = arena[:, 5, :].rearrange("p (u d) -> p u d", u=UNITS)
        l_inv = arena[0:CPT * UNITS, 6, :].rearrange("p (i j) -> p i j", i=CHUNK)
        xn_tok = arena[:, 7, :].rearrange("p (t c) -> p t c", t=TILES)
        xn_u = arena[:, 7, :].rearrange("p (u d) -> p u d", u=UNITS)

        x_in = sb("x_in", [P, TILES, C])
        x1_tok = sb("x1_tok", [P, TILES, C])
        x2_tok = sb("x2_tok", [P, TILES, C])
        xt_hi, xt_lo = sb("xt_hi", [P, HALVES, T], F32R), sb("xt_lo", [P, HALVES, T], F32R)
        bn, mv_all = sb("bn", [P, TILES, 6]), sb("mv_all", [P, 2, TILES, 2])
        std_all, rstd = sb("std_all", [P, 2, TILES]), sb("rstd", [P, TILES])
        mv = [mv_all[:, n > 0] for n in range(3)]
        std = [std_all[:, n > 0] for n in range(3)]
        h_f = sb("h_f", [P, 2, T])
        h_hi, h_lo = sb("h_hi", [P, RING, T], F32R), sb("h_lo", [P, RING, T], F32R)
        conv_acc = sb("conv_acc", [P, 2, T])
        qk_fm = sb("qk_fm", [P, HALVES, 2, T])
        wv = sb("wv", [P, 4, T])
        w_fm = wv[:, 0:2, :]
        v_fm = wv[:, 2:4, :]
        dv_fm = [wv[:, 0, :], wv[:, 1, :], arena[:, 6, 0:T], arena[:, 6, T:2 * T]]
        v_shift = sb("v_shift", [P, GROUPS, PAD + T])
        f_fm = sb("f_fm", [P, HEADS, T])
        rows_fm = sb("rows_fm", [96, T])
        rows_tok = sb("rows_tok", [P, 3, UNITS])
        nrm, inv = sb("nrm", [P, 2, UNITS]), sb("inv", [P, 2, UNITS])
        c1, c2n = sb("c1", [P, UNITS]), sb("c2n", [P, UNITS])
        l_tok = sb("l_tok", [P, UNITS, CHUNK])
        u_t = l_tok
        at_tok = sb("at_tok", [P, UNITS, CHUNK])
        l_prod = sb("l_prod", [CPT * UNITS, (CHUNK // 2) ** 2])
        t_tok = sb("t_tok", [P, UNITS, CHUNK])
        u1, u2n = sb("u1", [P, UNITS, CHUNK]), sb("u2n", [P, UNITS, CHUNK])
        s_sb = sb("s_sb", [P, HALVES, D])
        du = sb("du", [P, 2, HALVES, D])
        mx_tok = sb("mx_tok", [P, UNITS + HEADS, BR])
        stat_fm = sb("stat_fm", [P, T])
        lg_fm = stat_fm
        hid_fm = sb("hid_fm", [P, T])
        pre = h_f
        hm = sb("hm", [P, 2, T])
        lg = sb("lg", [P, UNITS, BR])
        lmax, lsum, linv = (sb(n, [P, UNITS]) for n in ("lmax", "lsum", "linv"))
        mix_w = sb("mix_w", [P, UNITS, BR])
        oss, onrm, oinv = (sb(n, [P, UNITS]) for n in ("oss", "onrm", "oinv"))
        taps_l = f_fm[:, 0, 0:GROUPS * (LONG + 1)].rearrange("p (g n) -> p g n", g=GROUPS)
        taps_s = f_fm[:, 1, 0:GROUPS * CONV].rearrange("p (g n) -> p g n", g=GROUPS)
        wv_flat = wv[:, :, :].rearrange("p a t -> p (a t)")
        stat_sel = wv_flat[0:D, 0:4 * BR * 3 * 32].rearrange("p (b m) -> p b m", m=3 * 32)
        mean_sel = wv[0:D, 3, 0:2 * P].rearrange("p (a m) -> p a m", a=2)
        stat_all = wv[0:3 * 32, 3, 2 * P:4 * P].rearrange("p (a m) -> p a m", a=2)
        head_mask = qk_fm[0:3 * 32, 0, 0, 0:HEADS]

        psum = ctx.enter_context(nc.psum_tensor("psum", [P, 8, 512], F32))
        BANKS = [psum[:, n, :] for n in range(8)]
        filled = [sem(f"filled{n}") for n in range(8)]
        emptied = [sem(f"emptied{n}") for n in range(8)]
        STATE = 7
        BY_ROWS = (0, 2, 1, 3)

        RECUR = [("du", (5, 6)), ("o", (0, 1) * TILES), ("state", (STATE,))]
        FFN_A = [("upa", (2, 3) + (2,) * (KT - 2)), ("outa", (3, 4))]
        STATS = [("dv_t", (0, 1, 5, 6)), ("stat", (2,))]
        LN2 = [("ln2", (7, 3)), ("beta", (7,)), ("k", (4, 0)), ("q", (5, 6)), ("v", (1, 2)), ("hidden", (3,))]
        GATE = [("gate", (4, 0, 5, 6))]
        K_Q = [("k_t", (7, 1)), ("ssq", (2,)), ("rows_t", (7,)), ("gram", (1, 2))]
        LOGIT = [("logit", (0,)), ("logit_t", (4,))]
        FIR = [("fir", (3, 5, 6, 7))]
        MIX = [("mix_t", (1, 2))]
        V_T = [("v_t", (3, 4))]
        WO = [("wo", (0, 5))]
        F_T = [("f_t", (1, 2, 3, 4))]
        FFN_C = [("ln3", (6, 7)), ("upc", (1, 7) * (KT // 2)), ("outc", (3, 4))]
        NEXT = [("next", (2, 6))]
        W = [("w", (0, 5, 1, 7))]
        first = [("next", (2, 6)), ("upa", (2, 0) * (KT // 2)), ("outa", (3, 4))]
        front = [LN2, K_Q, FIR, V_T, F_T]
        back = [RECUR, STATS, GATE, LOGIT, MIX, WO, FFN_C]
        both = [RECUR, FFN_A, STATS, LN2, GATE, K_Q, LOGIT, FIR, V_T, MIX, WO, F_T, FFN_C]
        ORDER = {"head": sum(front + [NEXT, W], first), "body": sum(both + [NEXT, W], []),
                 "last": sum(both + [W], []), "tail": sum(back, [])}
        ORDER = {m: [(w, k, b) for w, bs in o for k, b in enumerate(bs)] for m, o in ORDER.items()}
        QUIET = ("du", "state")

        class Pass:

            def __init__(self, mode, i=None):
                self.mode = mode
                self.i = None if mode == "head" else i
                self.j = 0 if mode == "head" else None if mode == "tail" else i + 1
                self.front, self.back = mode != "tail", mode != "head"
                self.next = mode in ("head", "body")

            def count(self, per):
                if self.mode == "head":
                    return 0
                if self.mode == "body":
                    return per("head") + self.i * per("body")
                return per("head") + (SEQS - 2) * per("body") + (per("last") if self.mode == "tail" else 0)

        def content(at, what, k):
            order = ORDER[at.mode]
            if what == "first":
                n = k
            else:
                n = [n for n, u in enumerate(order) if u[:2] == (what, k)][-1]
            b = order[n][2]
            uses = sum(u[2] == b for u in order[:n + 1])
            fills = sum(u[2] == b and u[0] not in QUIET for u in order[:n + 1])
            return b, at.count(lambda m: sum(u[2] == b for u in ORDER[m])) + uses, \
                at.count(lambda m: sum(u[2] == b and u[0] not in QUIET for u in ORDER[m])) + fills

        def claim(pe, at, what, k=0):
            b, uses, _ = content(at, what, k)
            pe.wait_ge(emptied[b], uses)
            return BANKS[b], filled[b]

        def arrive(eng, at, what, k=0):
            b, _, fills = content(at, what, k)
            eng.wait_ge(filled[b], fills)
            return BANKS[b], emptied[b]

        def copied(eng, at, what, k=0):
            b, uses, _ = content(at, what, k)
            eng.wait_ge(emptied[b], uses + 1)

        w_loaded = sem("w_loaded")
        c_loaded = sem("c_loaded")
        const_made = sem("const_made")
        setup_pe = sem("setup_pe")
        setup_dve = sem("setup_dve")
        x_loaded = sem("x_loaded")
        y_stored = sem("y_stored")
        bias1_added = sem("bias1_added")
        x2_begun = sem("x2_begun")
        bias2_added = sem("bias2_added")
        var_made = [sem(f"var_made{n}") for n in range(3)]
        std_made = [sem(f"std_made{n}") for n in range(3)]
        xn_made = [sem(f"xn_made{n}") for n in range(3)]
        next_ready = sem("next_ready")
        xhi_made = [sem(f"xhi_made{n}") for n in range(4)]
        gelu_made = [sem(f"gelu_made{n}") for n in range(2)]
        h_split = [sem(f"h_split{n}") for n in range(2)]
        h_used = [sem(f"h_used{n}") for n in range(2)]
        x1_made = sem("x1_made")
        y_made = sem("y_made")
        conv_made = sem("conv_made")
        silu_made = sem("silu_made")
        v_stored = sem("v_stored")
        v_shifted = sem("v_shifted")
        kq_squared = sem("kq_squared")
        kq_used = sem("kq_used")
        rows_made = sem("rows_made")
        nrm_made = sem("nrm_made")
        kqroot_made = sem("kqroot_made")
        l_made = sem("l_made")
        l_stored, l_loaded = sem("l_stored"), sem("l_loaded")
        inverted = sem("inverted")
        t_stored, t_loaded = sem("t_stored"), sem("t_loaded")
        u_made = sem("u_made")
        du_ready = sem("du_ready")
        du_made = sem("du_made")
        s_ready = sem("s_ready")
        s_made = sem("s_made")
        dl_made = sem("dl_made")
        stat_squared = sem("stat_squared")
        stat_used = sem("stat_used")
        max_made = sem("max_made")
        mean_made = sem("mean_made")
        stat_made = sem("stat_made")
        pre_made = sem("pre_made")
        hm_made = sem("hm_made")
        hm_used = sem("hm_used")
        lshift_made = sem("lshift_made")
        exp_made = sem("exp_made")
        mix_made = sem("mix_made")
        mix_squared = sem("mix_squared")
        onrm_made = sem("onrm_made")
        oroot_made = sem("oroot_made")
        norm_made = sem("norm_made")
        passed = sem("passed")
        dve_step = sem("dve_step")
        CHUNKS = TILES * CPT
        INV_STEPS = 2 * (CHUNK - 2)
        DVE_STEPS = {"head": 55, "body": 88, "last": 83, "tail": 38}
        CONST_MADE, C_LOADED, SETUP_DVE = 127, 57, 30

        x_v = x.rearrange("b (t p) c -> b p t c", p=P)
        out_v = out.rearrange("b (t p) c -> b p t c", p=P)

        def every_pass(eng, one_pass):
            one_pass(Pass("head"))
            with eng.Fori(0, SEQS - 2) as i:
                one_pass(Pass("body", i))
            one_pass(Pass("last", SEQS - 2))
            one_pass(Pass("tail", SEQS - 1))

        block = ctx.enter_context(nc.Block())

        @block.sync
        def _(sp):
            sp.dma_start(w1_st, w1.rearrange("(k p) n -> p k n", p=P)).then_inc(w_loaded, 16)
            sp.dma_start(w2_st, w2.rearrange("(k p) n -> p k n", p=P)).then_inc(w_loaded, 16)
            for n, w in enumerate((Wk, Wq, Wv)):
                sp.dma_start(wqkv_st[:, n], w.rearrange("(k p) n -> p k n", p=P)).then_inc(w_loaded, 16)
            sp.dma_start(wo_st, Wo.rearrange("(k p) n -> p k n", p=P)).then_inc(w_loaded, 16)
            sp.dma_start(wh_st, gW1[0:C, :].rearrange("(k p) n -> p k n", p=P)).then_inc(w_loaded, 16)
            sp.dma_start(b2_st, b2.partition_broadcast(P)).then_inc(w_loaded, 16)
            sp.sem_inc(y_stored, 1)

            def load_x(n):
                src = x_v[n:n + 1] if isinstance(n, int) else x_v[bass.ds(n, 1)]
                sp.dma_start(x_in[:, :, :], src.rearrange("a p t c -> (a p) t c")).then_inc(x_loaded, 16)

            load_x(0)

            def one_pass(at):
                if at.front:
                    j = at.j
                    if at.next:
                        sp.wait_ge(x1_made, 2 * j + 2)
                        load_x(j + 1)
                    sp.wait_ge(silu_made, 6 * j + 6)
                    sp.dma_start(v_dram.rearrange("h p t -> p h t"), v_fm).then_inc(v_stored, 16)
                    sp.wait_ge(v_stored, 16 * j + 16)
                    for s in range(CONV):
                        sp.dma_start(v_shift[32 * s:32 * s + 32, :, PAD + s:PAD + T],
                                     v_dram.rearrange("h (g c) t -> c (h g) t", c=32)[:, :, 0:T - s]).then_inc(v_shifted, 16)
                    sp.wait_ge(l_made, j + 1)
                    sp.dma_start(l_dram.rearrange("c i u j -> (c i) u j"), l_tok[:, :, :]).then_inc(l_stored, 16)
                    sp.wait_ge(l_stored, 16 * j + 16)
                    for c in range(CPT):
                        sp.dma_start(l_inv[UNITS * c:UNITS * c + UNITS, :, :],
                                     l_dram[c].rearrange("i u j -> u i j")).then_inc(l_loaded, 16)
                    sp.wait_ge(inverted, INV_STEPS * j + INV_STEPS)
                    sp.dma_start(t_dram.rearrange("c u i j -> (c u) i j"), l_inv[:, :, :]).then_inc(t_stored, 16)
                    sp.wait_ge(t_stored, 16 * j + 16)
                    for c in range(CPT):
                        sp.dma_start(t_tok[32 * c:32 * c + 32, :, :], t_dram[c].rearrange("u i j -> i u j")).then_inc(t_loaded, 16)
                if at.back:
                    i = at.i
                    sp.wait_ge(y_made, 2 * i + 2)
                    dst = out_v[i:i + 1] if isinstance(i, int) else out_v[bass.ds(i, 1)]
                    sp.dma_start(dst.rearrange("a p t c -> (a p) t c"), x2_tok[:, :, :]).then_inc(y_stored, 16)

            every_pass(sp, one_pass)
            sp.wait_ge(y_stored, SEQS * 16 + 1)

        @block.gpsimd
        def _(pool):
            made = 0

            def make(ins):
                nonlocal made
                made += 1
                ins.then_inc(const_made, 1)
                pool.wait_ge(const_made, made)

            loads = 0

            def load(dst, src, **kw):
                nonlocal loads
                loads += 1
                pool.dma_start(dst, src, **kw).then_inc(c_loaded, 16)

            for t, v in ((taps_l, 0.0), (taps_s, 0.0), (wb_pad[:, :, :], 0.0), (w2g_pad[:, :, :], 0.0),
                         (gb2_col[:, :], 0.0)):
                make(pool.memset(t, v))
            load(b1_col[:, :], b1.rearrange("(k p) -> p k", p=P), allow_slow_non_contiguous=True)
            load(gb1_col[:, :], gb1.rearrange("(p a) -> p a", a=1))
            for n, w in enumerate((kc_w, qc_w, vc_w)):
                load(conv_col[:, n], w.rearrange("(h p) j -> p h j", p=P))
            for s in range(CONV):
                rows = slice(32 * s, 32 * s + 32)
                load(taps_l[rows, :, 1:LONG + 1], fir_l.rearrange("h d j -> (h d) j").rearrange("(g c) j -> c g j", c=32))
                load(taps_s[rows, :, 1:SHORT + 1], fir_s.rearrange("h d j -> (h d) j").rearrange("(g c) j -> c g j", c=32))
            load(stat_rows, gW1[C:C + 3 * BR * D, :].rearrange("(s d) n -> d s n", d=D))
            br_rows = gW1[C + 3 * BR * D:, :].rearrange("(s d) n -> s d n", d=D)
            for n, pair in enumerate(((0, 1), (1, 0), (2, 3))):
                for half, b in enumerate(pair):
                    load(gate_w[D * half:D * half + D, n, :], br_rows[b])
            for h in range(HEADS):
                load(temp_col[32 * h:32 * h + 32, :], temp[h:h + 1].partition_broadcast(32))
                swap = (1, 0) if h % 2 else (0, 1)
                for slot, b in enumerate(swap):
                    load(gb2_col[32 * h + slot:32 * h + slot + 1, :], gb2[b:b + 1].rearrange("(p a) -> p a", a=1))
                    load(floor_b[:, h, slot:slot + 1], eps_floor[h, b:b + 1].partition_broadcast(P),
                         allow_slow_non_contiguous=True)
                load(gb2_col[32 * h + 2:32 * h + 4, :], gb2[2:4].rearrange("(p a) -> p a", a=1))
                load(floor_b[:, h, 2:4], eps_floor[h, 2:4].partition_broadcast(P))
            for h in range(2):
                load(onorm_col[D * h:D * h + D, :], onorm_w.rearrange("(p a) -> p a", a=1))
            load(wb_pad[:, :, 0:HEADS], Wb.rearrange("(k p) n -> p k n", p=P))
            for par in range(2):
                load(w2g_pad[:, par, 2:4], gW2[:, 2:4])
                for slot, b in enumerate((1, 0) if par else (0, 1)):
                    load(w2g_pad[:, par, slot:slot + 1], gW2[:, b:b + 1], allow_slow_non_contiguous=True)
            assert loads == C_LOADED, ("C_LOADED", loads)

            for t, v in ((ident[:, :], 0.0), (low_strict[:, :], 1.0), (up_incl[:, :], 1.0), (eye32[:, :], 0.0),
                         (stat_sel, 0.0), (mean_sel, 0.0), (head_mask, 0.0), (v_shift[:, :, :], 0.0),
                         (sq_sel[:, :, :, :], 0.0), (kq_sel[:, :, :], 0.0), (mx_tok[:, :, :], 0.0)):
                make(pool.memset(t, v))
            make(pool.affine_select(out=ident[:, :], in_=ident[:, :], compare_op=ALU.not_equal, fill=1.0, base=0,
                                    pattern=[[-1, P]], channel_multiplier=1))
            for c in range(CPT):
                rows = slice(32 * c, 32 * c + 32)
                make(pool.affine_select(out=low_strict[rows, :], in_=low_strict[rows, :], compare_op=ALU.is_gt, fill=0.0,
                                        base=0, pattern=[[-1, CHUNK]], channel_multiplier=1))
                make(pool.affine_select(out=up_incl[rows, :], in_=up_incl[rows, :], compare_op=ALU.is_ge, fill=0.0,
                                        base=0, pattern=[[1, CHUNK]], channel_multiplier=-1))
                make(pool.affine_select(out=eye32[rows, :], in_=eye32[rows, :], compare_op=ALU.not_equal, fill=1.0,
                                        base=0, pattern=[[-1, CHUNK]], channel_multiplier=1))
            for half in range(2):
                part = slice(D * half, D * half + D)
                make(pool.memset(mean_sel[:, half, part], 1.0 / D))
                for h in range(HEADS):
                    for pair in range(2):
                        at = BR * h + 2 * pair + half
                        make(pool.memset(sq_sel[part, pair, h, at:at + 1], 1.0))
                for hh in range(HALVES):
                    make(pool.memset(kq_sel[part, hh, 2 * hh + half:2 * hh + half + 1], 1.0))
            for par in range(2):
                for st in range(2):
                    for slot in range(BR):
                        for h in range(HEADS):
                            row = (64 if st else 32 * (h // 2)) + BR * h + slot
                            make(pool.memset(stat_sel[:, BR * (2 * par + st) + slot, row:row + 1], 1.0))
            for n in range(3):
                for slot in range(BR):
                    make(pool.affine_select(out=head_mask, in_=head_mask, compare_op=ALU.not_equal, fill=1.0,
                                            base=-(32 * n + slot), pattern=[[-BR, HEADS]], channel_multiplier=1))
            assert made == CONST_MADE, ("CONST_MADE", made)
            bias = b2_half[:, :].unsqueeze(1).broadcast_to([P, TILES, C])
            pool.wait_ge(setup_dve, SETUP_DVE)

            def one_pass(at):
                if at.back:
                    pool.wait_ge(y_stored, 16 * at.i + 1)
                    pool.wait_ge(x1_made, 2 * at.i + 2)
                    pool.sem_inc(passed, 1)
                    pool.tensor_copy(x2_tok[:, :, :], x1_tok[:, :, :]).then_inc(x2_begun, 1)
                    pool.wait_ge(x2_begun, at.i + 1)
                if at.front:
                    j = at.j
                    pool.wait_ge(x_loaded, 16 * j + 16)
                    pool.wait_ge(xn_made[0], j + 1)
                    pool.tensor_tensor(x_in[:, :, :], x_in[:, :, :], bias, ALU.add).then_inc(bias1_added, 1)
                    pool.wait_ge(bias1_added, j + 1)
                    pool.wait_ge(l_loaded, 64 * j + 64)
                    n = 0
                    for k in range(1, CHUNK - 1):
                        below = CHUNK - 1 - k
                        shape = [CPT * UNITS, below, k]
                        prod = l_prod[:, 0:below * k].rearrange("p (i j) -> p i j", i=below)
                        pool.tensor_tensor(prod, l_inv[:, k + 1:, k:k + 1].broadcast_to(shape),
                                           l_inv[:, k:k + 1, 0:k].broadcast_to(shape), ALU.mult).then_inc(inverted, 1)
                        n += 1
                        pool.wait_ge(inverted, INV_STEPS * j + n)
                        pool.tensor_tensor(l_inv[:, k + 1:, 0:k], l_inv[:, k + 1:, 0:k], prod, ALU.add).then_inc(inverted, 1)
                        n += 1
                        pool.wait_ge(inverted, INV_STEPS * j + n)
                    assert n == INV_STEPS
                if at.back:
                    pool.wait_ge(xn_made[2], at.i + 1)
                    pool.tensor_tensor(x2_tok[:, :, :], x2_tok[:, :, :], bias, ALU.add).then_inc(bias2_added, 1)
                    pool.wait_ge(bias2_added, at.i + 1)

            every_pass(pool, one_pass)

        @block.scalar
        def _(act):
            act.wait_ge(c_loaded, C_LOADED * 16)
            act.wait_ge(setup_dve, SETUP_DVE)

            def root(n, seq):
                act.wait_ge(var_made[n], seq + 1)
                act.activation(std[n], std[n], ACT.Sqrt).then_inc(std_made[n], 1)

            def high(at, n, seq, what):
                for h in range(HALVES):
                    bank, _ = arrive(act, at, what, h)
                    act.activation(xt_hi[:, h, :], bank, ACT.Copy).then_inc(xhi_made[n], 1)

            def gelu(at, f, seq, m):
                bank, read = arrive(act, at, ("upa", "upc")[f], m)
                if m >= 2:
                    act.wait_ge(h_split[f], KT * seq + m - 1)
                act.activation(h_f[:, m % 2, :], bank, ACT.Gelu, bias=b1_col[:, m:m + 1]).then_inc(read, 1)

            def out_of(at, what, k, dst, func=ACT.Copy, src=None, **kw):
                bank, read = arrive(act, at, what, k)
                act.activation(dst, bank if src is None else src(bank), func, **kw).then_inc(read, 1)

            def square(n, dst_used, seen, src, made):
                if n >= 2:
                    act.wait_ge(dst_used, seen + n - 1)
                act.activation(sq[:, n % 2, :], src, ACT.Square).then_inc(made, 1)

            after_state = {0: 0, 1: 1, 2: 2, 4: 3, 6: 4, 8: 5, 10: 6, 12: 7}

            def one_pass(at):
                i, j = at.i, at.j

                def silu(m):
                    act.wait_ge(conv_made, 6 * j + m + 1)
                    dst = qk_fm[:, m % 2, m // 2, :] if m < 4 else v_fm[:, m % 2, :]
                    act.activation(dst, conv_acc[:, m % 2, :], ACT.Silu).then_inc(silu_made, 1)

                if at.back:
                    for n in range(CHUNKS - 1):
                        act.wait_ge(s_ready, (CHUNKS - 1) * i + n + 1)
                        act.activation(s_sb[:, :, :], BANKS[STATE][:, 0:HALVES * D].rearrange("p (h d) -> p h d", h=HALVES),
                                       ACT.Copy).then_inc(s_made, 1)
                        if at.front and n in after_state:
                            gelu(at, 0, j, after_state[n])
                    act.wait_ge(s_made, (CHUNKS - 1) * (i + 1))
                    act.sem_inc(emptied[STATE], 1)
                    for k in range(2):
                        square(k, stat_used, 2 * HEADS * i, f_fm[:, BY_ROWS[k], :], stat_squared)
                    for h in range(HEADS):
                        out_of(at, "dv_t", h, dv_fm[h])
                    for k in range(2, HEADS):
                        square(k, stat_used, 2 * HEADS * i, f_fm[:, BY_ROWS[k], :], stat_squared)
                else:
                    root(0, j)
                    high(at, 0, j, "first")
                    for m in range(KT):
                        gelu(at, 0, j, m)
                if at.front:
                    root(1, j)
                if at.back:
                    copied(act, at, "dv_t", HEADS - 1)
                    for k, h in enumerate(BY_ROWS):
                        square(HEADS + k, stat_used, 2 * HEADS * i, dv_fm[h], stat_squared)
                if at.front:
                    high(at, 1, j, "ln2")
                if at.back:
                    act.wait_ge(mean_made, i + 1)
                    act.activation(stat_fm[0:64, :], stat_fm[0:64, :], ACT.Sqrt).then_inc(stat_made, 1)
                if at.front:
                    out_of(at, "beta", 0, rows_fm[64:96, :], ACT.Sigmoid, src=lambda b: b[64:96, :])
                    for m in range(4):
                        silu(m)
                    act.wait_ge(silu_made, 6 * j + 4)
                    for n in range(2):
                        square(n, kq_used, 3 * j, qk_fm[:, n % 2, n // 2, :], kq_squared)
                    for m in (4, 5):
                        silu(m)
                    for t in range(2):
                        out_of(at, "k_t", t, arena[:, 0, 512 * t:512 * t + 512])
                    for n in range(2, 4):
                        square(n, kq_used, 3 * j, qk_fm[:, n % 2, n // 2, :], kq_squared)
                    out_of(at, "ssq", 0, rows_fm[0:64, :], src=lambda b: b[0:64, :])
                    act.wait_ge(nrm_made, j + 1)
                    act.activation(nrm[:, :, :], nrm[:, :, :], ACT.Sqrt).then_inc(kqroot_made, 1)
                if at.back:
                    for h in range(HEADS):
                        act.wait_ge(pre_made, HEADS * i + h + 1)
                        if h >= 2:
                            act.wait_ge(hm_used, (HEADS - 1) * i + h - 1)
                        act.activation(hm[:, h % 2, :], pre[:, h % 2, :], ACT.Gelu, bias=gb1_col[:, 0:1]).then_inc(hm_made, 1)
                if at.front:
                    out_of(at, "hidden", 0, hid_fm[:, :])
                if at.back:
                    out_of(at, "logit", 0, lg_fm[:, :], ACT.Identity, bias=gbt_col[:, 0:1], scale=tinv_col[:, 0:1])
                    act.wait_ge(lshift_made, i + 1)
                    act.activation(lg[:, :, :], lg[:, :, :], ACT.Exp).then_inc(exp_made, 1)
                if at.front:
                    for h in range(2):
                        out_of(at, "fir", h, f_fm[:, h, :])
                if at.back:
                    act.wait_ge(mix_made, i + 1)
                    act.activation(sq_u, f_tok[:, :, 0, :], ACT.Square).then_inc(mix_squared, 1)
                    act.wait_ge(onrm_made, i + 1)
                    act.activation(onrm[:, :], onrm[:, :], ACT.Sqrt).then_inc(oroot_made, 1)
                if at.next:
                    root(0, j + 1)
                if at.front:
                    for h in range(2, HEADS):
                        out_of(at, "fir", h, f_fm[:, h, :])
                if at.back:
                    high(at, 3, i, "mix_t")
                if at.front:
                    for b in range(2):
                        out_of(at, "v_t", b, dv_tok[:, 8 * b:8 * b + 8, 1, :], src=lambda k: k.rearrange("p (u d) -> p u d", d=D))
                    for t in range(TILES):
                        out_of(at, "f_t", t, f_tok[:, HEADS * t:HEADS * t + HEADS, :, :],
                               src=lambda k: k.rearrange("p (u s d) -> p u s d", s=2, d=D))
                if at.back:
                    root(2, i)
                    high(at, 2, i, "ln3")
                    for m in range(KT):
                        gelu(at, 1, i, m)
                if at.next:
                    high(at, 0, j + 1, "next")

            every_pass(act, one_pass)

        def product3(pe, dst, a_hi, a_lo, b_hi, b_lo, first, last, **kw):
            pe.matmul(dst, a_hi, b_hi, start=first, stop=False, **kw)
            pe.matmul(dst, a_hi, b_lo, start=False, stop=False, **kw)
            return pe.matmul(dst, a_lo, b_hi, start=False, stop=last, **kw)

        @block.tensor
        def _(pe):
            pe.wait_ge(const_made, CONST_MADE)
            pe.wait_ge(c_loaded, C_LOADED * 16)
            for n, pair in enumerate(((0, 1), (1, 0), (2, 3))):
                for half, b in enumerate(pair):
                    pe.matmul(BANKS[0][:, P * n:P * n + P], mean_sel[:, half, :], stat_rows[:, 3 * b, :],
                              start=(half == 0), stop=(half == 1))
            for par in range(2):
                slots = (1, 0, 2, 3) if par else (0, 1, 2, 3)
                for n in range(2 * BR):
                    last = pe.matmul(BANKS[1][0:96, P * par:P * par + P], stat_sel[:, 2 * BR * par + n, :],
                                     stat_rows[:, 3 * slots[n % BR] + 1 + n // BR, :], start=(n == 0), stop=(n == 2 * BR - 1))
            last.then_inc(setup_pe, 1)
            pe.wait_ge(setup_dve, SETUP_DVE)

            def turn(at, what, k, src):
                bank, full = claim(pe, at, what, k)
                for n in range(4):
                    last = pe.transpose(bank[:, P * n:P * n + P], src(n), ident[:, :])
                last.then_inc(full, 1)

            def turn_rows(at, what, made, count):
                pe.wait_ge(made, count)
                for h in range(HALVES):
                    turn(at, what, h, lambda t: xn_tok[:, t, P * h:P * h + P])

            def to_tok(at, what, src):
                for t in range(2):
                    turn(at, what, t, lambda n: src(n % 2)[:, P * (2 * t + n // 2):P * (2 * t + n // 2) + P])

            def ffn(at, f, seq):
                up, outs = ("upa", "outa") if f == 0 else ("upc", "outc")
                state = {}

                def up_step(m, k):
                    if k == 0:
                        state["up"] = claim(pe, at, up, m)
                        if m == 0 and f == 0:
                            pe.wait_ge(next_ready, seq + 1)
                        elif m == 0:
                            copied(pe, at, "ln3", 0)
                            copied(pe, at, "ln3", 1)
                    bank, full = state["up"]
                    cols = slice(P * m, P * m + P)
                    last = product3(pe, bank, w1_hi[:, k, cols], w1_lo[:, k, cols], xt_hi[:, k, :], xt_lo[:, k, :],
                                    k == 0, k == HALVES - 1)
                    if k == HALVES - 1:
                        last.then_inc(full, 1)

                def down_step(m, pair):
                    if pair == 0:
                        pe.wait_ge(h_split[f], KT * seq + m + 1)
                    if m == 0:
                        state[pair] = claim(pe, at, outs, pair)
                    for t in (2 * pair, 2 * pair + 1):
                        last = product3(pe, state[pair][0][:, C * (t % 2):C * (t % 2) + C], h_hi[:, m % RING, P * t:P * t + P],
                                        h_lo[:, m % RING, P * t:P * t + P], w2_hi[:, m, :], w2_lo[:, m, :],
                                        m == 0 and t % 2 == 0, m == KT - 1, skip_group_check=True)
                    if m == KT - 1:
                        last.then_inc(state[pair][1], 1)
                    elif pair == 1:
                        last.then_inc(h_used[f], 1)

                steps = [(up_step, m, k) for m in (0, 1) for k in range(2)]
                for m in range(2, KT):
                    steps += [(up_step, m, k) for k in range(2)] + [(down_step, m - 2, k) for k in range(2)]
                steps += [(down_step, m, k) for m in (KT - 2, KT - 1) for k in range(2)]
                return [lambda step=step, m=m, k=k: step(m, k) for step, m, k in steps]

            by_head = [(2 * half + p, p, half, slice(D * p, D * p + D), slice(D * half, D * half + D))
                       for half in range(HALVES) for p in range(2)]

            def chunk(at, t, c, pu, po, o_full, fill):
                i = at.i
                rows = slice(32 * c, 32 * c + 32)
                cols_t = slice(P * t + CHUNK * c, P * t + CHUNK * c + CHUNK)
                n = CPT * t + c
                pe.sem_inc(passed, 1)
                for h, p, half, part, cols in by_head:
                    last = pe.matmul(pu[p][rows, cols], u1[rows, HEADS * t + h, :], dv_tok[rows, HEADS * t + h, 1, :],
                                     start=(half == 0), stop=(n == 0), skip_group_check=True)
                if n > 0:
                    pe.wait_ge(s_made, (CHUNKS - 1) * i + n)
                    pe.sem_inc(passed, 1)
                    for h, p, half, part, cols in by_head:
                        last = pe.matmul(pu[p][rows, cols], w_fm[part, half, cols_t], s_sb[part, half, :],
                                         start=False, stop=True, skip_group_check=True)
                last.then_inc(du_ready, 1)
                if n > 0:
                    for h, p, half, part, cols in by_head:
                        pe.matmul(po[p][rows, cols], qk_fm[part, half, 1, cols_t], s_sb[part, half, :],
                                  start=(half == 0), stop=False, skip_group_check=True)
                fill()
                pe.wait_ge(du_made, CHUNKS * i + n + 1)
                if n < CHUNKS - 1:
                    for h, p, half, part, cols in by_head:
                        last = pe.matmul(BANKS[STATE][part, cols], k_tok[rows, t, D * h:D * h + D],
                                         du[rows, p, half, :], start=(n == 0 and half == 0), stop=(n == CHUNKS - 2),
                                         skip_group_check=True)
                    last.then_inc(s_ready, 1)
                else:
                    pe.sem_inc(passed, 1)
                for h, p, half, part, cols in by_head:
                    last = pe.matmul(po[p][rows, cols], at_tok[rows, HEADS * t + h, :], du[rows, p, half, :],
                                     start=(n == 0 and half == 0), stop=True, skip_group_check=True)
                    if c == CPT - 1 and half == HALVES - 1:
                        last.then_inc(o_full[p], 1)
                fill()

            def projection(at, what, m, which):
                bank, full = claim(pe, at, what, m)
                cols = slice(P * m, P * m + P)
                for k in range(HALVES):
                    last = product3(pe, bank, wqkv_hi[:, which, k, cols], wqkv_lo[:, which, k, cols], xt_hi[:, k, :],
                                    xt_lo[:, k, :], k == 0, k == HALVES - 1)
                last.then_inc(full, 1)

            def gate(at, h):
                bank, full = claim(pe, at, "gate", h)
                pe.matmul(bank, gate_w[:, h % 2, :], f_fm[:, h, :], start=True, stop=False)
                pe.matmul(bank, gate_w[:, 2, :], dv_fm[h], start=False, stop=False)
                if h == 0:
                    pe.wait_ge(stat_made, at.i + 1)
                pe.matmul(bank, gate_st[:, h, :], stat_fm[0:96, :], start=False, stop=True).then_inc(full, 1)

            def firs(at, a, between=None):
                banks = [claim(pe, at, "fir", 2 * a + p) for p in range(2)]
                for n in [TAPG] + list(range(TAPG)):
                    if n == 2 and between:
                        between()
                    for p in range(2):
                        for g in range(2):
                            col = D * (p if n == TAPG else 1 - p) + 32 * g
                            group = 2 * (2 * a + p) + g
                            at_t = PAD if n == TAPG else 4 * n
                            last = pe.matmul(banks[p][0][col:col + 32, :], fir_w[:, group, n, :],
                                             v_shift[:, group, at_t:at_t + T], start=(n in (0, TAPG)), stop=(n >= TAPG - 1))
                        if n == TAPG - 1:
                            last.then_inc(banks[p][1], 1)

            def one_pass(at):
                i, j = at.i, at.j

                def logits_to_tok():
                    copied(pe, at, "logit")
                    turn(at, "logit_t", 0, lambda t: lg_fm[:, P * t:P * t + P])

                steps = ffn(at, 0, j) if at.front else []
                if at.back:
                    pu = [claim(pe, at, "du", p)[0] for p in range(2)]
                    claim(pe, at, "state")

                    def fill():
                        if steps:
                            steps.pop(0)()

                    for t in range(TILES):
                        po, o_full = zip(*[claim(pe, at, "o", 2 * t + p) for p in range(2)])
                        for c in range(CPT):
                            chunk(at, t, c, pu, po, o_full, fill)
                else:
                    turn_rows(at, "first", xn_made[0], j + 1)
                for step in steps:
                    step()
                if at.back:
                    pe.wait_ge(dl_made, TILES * i + TILES)
                    for h in range(HEADS):
                        turn(at, "dv_t", h, lambda t: dv_tok[:, HEADS * t + h, :, :].rearrange("p s d -> p (s d)"))
                    bank, full = claim(pe, at, "stat")
                    for pair in range(2):
                        for k, h in enumerate(BY_ROWS):
                            n = HEADS * pair + k
                            pe.wait_ge(stat_squared, 2 * HEADS * i + n + 1)
                            pe.matmul(bank[32 * (h // 2):32 * (h // 2) + 32, :], sq_sel[:, pair, h, :], sq[:, n % 2, :],
                                      start=(n < 2), stop=(n >= 2 * HEADS - 2), skip_group_check=True).then_inc(stat_used, 1)
                    pe.wait_ge(max_made, i + 1)
                    mx = mx_tok[:, :, :].rearrange("p u s -> p (u s)")
                    for t in range(TILES):
                        last = pe.matmul(bank[64:96, P * t:P * t + P], mx[:, BR * HEADS * t:BR * HEADS * t + 32], ident[:, :],
                                         start=True, stop=True)
                    last.then_inc(full, 1)
                if at.front:
                    turn_rows(at, "ln2", xn_made[1], j + 1)
                    copied(pe, at, "ln2", 0)
                    copied(pe, at, "ln2", 1)
                    bank, full = claim(pe, at, "beta")
                    for k in range(HALVES):
                        for n, part in enumerate((xt_hi, xt_lo)):
                            last = pe.matmul(bank[64:96, :], wb_pad[:, k, :], part[:, k, :].bitcast(F32),
                                             start=(k + n == 0), stop=(k + n == 2))
                    last.then_inc(full, 1)
                    for what, which in (("k", 0), ("q", 1), ("v", 2)):
                        for m in range(2):
                            projection(at, what, m, which)
                    bank, full = claim(pe, at, "hidden")
                    for k in range(HALVES):
                        last = product3(pe, bank, wh_hi[:, k, :], wh_lo[:, k, :], xt_hi[:, k, :], xt_lo[:, k, :],
                                        k == 0, k == HALVES - 1)
                    last.then_inc(full, 1)
                if at.back:
                    copied(pe, at, "dv_t", HEADS - 1)
                    for h in range(HEADS):
                        gate(at, h)
                if at.front:
                    pe.wait_ge(silu_made, 6 * j + 4)
                    to_tok(at, "k_t", lambda h: qk_fm[:, h, 0, :])
                    bank, full = claim(pe, at, "ssq")
                    for n in range(4):
                        pe.wait_ge(kq_squared, 4 * j + n + 1)
                        rows = slice(32 * (n // 2), 32 * (n // 2) + 32)
                        last = pe.matmul(bank[rows, :], kq_sel[:, n % 2, :], sq[:, n % 2, :], start=(n % 2 == 0),
                                         stop=(n % 2 == 1), skip_group_check=True)
                        last.then_inc(kq_used if n < 3 else full, 1)
                    copied(pe, at, "beta")
                    copied(pe, at, "ssq")
                    bank, full = claim(pe, at, "rows_t")
                    for t in range(TILES):
                        last = pe.transpose(bank[:, 96 * t:96 * t + 96], rows_fm[:, P * t:P * t + P], ident[0:96, 0:96])
                    last.then_inc(full, 1)
                    grams = [claim(pe, at, "gram", b) for b in range(2)]
                    pe.sem_inc(passed, 1)
                    for u in range(UNITS // 2):
                        t, half = u // HALVES, u % HALVES
                        for c in range(CPT):
                            cols = slice(P * t + CHUNK * c, P * t + CHUNK * c + CHUNK)
                            for b in range(2):
                                rows = slice(D * b, D * b + D)
                                last = pe.matmul(grams[b][0][32 * c:32 * c + 32, D * u:D * u + D], qk_fm[rows, half, 0, cols],
                                                 qk_fm[rows, half, :, cols], start=True, stop=True)
                                if u == UNITS // 2 - 1 and c == CPT - 1:
                                    last.then_inc(grams[b][1], 1)
                if at.back:
                    lbank, lfull = claim(pe, at, "logit")
                    for h in range(HEADS):
                        pe.wait_ge(hm_made, HEADS * i + h + 1)
                        last = pe.matmul(lbank[32 * h:32 * h + 32, :], w2g_pad[:, h % 2, :], hm[:, h % 2, :],
                                         start=True, stop=True)
                        last.then_inc(hm_used if h < HEADS - 1 else lfull, 1)
                if at.front:
                    pe.wait_ge(v_shifted, 64 * j + 64)
                    firs(at, 0, between=logits_to_tok if at.back else None)
                    firs(at, 1)
                else:
                    logits_to_tok()
                if at.front:
                    pe.wait_ge(silu_made, 6 * j + 6)
                    to_tok(at, "v_t", lambda h: v_fm[:, h, :])
                if at.back:
                    pe.wait_ge(norm_made, i + 1)
                    for h in range(HALVES):
                        turn(at, "mix_t", h, lambda t: xn_tok[:, t, P * h:P * h + P])
                if at.back:
                    copied(pe, at, "mix_t", 0)
                    copied(pe, at, "mix_t", 1)
                    for b in range(2):
                        bank, full = claim(pe, at, "wo", b)
                        for t in (2 * b, 2 * b + 1):
                            for k in range(HALVES):
                                rows = slice(P * t, P * t + P)
                                last = product3(pe, bank[:, C * (t % 2):C * (t % 2) + C], xt_hi[:, k, rows], xt_lo[:, k, rows],
                                                wo_hi[:, k, :], wo_lo[:, k, :], k == 0, k == HALVES - 1)
                        last.then_inc(full, 1)
                if at.front:
                    copied(pe, at, "fir", HEADS - 1)
                    for t in range(TILES):
                        turn(at, "f_t", t, lambda h: f_fm[:, h, P * t:P * t + P])
                ending = 2
                steps = []
                if at.back:
                    turn_rows(at, "ln3", xn_made[2], i + 1)
                    steps = ffn(at, 1, i)
                    for step in steps[:-ending]:
                        step()
                if at.next:
                    turn_rows(at, "next", xn_made[0], j + 2)
                for step in steps[-ending:]:
                    step()
                if at.front:
                    pe.wait_ge(u_made, j + 1)
                    banks = [claim(pe, at, "w", c) for c in range(CPT)]
                    pe.sem_inc(passed, 1)
                    for t in range(TILES):
                        for h in range(HEADS):
                            cols = slice(P * (h // 2) + CHUNK * t, P * (h // 2) + CHUNK * t + CHUNK)
                            for c in range(CPT):
                                rows = slice(32 * c, 32 * c + 32)
                                last = pe.matmul(banks[c][0][D * (h % 2):D * (h % 2) + D, cols], k_tok[rows, t, D * h:D * h + D],
                                                 u2n[rows, HEADS * t + h, :], start=True, stop=True)
                                if t == TILES - 1 and h == HEADS - 1:
                                    last.then_inc(banks[c][1], 1)
                    copied(pe, at, "v_t", 1)
                    for c in range(CPT):
                        copied(pe, at, "w", c)

            every_pass(pe, one_pass)

        @block.vector
        def _(dve):
            n = 0

            def step(ins):
                nonlocal n
                n += 1
                ins.then_inc(setup_dve, 1)

            def settle():
                dve.wait_ge(setup_dve, n)

            dve.wait_ge(w_loaded, 8 * 16)
            dve.wait_ge(const_made, CONST_MADE)
            dve.wait_ge(c_loaded, C_LOADED * 16)
            for s in range(CONV):
                rows = slice(32 * s, 32 * s + 32)
                shape = [32, GROUPS, TAPG, 32]
                e = eye32[rows, :].unsqueeze(1).broadcast_to([32, GROUPS * TAPG, 32]).rearrange("p (g n) c -> p g n c", g=GROUPS)
                tap = taps_l[rows, :, 3 - s:3 - s + 4 * (TAPG - 1) + 1:4]
                step(dve.tensor_tensor(fir_w[rows, :, 0:TAPG, :], e, tap.unsqueeze(3).broadcast_to(shape), ALU.mult))
                step(dve.tensor_tensor(fir_w[rows, :, TAPG, :], eye32[rows, :].unsqueeze(1).broadcast_to([32, GROUPS, 32]),
                                       taps_s[rows, :, 3 - s:4 - s].broadcast_to([32, GROUPS, 32]), ALU.mult))
            step(dve.tensor_scalar(b2_half[:, :], b2_st, 0.5, None, ALU.mult))
            step(dve.tensor_scalar(temp_col[:, :], temp_col[:, :], 0.2, 10.0, ALU.max, ALU.min))
            settle()
            step(dve.reciprocal(tinv_col[:, :], temp_col[:, :]))
            settle()
            step(dve.tensor_tensor(gbt_col[:, :], gb2_col[:, :], tinv_col[:, :], ALU.mult))
            step(dve.tensor_scalar(floor_b[:, :, :], floor_b[:, :, :], 1e-7, 0.1, ALU.max, ALU.min))
            step(dve.tensor_scalar(wo_st, wo_st, onorm_col[:, 0:1], None, ALU.mult))
            settle()
            for hi, lo, st in ((w1_hi, w1_lo, w1_st), (w2_hi, w2_lo, w2_st), (wqkv_hi, wqkv_lo, wqkv_st),
                               (wo_hi, wo_lo, wo_st), (wh_hi, wh_lo, wh_st)):
                dims = (slice(None),) * len(hi.shape)
                step(dve.tensor_copy(hi[dims], st))
                settle()
                step(dve.tensor_tensor(lo[dims], st, hi[dims].bitcast(F32), ALU.subtract))
            dve.wait_ge(setup_pe, 1)
            step(dve.tensor_tensor(gate_w[:, :, :], gate_w[:, :, :],
                                   BANKS[0][:, 0:3 * P].rearrange("p (b n) -> p b n", b=3), ALU.add))
            step(dve.tensor_copy(stat_all, BANKS[1][0:96, 0:2 * P].rearrange("p (b n) -> p b n", b=2)))
            settle()
            for h in range(HEADS):
                step(dve.tensor_scalar(gate_st[:, h, :], stat_all[:, h % 2, :], head_mask[:, h:h + 1], None, ALU.mult))
            settle()
            assert n == SETUP_DVE, ("SETUP_DVE", n)
            for bank in emptied:
                dve.sem_inc(bank, 1)

            after_du = {2: 0, 4: 1, 5: 2, 6: 3, 8: 4, 10: 5, 12: 6, 13: 7}

            def one_pass(at):
                i, j = at.i, at.j
                links = at.count(lambda m: DVE_STEPS[m])
                n = 0

                def link(ins):
                    nonlocal n
                    n += 1
                    ins.then_inc(dve_step, 1)
                    dve.wait_ge(dve_step, links + n)

                def stats(k, src):
                    for t in range(TILES):
                        last = dve.bn_stats(bn[:, t, :], src[:, t, :])
                    link(last)
                    dve.sem_inc(passed, 1)
                    for t in range(TILES):
                        last = dve.bn_aggr(mv[k][:, t, :], bn[:, t, :])
                    link(last)
                    dve.tensor_scalar(std[k], mv[k][:, :, 1], 1e-5, None, ALU.add).then_inc(var_made[k], 1)

                def normalise(k, seq, src):
                    dve.wait_ge(std_made[k], seq + 1)
                    link(dve.reciprocal(rstd[:, :], std[k]))
                    for t in range(TILES):
                        last = dve.tensor_scalar(xn_tok[:, t, :], src[:, t, :], mv[k][:, t, 0:1], rstd[:, t:t + 1],
                                                 ALU.subtract, ALU.mult)
                    last.then_inc(xn_made[k], 1)

                def low(k, seq, what):
                    for h in range(HALVES):
                        bank, read = arrive(dve, at, what, h)
                        dve.wait_ge(xhi_made[k], 2 * seq + h + 1)
                        ins = dve.tensor_tensor(xt_lo[:, h, :], bank, xt_hi[:, h, :].bitcast(F32), ALU.subtract)
                        if k > 0:
                            ins.then_inc(read, 1)
                        else:
                            link(ins)
                            dve.sem_inc(read, 1)
                    if k == 0:
                        dve.sem_inc(next_ready, 1)

                def split(f, seq, m):
                    copied(dve, at, ("upa", "upc")[f], m)
                    if m >= RING:
                        dve.wait_ge(h_used[f], (KT - 1) * seq + m - RING + 1)
                    link(dve.tensor_copy(h_hi[:, m % RING, :], h_f[:, m % 2, :]))
                    dve.tensor_tensor(h_lo[:, m % RING, :], h_f[:, m % 2, :], h_hi[:, m % RING, :].bitcast(F32),
                                      ALU.subtract).then_inc(h_split[f], 1)

                def residual(what, dst, base, made=None):
                    for b in range(2):
                        bank, read = arrive(dve, at, what, b)
                        two = slice(2 * b, 2 * b + 2)
                        link(dve.scalar_tensor_tensor(out=dst[:, two, :], in0=bank.rearrange("p (t c) -> p t c", t=2),
                                                      scalar=0.5, in1=base[:, two, :], op0=ALU.mult, op1=ALU.add))
                        dve.sem_inc(read, 1)
                        dve.sem_inc(made, 1)

                def conv(m):
                    which = m // 2
                    bank, read = arrive(dve, at, "kqv"[which], m % 2)
                    w = conv_col[:, which, m % 2, :]
                    acc = conv_acc[:, m % 2, :]
                    if m >= 2:
                        dve.wait_ge(silu_made, 6 * j + m - 1)
                    link(dve.tensor_scalar(acc, bank, w[:, CONV - 1:CONV], None, ALU.mult))
                    for s in range(1, CONV):
                        link(dve.scalar_tensor_tensor(out=acc[:, s:], in0=bank[:, 0:T - s], scalar=w[:, CONV - 1 - s:CONV - s],
                                                      in1=acc[:, s:], op0=ALU.mult, op1=ALU.add))
                    dve.sem_inc(read, 1)
                    dve.sem_inc(conv_made, 1)

                def per_row(v, m):
                    return v.unsqueeze(2).broadcast_to([P, UNITS, m])

                if at.back:
                    for t in range(TILES):
                        for c in range(CPT):
                            rows = slice(32 * c, 32 * c + 32)
                            k = CPT * t + c
                            dve.wait_ge(du_ready, CHUNKS * i + k + 1)
                            dve.tensor_copy(du[rows, :, :, :], psum[rows, 5:7, 0:HALVES * D]
                                            .rearrange("p a (h d) -> p a h d", h=HALVES)).then_inc(du_made, 1)
                            if at.front:
                                if k in after_du:
                                    split(0, j, after_du[k])
                        reads = [arrive(dve, at, "o", 2 * t + p)[1] for p in range(2)]
                        us = slice(HEADS * t, HEADS * t + HEADS)
                        for p in range(2):
                            ins = dve.tensor_tensor(dv_tok[:, us, 0, :][:, p::2, :],
                                                    psum[:, p, 0:HALVES * D].rearrange("p (h d) -> p h d", h=HALVES),
                                                    inv[:, 1, us][:, p::2].unsqueeze(2).broadcast_to([P, HALVES, D]), ALU.mult)
                        link(ins)
                        for read in reads:
                            dve.sem_inc(read, 1)
                        dve.sem_inc(dl_made, 1)
                    dve.wait_ge(du_made, CHUNKS * i + CHUNKS)
                    for b in (5, 6):
                        dve.sem_inc(emptied[b], 1)
                else:
                    dve.wait_ge(x_loaded, 16)
                    stats(0, x_in)
                    normalise(0, j, x_in)
                    low(0, j, "first")
                    for m in range(KT):
                        split(0, j, m)
                if at.front:
                    dve.wait_ge(bias1_added, j + 1)
                    if at.back:
                        dve.wait_ge(x2_begun, i + 1)
                    residual("outa", x1_tok, x_in, x1_made)
                    stats(1, x1_tok)
                if at.back:
                    dve.tensor_reduce(mx_tok[:, 0:UNITS, 0:2], f_tok[:, :, :, :], AX.X, ALU.max)
                    dve.tensor_reduce(mx_tok[:, 0:UNITS, 2:4], dv_tok[:, :, :, :], AX.X, ALU.max).then_inc(max_made, 1)
                if at.front:
                    normalise(1, j, x1_tok)
                    low(1, j, "ln2")
                if at.back:
                    bank, read = arrive(dve, at, "stat")
                    dve.tensor_copy(stat_fm[64:96, :], bank[64:96, :])
                    link(dve.tensor_scalar(stat_fm[0:64, :], bank[0:64, :], 1.0 / D, 1e-8, ALU.mult, ALU.max))
                    dve.sem_inc(read, 1)
                    dve.sem_inc(mean_made, 1)
                def hidden(h):
                    bank, read = arrive(dve, at, "gate", h)
                    if h >= 2:
                        dve.wait_ge(hm_made, HEADS * i + h - 1)
                    link(dve.tensor_tensor(pre[:, h % 2, :], bank, hid_fm[:, :], ALU.add))
                    dve.sem_inc(read, 1)
                    dve.sem_inc(pre_made, 1)

                if at.front:
                    for m in range(6):
                        conv(m)
                if at.back:
                    hidden(0)
                    hidden(1)
                if at.front:
                    bank, read = arrive(dve, at, "rows_t")
                    for r in range(3):
                        ins = dve.tensor_copy(rows_tok[:, r, :].rearrange("p (t h) -> p t h", t=TILES),
                                              bank[:, 0:TILES * 96].rearrange("p (t r h) -> p t r h", t=TILES, r=3)[:, :, r, 0:HEADS])
                    link(ins)
                    dve.sem_inc(read, 1)
                    dve.tensor_scalar(nrm[:, :, :], rows_tok[:, 0:2, :], 1e-6, None, ALU.add).then_inc(nrm_made, 1)
                    dve.wait_ge(kqroot_made, j + 1)
                    link(dve.reciprocal(inv[:, :, :], nrm[:, :, :]))
                    link(dve.tensor_tensor(c1[:, :], rows_tok[:, 2, :], inv[:, 0, :], ALU.mult))
                    link(dve.scalar_tensor_tensor(out=c2n[:, :], in0=c1[:, :], scalar=-1.0, in1=inv[:, 0, :],
                                                  op0=ALU.mult, op1=ALU.mult))
                if at.front:
                    for b in range(2):
                        bank, read = arrive(dve, at, "gram", b)
                        g = bank.rearrange("p (u a j) -> p u a j", u=UNITS // 2, a=2)
                        shape = [P, UNITS // 2, CHUNK]
                        link(dve.tensor_tensor(l_tok[:, b::2, :], g[:, :, 0, :], c2n[:, b::2].unsqueeze(2).broadcast_to(shape),
                                               ALU.mult))
                        dve.tensor_tensor(at_tok[:, b::2, :], g[:, :, 1, :], up_incl[:, :].unsqueeze(1).broadcast_to(shape),
                                          ALU.mult).then_inc(read, 1)
                    dve.tensor_tensor(l_tok[:, :, :], l_tok[:, :, :],
                                      low_strict[:, :].unsqueeze(1).broadcast_to([P, UNITS, CHUNK]), ALU.mult).then_inc(l_made, 1)
                if at.back:
                    hidden(2)
                    hidden(3)
                if at.next:
                    dve.wait_ge(x_loaded, 16 * j + 32)
                    stats(0, x_in)
                if at.back:
                    bank, read = arrive(dve, at, "logit_t")
                    link(dve.tensor_copy(lg[:, :, :].rearrange("p (t h) b -> p t h b", t=TILES),
                                         bank.rearrange("p (t h b) -> p t h b", t=TILES, h=HEADS)[:, :, :, 0:BR]))
                    dve.sem_inc(read, 1)
                    link(dve.tensor_reduce(lmax[:, :], lg[:, :, :], AX.X, ALU.max))
                    dve.tensor_tensor(lg[:, :, :], lg[:, :, :], per_row(lmax[:, :], BR), ALU.subtract).then_inc(lshift_made, 1)
                    dve.wait_ge(exp_made, i + 1)
                    link(dve.tensor_reduce(lsum[:, :], lg[:, :, :], AX.X, ALU.add))
                    link(dve.reciprocal(linv[:, :], lsum[:, :]))
                    link(dve.tensor_tensor(lg[:, :, :], lg[:, :, :], per_row(linv[:, :], BR), ALU.mult))
                    rows = lg[:, :, :].rearrange("p (t h) b -> p t (h b)", t=TILES)
                    link(dve.tensor_tensor(rows, rows, floor_b[:, :, :].rearrange("p h b -> p (h b)").unsqueeze(1)
                                           .broadcast_to([P, TILES, HEADS * BR]), ALU.max))
                    link(dve.tensor_reduce(lsum[:, :], lg[:, :, :], AX.X, ALU.add))
                    link(dve.reciprocal(linv[:, :], lsum[:, :]))
                    link(dve.tensor_tensor(mix_w[:, :, :], lg[:, :, :], per_row(linv[:, :], BR), ALU.mult))
                    for src, s in ((f_tok, 0), (dv_tok, 2)):
                        link(dve.tensor_tensor(src[:, :, :, :], src[:, :, :, :],
                                               mix_w[:, :, s:s + 2].unsqueeze(3).broadcast_to([P, UNITS, 2, D]), ALU.mult))
                    link(dve.tensor_tensor(f_tok[:, :, :, :], f_tok[:, :, :, :], dv_tok[:, :, :, :], ALU.add))
                    dve.tensor_tensor(f_tok[:, :, 0, :], f_tok[:, :, 0, :], f_tok[:, :, 1, :], ALU.add).then_inc(mix_made, 1)
                if at.back:
                    dve.wait_ge(mix_squared, i + 1)
                    link(dve.tensor_reduce(oss[:, :], sq_u, AX.X, ALU.add))
                    dve.tensor_scalar(onrm[:, :], oss[:, :], 1.0 / D, 1e-5, ALU.mult, ALU.add).then_inc(onrm_made, 1)
                    dve.wait_ge(oroot_made, i + 1)
                    link(dve.reciprocal(oinv[:, :], onrm[:, :]))
                    dve.tensor_tensor(xn_u, f_tok[:, :, 0, :], per_row(oinv[:, :], D), ALU.mult).then_inc(norm_made, 1)
                    low(3, i, "mix_t")
                    dve.wait_ge(x2_begun, i + 1)
                    for b in range(2):
                        bank, read = arrive(dve, at, "wo", b)
                        two = slice(2 * b, 2 * b + 2)
                        link(dve.tensor_tensor(x2_tok[:, two, :], bank.rearrange("p (t c) -> p t c", t=2), x2_tok[:, two, :],
                                               ALU.add))
                        dve.sem_inc(read, 1)
                    stats(2, x2_tok)
                    normalise(2, i, x2_tok)
                    low(2, i, "ln3")
                if at.next:
                    normalise(0, j + 1, x_in)
                if at.back:
                    for m in range(KT):
                        split(1, i, m)
                if at.next:
                    low(0, j + 1, "next")
                if at.front:
                    dve.wait_ge(t_loaded, 64 * j + 64)
                    link(dve.transpose(u_t[:, :, :].rearrange("p u j -> p (u j)"), t_tok[:, :, :].rearrange("p u j -> p (u j)")))
                    link(dve.tensor_tensor(u_t[:, :, :], u_t[:, :, :], eye32[:, :].unsqueeze(1).broadcast_to([P, UNITS, CHUNK]),
                                           ALU.add))
                    dve.tensor_tensor(u1[:, :, :], u_t[:, :, :], per_row(c1[:, :], CHUNK), ALU.mult)
                    dve.tensor_tensor(u2n[:, :, :], u_t[:, :, :], per_row(c2n[:, :], CHUNK), ALU.mult).then_inc(u_made, 1)
                if at.back:
                    dve.wait_ge(bias2_added, i + 1)
                    residual("outc", x2_tok, x2_tok, y_made)
                if at.front:
                    for c in range(CPT):
                        bank, read = arrive(dve, at, "w", c)
                        dve.tensor_copy(w_fm.rearrange("p h (t c j) -> p h t c j", t=TILES, c=CPT)[:, :, :, c, :],
                                        bank[:, 0:HALVES * P].rearrange("p (h t j) -> p h t j", h=HALVES, t=TILES)).then_inc(read, 1)
                assert n == DVE_STEPS[at.mode], ("DVE_STEPS", at.mode, n)

            every_pass(dve, one_pass)


_INS = ["x", "Wq", "Wk", "Wv", "Wb", "qc_w", "kc_w", "vc_w", "fir_s", "fir_l", "gW1", "gb1", "gW2", "gb2", "temp",
        "eps_floor", "onorm_w", "Wo"]
_FFN = ["w1", "b1", "w2", "b2"]


def kernel(**inputs):
    import numpy as _np
    import concourse.bacc as _bacc
    from concourse import mybir as _mybir
    from concourse.bass_utils import run_bass_kernel_spmd as _run

    nc = _bacc.Bacc("TRN2", target_bir_lowering=False, num_devices=1)
    arrays, args = {}, []
    for name in [f"L0_attn_{n}" for n in _INS] + [f"L0_ffn_{n}" for n in _FFN]:
        a = _np.ascontiguousarray(inputs[name])
        arrays[f"in_{name}"] = a
        args.append(nc.dram_tensor(f"in_{name}", a.shape, _mybir.dt.from_np(a.dtype), kind="ExternalInput").ap())
    args.append(nc.dram_tensor("out_0", (SEQS, T, C), _mybir.dt.float32, kind="ExternalOutput").ap())
    macaron_kernel(nc, *args)
    r = _run(nc, [arrays], core_ids=[0])
    return r.results[0]["out_0"]
```

```python
from contextlib import ExitStack

import concourse.bass as bass
from concourse import mybir

F32 = mybir.dt.float32
F32R = mybir.dt.float32r
ALU = mybir.AluOpType
ACT = mybir.ActivationFunctionType
AX = mybir.AxisListType

SEQS, T, C = 8, 512, 256
P = 128
TILES = T // P
HALVES = C // P
HEADS, D = 4, 64
HID = 1024
KT = HID // P
CHUNK = 32
CPT = P // CHUNK
UNITS = TILES * HEADS
BR = 4
CONV = 4
GROUPS = C // 32
LONG, SHORT = 31, 3
TAPG = 8
PAD = 4 * (TAPG - 1)
RING = 2


def macaron_kernel(nc, x, Wq, Wk, Wv, Wb, qc_w, kc_w, vc_w, fir_s, fir_l, gW1, gb1, gW2, gb2,
                   temp, eps_floor, onorm_w, Wo, w1, b1, w2, b2, out):
    ctx = ExitStack()
    with ctx:
        def sb(name, shape, dt=F32):
            return ctx.enter_context(nc.sbuf_tensor(name, shape, dt))

        def sem(name):
            return ctx.enter_context(nc.semaphore(name))

        l_dram = nc.dram_tensor("l_dram", [CPT, CHUNK, UNITS, CHUNK], F32, kind="Internal").ap()
        t_dram = nc.dram_tensor("t_dram", [CPT, UNITS, CHUNK, CHUNK], F32, kind="Internal").ap()
        v_dram = nc.dram_tensor("v_dram", [HALVES, P, T], F32, kind="Internal").ap()

        ident = sb("ident", [P, P])
        low_strict = sb("low_strict", [P, CHUNK])
        up_incl = sb("up_incl", [P, CHUNK])
        eye32 = sb("eye32", [P, CHUNK])
        w1_hi, w1_lo = sb("w1_hi", [P, HALVES, HID], F32R), sb("w1_lo", [P, HALVES, HID], F32R)
        w2_hi, w2_lo = sb("w2_hi", [P, KT, C], F32R), sb("w2_lo", [P, KT, C], F32R)
        wqkv_hi, wqkv_lo = sb("wqkv_hi", [P, 3, HALVES, C], F32R), sb("wqkv_lo", [P, 3, HALVES, C], F32R)
        wo_hi, wo_lo = sb("wo_hi", [P, HALVES, C], F32R), sb("wo_lo", [P, HALVES, C], F32R)
        wh_hi, wh_lo = sb("wh_hi", [P, HALVES, P], F32R), sb("wh_lo", [P, HALVES, P], F32R)
        b1_col = sb("b1_col", [P, KT])
        b2_half = sb("b2_half", [P, C])
        wb_pad = sb("wb_pad", [P, HALVES, 32])
        conv_col = sb("conv_col", [P, 3, HALVES, CONV])
        fir_w = sb("fir_w", [P, GROUPS, TAPG + 1, 32])
        gate_w = sb("gate_w", [P, 3, P])
        gate_st = sb("gate_st", [2 * 32, HEADS, P])
        kq_sel = sb("kq_sel", [P, HALVES, 32])
        gb1_col = sb("gb1_col", [P, 1])
        w2g_pad = sb("w2g_pad", [P, 2, 32])
        temp_col, tinv_col, gb2_col, gbt_col = (sb(n, [P, 1]) for n in ("temp_col", "tinv_col", "gb2_col", "gbt_col"))
        floor_b = sb("floor_b", [P, HEADS, BR])
        onorm_col = sb("onorm_col", [P, 1])

        arena = sb("arena", [P, 8, TILES * C])
        flat = arena[:, :, :].rearrange("p a b -> p (a b)")
        w1_st = flat[:, 0:2048].rearrange("p (k n) -> p k n", k=HALVES)
        w2_st = flat[:, 2048:4096].rearrange("p (k n) -> p k n", k=KT)
        wqkv_st = flat[:, 4096:5632].rearrange("p (w k n) -> p w k n", w=3, k=HALVES)
        wo_st = flat[:, 5632:6144].rearrange("p (k n) -> p k n", k=HALVES)
        wh_st = flat[:, 6144:6400].rearrange("p (k n) -> p k n", k=HALVES)
        b2_st = flat[:, 6400:6656]

        def units(n, slots):
            return arena[:, n:n + slots, :].rearrange("p a (b d) -> p (a b) d", d=D)

        k_tok = arena[:, 0, :].rearrange("p (t c) -> p t c", t=TILES)
        dv_tok = flat[:, 1024:3072].rearrange("p (u s d) -> p u s d", u=UNITS, s=2)
        f_tok = flat[:, 3072:5120].rearrange("p (u s d) -> p u s d", u=UNITS, s=2)
        sq = arena[:, 5, :].rearrange("p (n t) -> p n t", n=2)
        sq_u = arena[:, 5, :].rearrange("p (u d) -> p u d", u=UNITS)
        l_inv = arena[0:CPT * UNITS, 6, :].rearrange("p (i j) -> p i j", i=CHUNK)
        xn_tok = arena[:, 7, :].rearrange("p (t c) -> p t c", t=TILES)
        xn_u = arena[:, 7, :].rearrange("p (u d) -> p u d", u=UNITS)

        x_in = sb("x_in", [P, TILES, C])
        x1_tok = sb("x1_tok", [P, TILES, C])
        x2_tok = sb("x2_tok", [P, TILES, C])
        xt_hi, xt_lo = sb("xt_hi", [P, HALVES, T], F32R), sb("xt_lo", [P, HALVES, T], F32R)
        bn, mv_all = sb("bn", [P, TILES, 6]), sb("mv_all", [P, 2, TILES, 2])
        std_all, rstd = sb("std_all", [P, 2, TILES]), sb("rstd", [P, TILES])
        mv = [mv_all[:, n > 0] for n in range(3)]
        std = [std_all[:, n > 0] for n in range(3)]
        h_f = sb("h_f", [P, 2, T])
        h_hi, h_lo = sb("h_hi", [P, RING, T], F32R), sb("h_lo", [P, RING, T], F32R)
        conv_acc = sb("conv_acc", [P, 2, T])
        qk_fm = sb("qk_fm", [P, HALVES, 2, T])
        wv = sb("wv", [P, 4, T])
        w_fm = wv[:, 0:2, :]
        v_fm = wv[:, 2:4, :]
        dv_fm = [wv[:, 0, :], wv[:, 1, :], arena[:, 6, 0:T], arena[:, 6, T:2 * T]]
        v_shift = sb("v_shift", [P, GROUPS, PAD + T])
        f_fm = sb("f_fm", [P, HEADS, T])
        rows_fm = sb("rows_fm", [96, T])
        rows_tok = sb("rows_tok", [P, 3, UNITS])
        nrm, inv = sb("nrm", [P, 2, UNITS]), sb("inv", [P, 2, UNITS])
        c1, c2n = sb("c1", [P, UNITS]), sb("c2n", [P, UNITS])
        l_tok = sb("l_tok", [P, UNITS, CHUNK])
        u_t = l_tok
        at_tok = sb("at_tok", [P, UNITS, CHUNK])
        l_prod = sb("l_prod", [CPT * UNITS, (CHUNK // 2) ** 2])
        t_tok = sb("t_tok", [P, UNITS, CHUNK])
        u1, u2n = sb("u1", [P, UNITS, CHUNK]), sb("u2n", [P, UNITS, CHUNK])
        s_sb = sb("s_sb", [P, HALVES, D])
        du = sb("du", [P, 2, HALVES, D])
        ms_tok, mx_tok = sb("ms_tok", [P, UNITS + HEADS, BR]), sb("mx_tok", [P, UNITS + HEADS, BR])
        stat_fm = sb("stat_fm", [P, T])
        lg_fm = stat_fm
        hid_fm = sb("hid_fm", [P, T])
        pre = h_f
        hm = sb("hm", [P, 2, T])
        lg = sb("lg", [P, UNITS, BR])
        lmax, lsum, linv = (sb(n, [P, UNITS]) for n in ("lmax", "lsum", "linv"))
        mix_w = sb("mix_w", [P, UNITS, BR])
        oss, onrm, oinv = (sb(n, [P, UNITS]) for n in ("oss", "onrm", "oinv"))
        stat_rows = [x2_tok[0:D, :, :].rearrange("d t (s n) -> d (t s) n", n=P),
                     hm[0:D, :, :].rearrange("d a (s n) -> d (a s) n", n=P)]

        def stat_row(n):
            return stat_rows[n // 8][:, n % 8, :]

        taps_l = f_fm[:, 0, 0:GROUPS * (LONG + 1)].rearrange("p (g n) -> p g n", g=GROUPS)
        taps_s = f_fm[:, 1, 0:GROUPS * CONV].rearrange("p (g n) -> p g n", g=GROUPS)
        wv_flat = wv[:, :, :].rearrange("p a t -> p (a t)")
        stat_sel = wv_flat[0:D, 0:4 * BR * 2 * 32].rearrange("p (b m) -> p b m", m=2 * 32)
        mean_sel = wv[0:D, 3, 0:2 * P].rearrange("p (a m) -> p a m", a=2)
        stat_all = wv[0:2 * 32, 3, 2 * P:4 * P].rearrange("p (a m) -> p a m", a=2)
        head_mask = qk_fm[0:2 * 32, 0, 0, 0:HEADS]

        psum = ctx.enter_context(nc.psum_tensor("psum", [P, 8, 512], F32))
        BANKS = [psum[:, n, :] for n in range(8)]
        filled = [sem(f"filled{n}") for n in range(8)]
        emptied = [sem(f"emptied{n}") for n in range(8)]
        STATE = 7

        RECUR = [("du", (5, 6)), ("o", (0, 1) * TILES), ("state", (STATE,))]
        FFN_A = [("upa", (2, 3) + (2,) * (KT - 2)), ("outa", (3, 4))]
        STATS = [("dv_t", (0, 1, 5, 6)), ("stat", (2,)), ("gate", (7, 0, 1, 5))]
        LN2 = [("ln2", (6, 3)), ("k", (4, 2)), ("q", (6, 3)), ("v", (4, 2)), ("hidden", (3,))]
        K_Q = [("k_t", (7, 0)), ("rows", (6,)), ("gram", (7, 0)), ("rows_t", (6,))]
        LOGIT = [("logit", (4,)), ("logit_t", (4,))]
        FIR = [("fir", (2, 1, 5, 3))]
        MIX = [("mix_t", (6, 4)), ("wo", (7, 0))]
        V_T = [("v_t", (2, 1)), ("f_t", (5, 3, 6, 4))]
        FFN_C = [("ln3", (2, 1)), ("upc", (1, 7) * (KT // 2)), ("outc", (3, 4))]
        NEXT = [("next", (2, 0))]
        W = [("w", (0, 5, 2, 6))]
        first = [("next", (2, 6)), ("upa", (2, 0) * (KT // 2)), ("outa", (3, 4)), ("sums", (5, 1))]
        front = [LN2, K_Q, FIR, V_T]
        back = [RECUR, STATS, LOGIT, MIX, FFN_C]
        both = [RECUR, FFN_A, STATS, LN2, K_Q, LOGIT, FIR, MIX, V_T, FFN_C]
        ORDER = {"head": sum(front + [W, NEXT], first), "body": sum(both + [W, NEXT], []),
                 "last": sum(both + [W], []), "tail": sum(back, [])}
        ORDER = {m: [(w, k, b) for w, bs in o for k, b in enumerate(bs)] for m, o in ORDER.items()}
        QUIET = ("du", "state")

        class Pass:

            def __init__(self, mode, i=None):
                self.mode = mode
                self.i = None if mode == "head" else i
                self.j = 0 if mode == "head" else None if mode == "tail" else i + 1
                self.front, self.back = mode != "tail", mode != "head"
                self.next = mode in ("head", "body")

            def count(self, per):
                if self.mode == "head":
                    return 0
                if self.mode == "body":
                    return per("head") + self.i * per("body")
                return per("head") + (SEQS - 2) * per("body") + (per("last") if self.mode == "tail" else 0)

        def content(at, what, k):
            order = ORDER[at.mode]
            if what == "first":
                n = k
            else:
                n = [n for n, u in enumerate(order) if u[:2] == (what, k)][-1]
            b = order[n][2]
            uses = sum(u[2] == b for u in order[:n + 1])
            fills = sum(u[2] == b and u[0] not in QUIET for u in order[:n + 1])
            return b, at.count(lambda m: sum(u[2] == b for u in ORDER[m])) + uses, \
                at.count(lambda m: sum(u[2] == b and u[0] not in QUIET for u in ORDER[m])) + fills

        def claim(pe, at, what, k=0):
            b, uses, _ = content(at, what, k)
            pe.wait_ge(emptied[b], uses)
            return BANKS[b], filled[b]

        def where(at, what, k=0):
            b, _, _ = content(at, what, k)
            return BANKS[b], filled[b]

        def arrive(eng, at, what, k=0):
            b, _, fills = content(at, what, k)
            eng.wait_ge(filled[b], fills)
            return BANKS[b], emptied[b]

        def copied(eng, at, what, k=0):
            b, uses, _ = content(at, what, k)
            eng.wait_ge(emptied[b], uses + 1)

        ffn_loaded = sem("ffn_loaded")
        w_loaded = sem("w_loaded")
        c_loaded = sem("c_loaded")
        const_made = sem("const_made")
        setup_dve = sem("setup_dve")
        x_loaded = sem("x_loaded")
        y_stored = sem("y_stored")
        bias1_added = sem("bias1_added")
        x2_begun = sem("x2_begun")
        bias2_added = sem("bias2_added")
        var_made = [sem(f"var_made{n}") for n in range(3)]
        std_made = [sem(f"std_made{n}") for n in range(3)]
        xn_made = [sem(f"xn_made{n}") for n in range(3)]
        next_ready = sem("next_ready")
        xhi_made = [sem(f"xhi_made{n}") for n in range(4)]
        h_split = [sem(f"h_split{n}") for n in range(2)]
        h_used = [sem(f"h_used{n}") for n in range(2)]
        x1_made = sem("x1_made")
        y_made = sem("y_made")
        tap_made = sem("tap_made")
        conv_made = sem("conv_made")
        silu_made = sem("silu_made")
        v_stored = sem("v_stored")
        v_shifted = sem("v_shifted")
        kq_squared = sem("kq_squared")
        nrm_made = sem("nrm_made")
        kqroot_made = sem("kqroot_made")
        l_made = sem("l_made")
        l_stored, l_loaded = sem("l_stored"), sem("l_loaded")
        inverted = sem("inverted")
        t_stored, t_loaded = sem("t_stored"), sem("t_loaded")
        u_made = sem("u_made")
        du_ready = sem("du_ready")
        du_made = sem("du_made")
        s_ready = sem("s_ready")
        s_made = sem("s_made")
        dl_made = sem("dl_made")
        stat_squared = sem("stat_squared")
        stat_used = sem("stat_used")
        max_made = sem("max_made")
        mean_made = sem("mean_made")
        stat_made = sem("stat_made")
        pre_made = sem("pre_made")
        hm_made = sem("hm_made")
        hm_used = sem("hm_used")
        lshift_made = sem("lshift_made")
        exp_made = sem("exp_made")
        mix_made = sem("mix_made")
        mix_squared = sem("mix_squared")
        onrm_made = sem("onrm_made")
        oroot_made = sem("oroot_made")
        norm_made = sem("norm_made")
        passed = sem("passed")
        dve_step = sem("dve_step")
        CHUNKS = TILES * CPT
        INV_STEPS = 2 * (CHUNK - 2)
        DVE_STEPS = {"head": 49, "body": 82, "last": 77, "tail": 38}
        CONST_MADE, C_LOADED, SETUP_DVE = 59, 57, 30
        ZEROED, IDENT_MADE = 5, 7
        SETUP_FFN, SETUP_LARGE = 5, 24

        x_v = x.rearrange("b (t p) c -> b p t c", p=P)
        out_v = out.rearrange("b (t p) c -> b p t c", p=P)

        def every_pass(eng, one_pass):
            one_pass(Pass("head"))
            with eng.Fori(0, SEQS - 2) as i:
                one_pass(Pass("body", i))
            one_pass(Pass("last", SEQS - 2))
            one_pass(Pass("tail", SEQS - 1))

        block = ctx.enter_context(nc.Block())

        @block.sync
        def _(sp):
            sp.sem_inc(y_stored, 1)
            loads = 0

            def load(dst, src, **kw):
                nonlocal loads
                loads += 1
                sp.dma_start(dst, src, **kw).then_inc(c_loaded, 16)

            def load_x(n):
                src = x_v[n:n + 1] if isinstance(n, int) else x_v[bass.ds(n, 1)]
                sp.dma_start(x_in[:, :, :], src.rearrange("a p t c -> (a p) t c")).then_inc(x_loaded, 16)

            load_x(0)
            sp.dma_start(w1_st, w1.rearrange("(k p) n -> p k n", p=P)).then_inc(ffn_loaded, 16)
            sp.dma_start(b1_col[:, :], b1.rearrange("(k p) -> p k", p=P), allow_slow_non_contiguous=True).then_inc(ffn_loaded, 16)
            sp.dma_start(w2_st, w2.rearrange("(k p) n -> p k n", p=P)).then_inc(ffn_loaded, 16)
            sp.dma_start(b2_st, b2.partition_broadcast(P)).then_inc(ffn_loaded, 16)
            for n, w in enumerate((Wk, Wq, Wv)):
                sp.dma_start(wqkv_st[:, n], w.rearrange("(k p) n -> p k n", p=P)).then_inc(w_loaded, 16)
            sp.dma_start(wh_st, gW1[0:C, :].rearrange("(k p) n -> p k n", p=P)).then_inc(w_loaded, 16)
            sp.dma_start(wo_st, Wo.rearrange("(k p) n -> p k n", p=P)).then_inc(w_loaded, 16)
            sp.wait_ge(const_made, ZEROED)
            load(gb1_col[:, :], gb1.rearrange("(p a) -> p a", a=1))
            for n, w in enumerate((kc_w, qc_w, vc_w)):
                load(conv_col[:, n], w.rearrange("(h p) j -> p h j", p=P))
            for s in range(CONV):
                rows = slice(32 * s, 32 * s + 32)
                load(taps_l[rows, :, 1:LONG + 1], fir_l.rearrange("h d j -> (h d) j").rearrange("(g c) j -> c g j", c=32))
                load(taps_s[rows, :, 1:SHORT + 1], fir_s.rearrange("h d j -> (h d) j").rearrange("(g c) j -> c g j", c=32))
            rows = gW1[C:C + 3 * BR * D, :].rearrange("(s d) n -> d s n", d=D)
            load(stat_rows[0], rows[:, 0:8, :])
            load(stat_rows[1][:, 0:BR, :], rows[:, 8:, :])
            br_rows = gW1[C + 3 * BR * D:, :].rearrange("(s d) n -> s d n", d=D)
            for n, pair in enumerate(((0, 1), (1, 0), (2, 3))):
                for half, b in enumerate(pair):
                    load(gate_w[D * half:D * half + D, n, :], br_rows[b])
            for h in range(HEADS):
                load(temp_col[32 * h:32 * h + 32, :], temp[h:h + 1].partition_broadcast(32))
                swap = (1, 0) if h % 2 else (0, 1)
                for slot, b in enumerate(swap):
                    load(gb2_col[32 * h + slot:32 * h + slot + 1, :], gb2[b:b + 1].rearrange("(p a) -> p a", a=1))
                    load(floor_b[:, h, slot:slot + 1], eps_floor[h, b:b + 1].partition_broadcast(P),
                         allow_slow_non_contiguous=True)
                load(gb2_col[32 * h + 2:32 * h + 4, :], gb2[2:4].rearrange("(p a) -> p a", a=1))
                load(floor_b[:, h, 2:4], eps_floor[h, 2:4].partition_broadcast(P))
            for h in range(2):
                load(onorm_col[D * h:D * h + D, :], onorm_w.rearrange("(p a) -> p a", a=1))
            load(wb_pad[:, :, 0:HEADS], Wb.rearrange("(k p) n -> p k n", p=P))
            for par in range(2):
                load(w2g_pad[:, par, 2:4], gW2[:, 2:4])
                for slot, b in enumerate((1, 0) if par else (0, 1)):
                    load(w2g_pad[:, par, slot:slot + 1], gW2[:, b:b + 1], allow_slow_non_contiguous=True)
            assert loads == C_LOADED, ("C_LOADED", loads)
            sp.wait_ge(const_made, CONST_MADE)

            def one_pass(at):
                if at.front:
                    j = at.j
                    if at.next:
                        sp.wait_ge(x1_made, 2 * j + 2)
                        load_x(j + 1)
                    sp.wait_ge(silu_made, 6 * j + 6)
                    sp.dma_start(v_dram.rearrange("h p t -> p h t"), v_fm).then_inc(v_stored, 16)
                    sp.wait_ge(v_stored, 16 * j + 16)
                    for s in range(CONV):
                        sp.dma_start(v_shift[32 * s:32 * s + 32, :, PAD + s:PAD + T],
                                     v_dram.rearrange("h (g c) t -> c (h g) t", c=32)[:, :, 0:T - s]).then_inc(v_shifted, 16)
                    sp.wait_ge(l_made, j + 1)
                    sp.dma_start(l_dram.rearrange("c i u j -> (c i) u j"), l_tok[:, :, :]).then_inc(l_stored, 16)
                    sp.wait_ge(l_stored, 16 * j + 16)
                    for c in range(CPT):
                        sp.dma_start(l_inv[UNITS * c:UNITS * c + UNITS, :, :],
                                     l_dram[c].rearrange("i u j -> u i j")).then_inc(l_loaded, 16)
                    sp.wait_ge(inverted, INV_STEPS * j + INV_STEPS)
                    sp.dma_start(t_dram.rearrange("c u i j -> (c u) i j"), l_inv[:, :, :]).then_inc(t_stored, 16)
                    sp.wait_ge(t_stored, 16 * j + 16)
                    for c in range(CPT):
                        sp.dma_start(t_tok[32 * c:32 * c + 32, :, :], t_dram[c].rearrange("u i j -> i u j")).then_inc(t_loaded, 16)
                if at.back:
                    i = at.i
                    sp.wait_ge(y_made, 2 * i + 2)
                    dst = out_v[i:i + 1] if isinstance(i, int) else out_v[bass.ds(i, 1)]
                    sp.dma_start(dst.rearrange("a p t c -> (a p) t c"), x2_tok[:, :, :]).then_inc(y_stored, 16)

            every_pass(sp, one_pass)
            sp.wait_ge(y_stored, SEQS * 16 + 1)

        @block.gpsimd
        def _(pool):
            made = 0

            def make(ins):
                nonlocal made
                made += 1
                ins.then_inc(const_made, 1)
                pool.wait_ge(const_made, made)

            for t, v in ((taps_l, 0.0), (taps_s, 0.0), (wb_pad[:, :, :], 0.0), (w2g_pad[:, :, :], 0.0),
                         (gb2_col[:, :], 0.0)):
                make(pool.memset(t, v))
            assert made == ZEROED
            make(pool.memset(ident[:, :], 0.0))
            make(pool.affine_select(out=ident[:, :], in_=ident[:, :], compare_op=ALU.not_equal, fill=1.0, base=0,
                                    pattern=[[-1, P]], channel_multiplier=1))
            assert made == IDENT_MADE
            for t, v in ((low_strict[:, :], 1.0), (up_incl[:, :], 1.0), (eye32[:, :], 0.0),
                         (stat_sel, 0.0), (mean_sel, 0.0), (head_mask, 0.0), (v_shift[:, :, :], 0.0),
                         (kq_sel[:, :, :], 0.0), (ms_tok[:, :, :], 0.0), (mx_tok[:, :, :], 0.0)):
                make(pool.memset(t, v))
            for c in range(CPT):
                rows = slice(32 * c, 32 * c + 32)
                make(pool.affine_select(out=low_strict[rows, :], in_=low_strict[rows, :], compare_op=ALU.is_gt, fill=0.0,
                                        base=0, pattern=[[-1, CHUNK]], channel_multiplier=1))
                make(pool.affine_select(out=up_incl[rows, :], in_=up_incl[rows, :], compare_op=ALU.is_ge, fill=0.0,
                                        base=0, pattern=[[1, CHUNK]], channel_multiplier=-1))
                make(pool.affine_select(out=eye32[rows, :], in_=eye32[rows, :], compare_op=ALU.not_equal, fill=1.0,
                                        base=0, pattern=[[-1, CHUNK]], channel_multiplier=1))
            for half in range(2):
                part = slice(D * half, D * half + D)
                make(pool.memset(mean_sel[:, half, part], 1.0 / D))
                for hh in range(HALVES):
                    make(pool.memset(kq_sel[part, hh, 2 * hh + half:2 * hh + half + 1], 1.0))
            for par in range(2):
                for st in range(2):
                    for slot in range(BR):
                        rows = stat_sel[:, BR * (2 * par + st) + slot, 32 * st:32 * st + BR * HEADS]
                        make(pool.memset(rows.rearrange("d (h s) -> d h s", s=BR)[:, :, slot:slot + 1], 1.0))
            for n in range(2):
                for slot in range(BR):
                    make(pool.affine_select(out=head_mask, in_=head_mask, compare_op=ALU.not_equal, fill=1.0,
                                            base=-(32 * n + slot), pattern=[[-BR, HEADS]], channel_multiplier=1))
            assert made == CONST_MADE, ("CONST_MADE", made)
            bias = b2_half[:, :].unsqueeze(1).broadcast_to([P, TILES, C])
            pool.wait_ge(setup_dve, SETUP_FFN)

            def one_pass(at):
                if at.back:
                    pool.wait_ge(y_stored, 16 * at.i + 1)
                    pool.wait_ge(x1_made, 2 * at.i + 2)
                    pool.sem_inc(passed, 1)
                    pool.tensor_copy(x2_tok[:, :, :], x1_tok[:, :, :]).then_inc(x2_begun, 1)
                    pool.wait_ge(x2_begun, at.i + 1)
                if at.front:
                    j = at.j
                    pool.wait_ge(x_loaded, 16 * j + 16)
                    pool.wait_ge(xn_made[0], j + 1)
                    pool.tensor_tensor(x_in[:, :, :], x_in[:, :, :], bias, ALU.add).then_inc(bias1_added, 1)
                    pool.wait_ge(bias1_added, j + 1)
                    pool.wait_ge(l_loaded, 64 * j + 64)
                    n = 0
                    for k in range(1, CHUNK - 1):
                        below = CHUNK - 1 - k
                        shape = [CPT * UNITS, below, k]
                        prod = l_prod[:, 0:below * k].rearrange("p (i j) -> p i j", i=below)
                        pool.tensor_tensor(prod, l_inv[:, k + 1:, k:k + 1].broadcast_to(shape),
                                           l_inv[:, k:k + 1, 0:k].broadcast_to(shape), ALU.mult).then_inc(inverted, 1)
                        n += 1
                        pool.wait_ge(inverted, INV_STEPS * j + n)
                        pool.tensor_tensor(l_inv[:, k + 1:, 0:k], l_inv[:, k + 1:, 0:k], prod, ALU.add).then_inc(inverted, 1)
                        n += 1
                        pool.wait_ge(inverted, INV_STEPS * j + n)
                    assert n == INV_STEPS
                if at.back:
                    pool.wait_ge(xn_made[2], at.i + 1)
                    pool.tensor_tensor(x2_tok[:, :, :], x2_tok[:, :, :], bias, ALU.add).then_inc(bias2_added, 1)
                    pool.wait_ge(bias2_added, at.i + 1)

            every_pass(pool, one_pass)

        @block.scalar
        def _(act):
            act.wait_ge(ffn_loaded, 4 * 16)

            def root(n, seq):
                act.wait_ge(var_made[n], seq + 1)
                act.activation(std[n], std[n], ACT.Sqrt).then_inc(std_made[n], 1)

            def high(at, n, seq, what):
                for h in range(HALVES):
                    bank, _ = arrive(act, at, what, h)
                    act.activation(xt_hi[:, h, :], bank, ACT.Copy).then_inc(xhi_made[n], 1)

            def gelu(at, f, seq, m):
                bank, read = arrive(act, at, ("upa", "upc")[f], m)
                if m >= 2:
                    act.wait_ge(h_split[f], KT * seq + m - 1)
                act.activation(h_f[:, m % 2, :], bank, ACT.Gelu, bias=b1_col[:, m:m + 1]).then_inc(read, 1)

            def out_of(at, what, k, dst, func=ACT.Copy, src=None, **kw):
                bank, read = arrive(act, at, what, k)
                act.activation(dst, bank if src is None else src(bank), func, **kw).then_inc(read, 1)

            def stat_square(at, n):
                t, us = n // 2, slice(HEADS * (n // 2), HEADS * (n // 2) + HEADS)
                if n % 2:
                    act.wait_ge(dl_made, TILES * at.i + t + 1)
                if n >= 2:
                    act.wait_ge(stat_used, 2 * TILES * at.i + n - 1)
                src = (dv_tok if n % 2 else f_tok)[:, us, :, :].rearrange("p u s d -> p (u s d)")
                act.activation(sq[:, n % 2, :], src, ACT.Square).then_inc(stat_squared, 1)

            SQUARE_BEHIND = (3, 5, 7, 9, 11, 13, 14)
            after_state = {0: 0, 1: 1, 2: 2, 4: 3, 6: 4, 8: 5, 10: 6, 12: 7}

            def one_pass(at):
                i, j = at.i, at.j

                def tap(m):
                    bank, _ = arrive(act, at, "kqv"[m // 2], m % 2)
                    if m >= 2:
                        act.wait_ge(silu_made, 6 * j + m - 1)
                    act.activation(conv_acc[:, m % 2, :], bank, ACT.Identity,
                                   scale=conv_col[:, m // 2, m % 2, CONV - 1:CONV]).then_inc(tap_made, 1)

                def silu(m):
                    act.wait_ge(conv_made, 6 * j + m + 1)
                    dst = qk_fm[:, m % 2, m // 2, :] if m < 4 else v_fm[:, m % 2, :]
                    act.activation(dst, conv_acc[:, m % 2, :], ACT.Silu).then_inc(silu_made, 1)

                if at.back:
                    for n in range(CHUNKS - 1):
                        act.wait_ge(s_ready, (CHUNKS - 1) * i + n + 1)
                        act.activation(s_sb[:, :, :], BANKS[STATE][:, 0:HALVES * D].rearrange("p (h d) -> p h d", h=HALVES),
                                       ACT.Copy).then_inc(s_made, 1)
                        if at.front and n in after_state:
                            gelu(at, 0, j, after_state[n])
                        if n in SQUARE_BEHIND:
                            stat_square(at, SQUARE_BEHIND.index(n))
                    act.wait_ge(s_made, (CHUNKS - 1) * (i + 1))
                    act.sem_inc(emptied[STATE], 1)
                    for h in range(HEADS):
                        out_of(at, "dv_t", h, dv_fm[h])
                else:
                    root(0, j)
                    high(at, 0, j, "first")
                    for m in range(KT):
                        gelu(at, 0, j, m)
                if at.front:
                    root(1, j)
                if at.back:
                    stat_square(at, 2 * TILES - 1)
                    act.wait_ge(mean_made, i + 1)
                    act.activation(stat_fm[0:32, :], stat_fm[0:32, :], ACT.Sqrt).then_inc(stat_made, 1)
                if at.front:
                    high(at, 1, j, "ln2")
                    if not at.back:
                        act.wait_ge(c_loaded, C_LOADED * 16)
                    tap(0)
                    tap(1)
                    for m in range(4):
                        silu(m)
                        tap(m + 2)
                    act.wait_ge(silu_made, 6 * j + 4)
                    for n in range(4):
                        dst = sq[:, n % 2, :] if n < 2 else hm[:, n % 2, :]
                        act.activation(dst, qk_fm[:, n % 2, n // 2, :], ACT.Square).then_inc(kq_squared, 1)
                    silu(4)
                    for t in range(2):
                        out_of(at, "k_t", t, arena[:, 0, 512 * t:512 * t + 512])
                    silu(5)
                    rows, read = arrive(act, at, "rows")
                    act.activation(rows_fm[0:64, :], rows[0:64, :], ACT.Copy)
                    act.activation(rows_fm[64:96, :], rows[64:96, :], ACT.Sigmoid).then_inc(read, 1)
                    act.wait_ge(nrm_made, j + 1)
                    act.activation(nrm[:, :, :], nrm[:, :, :], ACT.Sqrt).then_inc(kqroot_made, 1)
                if at.back:
                    for h in range(HEADS):
                        act.wait_ge(pre_made, HEADS * i + h + 1)
                        if h >= 2:
                            act.wait_ge(hm_used, (HEADS - 1) * i + h - 1)
                        act.activation(hm[:, h % 2, :], pre[:, h % 2, :], ACT.Gelu, bias=gb1_col[:, 0:1]).then_inc(hm_made, 1)
                if at.front:
                    out_of(at, "hidden", 0, hid_fm[:, :])
                if at.back:
                    out_of(at, "logit", 0, lg_fm[:, :], ACT.Identity, bias=gbt_col[:, 0:1], scale=tinv_col[:, 0:1])
                if at.back:
                    act.wait_ge(lshift_made, i + 1)
                    act.activation(lg[:, :, :], lg[:, :, :], ACT.Exp).then_inc(exp_made, 1)
                if at.front:
                    for h in range(2):
                        out_of(at, "fir", h, f_fm[:, h, :])
                if at.back:
                    act.wait_ge(mix_made, i + 1)
                    act.activation(sq_u, f_tok[:, :, 0, :], ACT.Square).then_inc(mix_squared, 1)
                if at.back:
                    act.wait_ge(onrm_made, i + 1)
                    act.activation(onrm[:, :], onrm[:, :], ACT.Sqrt).then_inc(oroot_made, 1)
                if at.next:
                    root(0, j + 1)
                if at.back:
                    high(at, 3, i, "mix_t")
                if at.front:
                    for h in range(2, HEADS):
                        out_of(at, "fir", h, f_fm[:, h, :])
                    for b in range(2):
                        out_of(at, "v_t", b, dv_tok[:, 8 * b:8 * b + 8, 1, :], src=lambda k: k.rearrange("p (u d) -> p u d", d=D))
                    for t in range(TILES):
                        out_of(at, "f_t", t, f_tok[:, HEADS * t:HEADS * t + HEADS, :, :],
                               src=lambda k: k.rearrange("p (u s d) -> p u s d", s=2, d=D))
                if at.back:
                    root(2, i)
                    high(at, 2, i, "ln3")
                    for m in range(KT):
                        gelu(at, 1, i, m)
                if at.next:
                    high(at, 0, j + 1, "next")
                if at.mode == "head":
                    act.wait_ge(setup_dve, SETUP_DVE)

            every_pass(act, one_pass)

        def product3(pe, dst, a_hi, a_lo, b_hi, b_lo, first, last, **kw):
            pe.matmul(dst, a_hi, b_hi, start=first, stop=False, **kw)
            pe.matmul(dst, a_hi, b_lo, start=False, stop=False, **kw)
            return pe.matmul(dst, a_lo, b_hi, start=False, stop=last, **kw)

        @block.tensor
        def _(pe):
            pe.wait_ge(const_made, IDENT_MADE)

            def gate_sums(at):
                pe.wait_ge(const_made, CONST_MADE)
                pe.wait_ge(c_loaded, C_LOADED * 16)
                bank, full = claim(pe, at, "sums", 0)
                for n, pair in enumerate(((0, 1), (1, 0), (2, 3))):
                    for half, b in enumerate(pair):
                        last = pe.matmul(bank[:, P * n:P * n + P], mean_sel[:, half, :], stat_row(3 * b), start=(half == 0),
                                         stop=(half == 1))
                last.then_inc(full, 1)
                bank, full = claim(pe, at, "sums", 1)
                for par in range(2):
                    slots = (1, 0, 2, 3) if par else (0, 1, 2, 3)
                    for n in range(2 * BR):
                        last = pe.matmul(bank[0:64, P * par:P * par + P], stat_sel[:, 2 * BR * par + n, :],
                                         stat_row(3 * slots[n % BR] + 1 + n // BR), start=(n == 0), stop=(n == 2 * BR - 1))
                last.then_inc(full, 1)

            def turn(at, what, k, src):
                bank, full = claim(pe, at, what, k)
                for n in range(4):
                    last = pe.transpose(bank[:, P * n:P * n + P], src(n), ident[:, :])
                last.then_inc(full, 1)

            def turn_rows(at, what, made, count):
                pe.wait_ge(made, count)
                for h in range(HALVES):
                    turn(at, what, h, lambda t: xn_tok[:, t, P * h:P * h + P])

            def to_tok(at, what, src):
                for t in range(2):
                    turn(at, what, t, lambda n: src(n % 2)[:, P * (2 * t + n // 2):P * (2 * t + n // 2) + P])

            STEPS = [("up", m, k) for m in (0, 1) for k in range(2)]
            for m in range(2, KT):
                STEPS += [("up", m, k) for k in range(2)] + [("down", m - 2, k) for k in range(2)]
            STEPS += [("down", m, k) for m in (KT - 2, KT - 1) for k in range(2)]

            def ffn_step(at, f, seq, n):
                kind, m, k = STEPS[n]
                up, outs = ("upa", "outa") if f == 0 else ("upc", "outc")
                if kind == "up":
                    bank, full = claim(pe, at, up, m) if k == 0 else where(at, up, m)
                    if m == 0 and k == 0 and f == 0:
                        pe.wait_ge(next_ready, seq + 1)
                    elif m == 0 and k == 0:
                        copied(pe, at, "ln3", 0)
                        copied(pe, at, "ln3", 1)
                    cols = slice(P * m, P * m + P)
                    last = product3(pe, bank, w1_hi[:, k, cols], w1_lo[:, k, cols], xt_hi[:, k, :], xt_lo[:, k, :],
                                    k == 0, k == HALVES - 1)
                    if k == HALVES - 1:
                        last.then_inc(full, 1)
                else:
                    if k == 0:
                        pe.wait_ge(h_split[f], KT * seq + m + 1)
                    bank, full = claim(pe, at, outs, k) if m == 0 else where(at, outs, k)
                    for t in (2 * k, 2 * k + 1):
                        last = product3(pe, bank[:, C * (t % 2):C * (t % 2) + C], h_hi[:, m % RING, P * t:P * t + P],
                                        h_lo[:, m % RING, P * t:P * t + P], w2_hi[:, m, :], w2_lo[:, m, :],
                                        m == 0 and t % 2 == 0, m == KT - 1, skip_group_check=True)
                    if m == KT - 1:
                        last.then_inc(full, 1)
                    elif k == 1:
                        last.then_inc(h_used[f], 1)

            by_head = [(2 * half + p, p, half, slice(D * p, D * p + D), slice(D * half, D * half + D))
                       for half in range(HALVES) for p in range(2)]

            def chunk(at, t, c, pu, po, o_full):
                i = at.i
                rows = slice(32 * c, 32 * c + 32)
                cols_t = slice(P * t + CHUNK * c, P * t + CHUNK * c + CHUNK)
                n = CPT * t + c
                pe.sem_inc(passed, 1)
                for h, p, half, part, cols in by_head:
                    last = pe.matmul(pu[p][rows, cols], u1[rows, HEADS * t + h, :], dv_tok[rows, HEADS * t + h, 1, :],
                                     start=(half == 0), stop=(n == 0), skip_group_check=True)
                if n > 0:
                    pe.wait_ge(s_made, (CHUNKS - 1) * i + n)
                    pe.sem_inc(passed, 1)
                    for h, p, half, part, cols in by_head:
                        last = pe.matmul(pu[p][rows, cols], w_fm[part, half, cols_t], s_sb[part, half, :],
                                         start=False, stop=True, skip_group_check=True)
                last.then_inc(du_ready, 1)
                if n > 0:
                    for h, p, half, part, cols in by_head:
                        pe.matmul(po[p][rows, cols], qk_fm[part, half, 1, cols_t], s_sb[part, half, :],
                                  start=(half == 0), stop=False, skip_group_check=True)
                if at.front:
                    ffn_step(at, 0, at.j, 2 * n)
                pe.wait_ge(du_made, CHUNKS * i + n + 1)
                if n < CHUNKS - 1:
                    for h, p, half, part, cols in by_head:
                        last = pe.matmul(BANKS[STATE][part, cols], k_tok[rows, t, D * h:D * h + D],
                                         du[rows, p, half, :], start=(n == 0 and half == 0), stop=(n == CHUNKS - 2),
                                         skip_group_check=True)
                    last.then_inc(s_ready, 1)
                else:
                    pe.sem_inc(passed, 1)
                for h, p, half, part, cols in by_head:
                    last = pe.matmul(po[p][rows, cols], at_tok[rows, HEADS * t + h, :], du[rows, p, half, :],
                                     start=(n == 0 and half == 0), stop=True, skip_group_check=True)
                    if c == CPT - 1 and half == HALVES - 1:
                        last.then_inc(o_full[p], 1)
                if at.front:
                    ffn_step(at, 0, at.j, 2 * n + 1)

            def projection(at, what, m, which):
                bank, full = claim(pe, at, what, m)
                cols = slice(P * m, P * m + P)
                for k in range(HALVES):
                    last = product3(pe, bank, wqkv_hi[:, which, k, cols], wqkv_lo[:, which, k, cols], xt_hi[:, k, :],
                                    xt_lo[:, k, :], k == 0, k == HALVES - 1)
                last.then_inc(full, 1)

            def gate_branches(at, h):
                bank, _ = claim(pe, at, "gate", h)
                pe.matmul(bank, gate_w[:, h % 2, :], f_fm[:, h, :], start=True, stop=False)
                pe.matmul(bank, gate_w[:, 2, :], dv_fm[h], start=False, stop=False)

            def gate_stats(at, h):
                bank, full = where(at, "gate", h)
                pe.matmul(bank, gate_st[:, h, :], stat_fm[0:64, :], start=False, stop=True).then_inc(full, 1)

            def k_and_q(at):
                j = at.j
                pe.wait_ge(silu_made, 6 * j + 4)
                to_tok(at, "k_t", lambda h: qk_fm[:, h, 0, :])
                bank, full = claim(pe, at, "rows")
                for k in range(HALVES):
                    for n, part in enumerate((xt_hi, xt_lo)):
                        pe.matmul(bank[64:96, :], wb_pad[:, k, :], part[:, k, :].bitcast(F32), start=(k + n == 0),
                                  stop=(k + n == 2))
                for n in range(4):
                    pe.wait_ge(kq_squared, 4 * j + n + 1)
                    rows = slice(32 * (n // 2), 32 * (n // 2) + 32)
                    squares = sq[:, n % 2, :] if n < 2 else hm[:, n % 2, :]
                    last = pe.matmul(bank[rows, :], kq_sel[:, n % 2, :], squares, start=(n % 2 == 0), stop=(n % 2 == 1),
                                     skip_group_check=True)
                last.then_inc(full, 1)
                grams = [claim(pe, at, "gram", b) for b in range(2)]
                pe.sem_inc(passed, 1)
                for u in range(UNITS // 2):
                    t, half = u // HALVES, u % HALVES
                    for c in range(CPT):
                        cols = slice(P * t + CHUNK * c, P * t + CHUNK * c + CHUNK)
                        for b in range(2):
                            rows = slice(D * b, D * b + D)
                            last = pe.matmul(grams[b][0][32 * c:32 * c + 32, D * u:D * u + D], qk_fm[rows, half, 0, cols],
                                             qk_fm[rows, half, :, cols], start=True, stop=True)
                            if u == UNITS // 2 - 1 and c == CPT - 1:
                                last.then_inc(grams[b][1], 1)
                copied(pe, at, "rows")
                bank, full = claim(pe, at, "rows_t")
                for t in range(TILES):
                    last = pe.transpose(bank[:, 96 * t:96 * t + 96], rows_fm[:, P * t:P * t + P], ident[0:96, 0:96])
                last.then_inc(full, 1)

            def firs(at, a, between=None):
                banks = [claim(pe, at, "fir", 2 * a + p) for p in range(2)]
                for n in [TAPG] + list(range(TAPG)):
                    if n == 4 and between:
                        between()
                    for p in range(2):
                        for g in range(2):
                            col = D * (p if n == TAPG else 1 - p) + 32 * g
                            group = 2 * (2 * a + p) + g
                            at_t = PAD if n == TAPG else 4 * n
                            last = pe.matmul(banks[p][0][col:col + 32, :], fir_w[:, group, n, :],
                                             v_shift[:, group, at_t:at_t + T], start=(n in (0, TAPG)), stop=(n >= TAPG - 1))
                        if n == TAPG - 1:
                            last.then_inc(banks[p][1], 1)

            def one_pass(at):
                i, j = at.i, at.j
                if at.back:
                    pu = [claim(pe, at, "du", p)[0] for p in range(2)]
                    claim(pe, at, "state")

                    for t in range(TILES):
                        po, o_full = zip(*[claim(pe, at, "o", 2 * t + p) for p in range(2)])
                        for c in range(CPT):
                            chunk(at, t, c, pu, po, o_full)
                else:
                    turn_rows(at, "first", xn_made[0], j + 1)
                    pe.wait_ge(setup_dve, SETUP_FFN)
                    for n in range(len(STEPS)):
                        ffn_step(at, 0, j, n)
                    gate_sums(at)
                if at.back:
                    pe.wait_ge(dl_made, TILES * i + TILES)
                    for h in range(HEADS):
                        turn(at, "dv_t", h, lambda t: dv_tok[:, HEADS * t + h, :, :].rearrange("p s d -> p (s d)"))
                    copied(pe, at, "dv_t", HEADS - 1)
                    gate_branches(at, 0)
                    gate_branches(at, 1)
                    pe.wait_ge(max_made, i + 1)
                    bank, full = claim(pe, at, "stat")
                    for n, src in enumerate((ms_tok, mx_tok)):
                        src = src[:, :, :].rearrange("p u s -> p (u s)")
                        for t in range(TILES):
                            last = pe.matmul(bank[32 * n:32 * n + 32, P * t:P * t + P],
                                             src[:, BR * HEADS * t:BR * HEADS * t + 32], ident[:, :], start=True, stop=True)
                    last.then_inc(full, 1)
                if at.front:
                    turn_rows(at, "ln2", xn_made[1], j + 1)
                if at.back:
                    gate_branches(at, 2)
                if at.front:
                    copied(pe, at, "ln2", 0)
                    copied(pe, at, "ln2", 1)
                    if not at.back:
                        pe.wait_ge(setup_dve, SETUP_LARGE)
                    for m in range(2):
                        projection(at, "k", m, 0)
                    for m in range(2):
                        projection(at, "q", m, 1)
                if at.back:
                    pe.wait_ge(stat_made, i + 1)
                    for h in range(HEADS - 1):
                        gate_stats(at, h)
                    gate_branches(at, 3)
                    gate_stats(at, 3)
                if at.front:
                    for m in range(2):
                        projection(at, "v", m, 2)
                    bank, full = claim(pe, at, "hidden")
                    for k in range(HALVES):
                        last = product3(pe, bank, wh_hi[:, k, :], wh_lo[:, k, :], xt_hi[:, k, :], xt_lo[:, k, :],
                                        k == 0, k == HALVES - 1)
                    last.then_inc(full, 1)
                    k_and_q(at)
                if at.back:
                    bank, full = claim(pe, at, "logit")
                    for h in range(HEADS):
                        pe.wait_ge(hm_made, HEADS * i + h + 1)
                        last = pe.matmul(bank[32 * h:32 * h + 32, :], w2g_pad[:, h % 2, :], hm[:, h % 2, :],
                                         start=True, stop=True)
                        last.then_inc(hm_used if h < HEADS - 1 else full, 1)
                    copied(pe, at, "logit")
                    turn(at, "logit_t", 0, lambda t: lg_fm[:, P * t:P * t + P])

                def mix_to_fm():
                    pe.wait_ge(norm_made, i + 1)
                    for h in range(HALVES):
                        turn(at, "mix_t", h, lambda t: xn_tok[:, t, P * h:P * h + P])

                if at.front:
                    pe.wait_ge(v_shifted, 64 * j + 64)
                    if not at.back:
                        pe.wait_ge(inverted, 3 * INV_STEPS // 4)
                    firs(at, 0)
                    firs(at, 1, between=mix_to_fm if at.back else None)
                else:
                    mix_to_fm()
                if at.back:
                    copied(pe, at, "mix_t", 0)
                    copied(pe, at, "mix_t", 1)
                    for b in range(2):
                        bank, full = claim(pe, at, "wo", b)
                        for t in (2 * b, 2 * b + 1):
                            for k in range(HALVES):
                                rows = slice(P * t, P * t + P)
                                last = product3(pe, bank[:, C * (t % 2):C * (t % 2) + C], xt_hi[:, k, rows], xt_lo[:, k, rows],
                                                wo_hi[:, k, :], wo_lo[:, k, :], k == 0, k == HALVES - 1)
                        last.then_inc(full, 1)
                if at.front:
                    to_tok(at, "v_t", lambda h: v_fm[:, h, :])
                    copied(pe, at, "fir", HEADS - 1)
                    for t in range(TILES):
                        turn(at, "f_t", t, lambda h: f_fm[:, h, P * t:P * t + P])
                w_at, next_at = 18, len(STEPS) - 4
                if at.back:
                    turn_rows(at, "ln3", xn_made[2], i + 1)
                    for n in range(w_at):
                        ffn_step(at, 1, i, n)
                if at.front:
                    pe.wait_ge(u_made, j + 1)
                    banks = [claim(pe, at, "w", c) for c in range(CPT)]
                    pe.sem_inc(passed, 1)
                    for t in range(TILES):
                        for half in range(HALVES):
                            cols = slice(D * (HALVES * t + half), D * (HALVES * t + half) + D)
                            for c in range(CPT):
                                rows = slice(32 * c, 32 * c + 32)
                                us = slice(HEADS * t + 2 * half, HEADS * t + 2 * half + 2)
                                last = pe.matmul(banks[c][0][:, cols], k_tok[rows, t, P * half:P * half + P],
                                                 u2n[rows, us, :].rearrange("p h j -> p (h j)"), start=True, stop=True)
                                if t == TILES - 1 and half == HALVES - 1:
                                    last.then_inc(banks[c][1], 1)
                if at.back:
                    for n in range(w_at, next_at):
                        ffn_step(at, 1, i, n)
                if at.next:
                    turn_rows(at, "next", xn_made[0], j + 2)
                if at.back:
                    for n in range(next_at, len(STEPS)):
                        ffn_step(at, 1, i, n)
                if at.front:
                    copied(pe, at, "v_t", 1)
                    for c in range(CPT):
                        copied(pe, at, "w", c)

            every_pass(pe, one_pass)

        @block.vector
        def _(dve):
            setup = 0

            def step(ins):
                nonlocal setup
                setup += 1
                ins.then_inc(setup_dve, 1)

            def settle():
                dve.wait_ge(setup_dve, setup)

            def split_weights(hi, lo, staged):
                dims = (slice(None),) * len(hi.shape)
                step(dve.tensor_copy(hi[dims], staged))
                settle()
                step(dve.tensor_tensor(lo[dims], staged, hi[dims].bitcast(F32), ALU.subtract))

            def fir_weights(s):
                rows = slice(32 * s, 32 * s + 32)
                shape = [32, GROUPS, TAPG, 32]
                e = eye32[rows, :].unsqueeze(1).broadcast_to([32, GROUPS * TAPG, 32]).rearrange("p (g n) c -> p g n c", g=GROUPS)
                tap = taps_l[rows, :, 3 - s:3 - s + 4 * (TAPG - 1) + 1:4]
                step(dve.tensor_tensor(fir_w[rows, :, 0:TAPG, :], e, tap.unsqueeze(3).broadcast_to(shape), ALU.mult))
                step(dve.tensor_tensor(fir_w[rows, :, TAPG, :], eye32[rows, :].unsqueeze(1).broadcast_to([32, GROUPS, 32]),
                                       taps_s[rows, :, 3 - s:4 - s].broadcast_to([32, GROUPS, 32]), ALU.mult))

            def small_weights():
                step(dve.tensor_scalar(temp_col[:, :], temp_col[:, :], 0.2, 10.0, ALU.max, ALU.min))
                settle()
                step(dve.reciprocal(tinv_col[:, :], temp_col[:, :]))
                settle()
                step(dve.tensor_tensor(gbt_col[:, :], gb2_col[:, :], tinv_col[:, :], ALU.mult))
                step(dve.tensor_scalar(floor_b[:, :, :], floor_b[:, :, :], 1e-7, 0.1, ALU.max, ALU.min))
                step(dve.tensor_scalar(wo_st, wo_st, onorm_col[:, 0:1], None, ALU.mult))
                settle()
                split_weights(wo_hi, wo_lo, wo_st)

            def gate_weights(at):
                bank, read = arrive(dve, at, "sums", 0)
                step(dve.tensor_tensor(gate_w[:, :, :], gate_w[:, :, :], bank[:, 0:3 * P].rearrange("p (b n) -> p b n", b=3),
                                       ALU.add))
                settle()
                dve.sem_inc(read, 1)
                bank, read = arrive(dve, at, "sums", 1)
                step(dve.tensor_copy(stat_all, bank[0:64, 0:2 * P].rearrange("p (b n) -> p b n", b=2)))
                settle()
                dve.sem_inc(read, 1)
                for h in range(HEADS):
                    step(dve.tensor_scalar(gate_st[:, h, :], stat_all[:, h % 2, :], head_mask[:, h:h + 1], None, ALU.mult))

            for bank in emptied:
                dve.sem_inc(bank, 1)

            MAX_BEHIND = (0, 1, 9, 14)
            SUM_BEHIND = (5, 7, 9, 11, 13)
            after_du = {2: 0, 4: 1, 5: 2, 6: 3, 8: 4, 10: 5, 12: 6, 13: 7}

            def one_pass(at):
                i, j = at.i, at.j
                links = at.count(lambda m: DVE_STEPS[m])
                n = 0

                def link(ins):
                    nonlocal n
                    n += 1
                    ins.then_inc(dve_step, 1)
                    dve.wait_ge(dve_step, links + n)

                def stats(k, src):
                    for t in range(TILES):
                        last = dve.bn_stats(bn[:, t, :], src[:, t, :])
                    link(last)
                    dve.sem_inc(passed, 1)
                    for t in range(TILES):
                        last = dve.bn_aggr(mv[k][:, t, :], bn[:, t, :])
                    link(last)
                    dve.tensor_scalar(std[k], mv[k][:, :, 1], 1e-5, None, ALU.add).then_inc(var_made[k], 1)

                def normalise(k, seq, src):
                    dve.wait_ge(std_made[k], seq + 1)
                    link(dve.reciprocal(rstd[:, :], std[k]))
                    for t in range(TILES):
                        last = dve.tensor_scalar(xn_tok[:, t, :], src[:, t, :], mv[k][:, t, 0:1], rstd[:, t:t + 1],
                                                 ALU.subtract, ALU.mult)
                    last.then_inc(xn_made[k], 1)

                def low(k, seq, what):
                    for h in range(HALVES):
                        bank, read = arrive(dve, at, what, h)
                        dve.wait_ge(xhi_made[k], 2 * seq + h + 1)
                        ins = dve.tensor_tensor(xt_lo[:, h, :], bank, xt_hi[:, h, :].bitcast(F32), ALU.subtract)
                        if k > 0:
                            ins.then_inc(read, 1)
                        else:
                            link(ins)
                            dve.sem_inc(read, 1)
                    if k == 0:
                        dve.sem_inc(next_ready, 1)

                def split(f, seq, m):
                    copied(dve, at, ("upa", "upc")[f], m)
                    if m >= RING:
                        dve.wait_ge(h_used[f], (KT - 1) * seq + m - RING + 1)
                    link(dve.tensor_copy(h_hi[:, m % RING, :], h_f[:, m % 2, :]))
                    dve.tensor_tensor(h_lo[:, m % RING, :], h_f[:, m % 2, :], h_hi[:, m % RING, :].bitcast(F32),
                                      ALU.subtract).then_inc(h_split[f], 1)

                def residual(what, dst, base, made=None):
                    for b in range(2):
                        bank, read = arrive(dve, at, what, b)
                        two = slice(2 * b, 2 * b + 2)
                        link(dve.scalar_tensor_tensor(out=dst[:, two, :], in0=bank.rearrange("p (t c) -> p t c", t=2),
                                                      scalar=0.5, in1=base[:, two, :], op0=ALU.mult, op1=ALU.add))
                        dve.sem_inc(read, 1)
                        dve.sem_inc(made, 1)

                def conv(m):
                    bank, read = arrive(dve, at, "kqv"[m // 2], m % 2)
                    w = conv_col[:, m // 2, m % 2, :]
                    acc = conv_acc[:, m % 2, :]
                    dve.wait_ge(tap_made, 6 * j + m + 1)
                    for s in range(1, CONV):
                        link(dve.scalar_tensor_tensor(out=acc[:, s:], in0=bank[:, 0:T - s], scalar=w[:, CONV - 1 - s:CONV - s],
                                                      in1=acc[:, s:], op0=ALU.mult, op1=ALU.add))
                    dve.sem_inc(read, 1)
                    dve.sem_inc(conv_made, 1)

                def stat_sum(n):
                    us, slots = slice(HEADS * (n // 2), HEADS * (n // 2) + HEADS), slice(2 * (n % 2), 2 * (n % 2) + 2)
                    dve.wait_ge(stat_squared, 2 * TILES * i + n + 1)
                    return dve.tensor_reduce(ms_tok[:, us, slots], sq[:, n % 2, :].rearrange("p (u s d) -> p u s d", s=2, d=D),
                                             AX.X, ALU.add).then_inc(stat_used, 1)

                def per_row(v, m):
                    return v.unsqueeze(2).broadcast_to([P, UNITS, m])

                if at.back:
                    for t in range(TILES):
                        for c in range(CPT):
                            rows = slice(32 * c, 32 * c + 32)
                            k = CPT * t + c
                            dve.wait_ge(du_ready, CHUNKS * i + k + 1)
                            dve.tensor_copy(du[rows, :, :, :], psum[rows, 5:7, 0:HALVES * D]
                                            .rearrange("p a (h d) -> p a h d", h=HALVES)).then_inc(du_made, 1)
                            if at.front and k in after_du:
                                split(0, j, after_du[k])
                            if k in MAX_BEHIND:
                                us = slice(HEADS * MAX_BEHIND.index(k), HEADS * MAX_BEHIND.index(k) + HEADS)
                                dve.tensor_reduce(mx_tok[:, us, 0:2], f_tok[:, us, :, :], AX.X, ALU.max)
                            if k in SUM_BEHIND and c < CPT - 1:
                                stat_sum(SUM_BEHIND.index(k))
                        reads = [arrive(dve, at, "o", 2 * t + p)[1] for p in range(2)]
                        us = slice(HEADS * t, HEADS * t + HEADS)
                        for p in range(2):
                            ins = dve.tensor_tensor(dv_tok[:, us, 0, :][:, p::2, :],
                                                    psum[:, p, 0:HALVES * D].rearrange("p (h d) -> p h d", h=HALVES),
                                                    inv[:, 1, us][:, p::2].unsqueeze(2).broadcast_to([P, HALVES, D]), ALU.mult)
                        link(ins)
                        for read in reads:
                            dve.sem_inc(read, 1)
                        dve.sem_inc(dl_made, 1)
                        if t < TILES - 1:
                            dve.tensor_reduce(mx_tok[:, us, 2:4], dv_tok[:, us, :, :], AX.X, ALU.max)
                        if k in SUM_BEHIND:
                            stat_sum(SUM_BEHIND.index(k))
                    dve.wait_ge(du_made, CHUNKS * i + CHUNKS)
                    for b in (5, 6):
                        dve.sem_inc(emptied[b], 1)
                else:
                    dve.wait_ge(x_loaded, 16)
                    stats(0, x_in)
                    normalise(0, j, x_in)
                    dve.wait_ge(ffn_loaded, 4 * 16)
                    split_weights(w1_hi, w1_lo, w1_st)
                    low(0, j, "first")
                    split_weights(w2_hi, w2_lo, w2_st)
                    step(dve.tensor_scalar(b2_half[:, :], b2_st, 0.5, None, ALU.mult))
                    assert setup == SETUP_FFN
                    for m in range(KT):
                        split(0, j, m)
                        if m == 0:
                            dve.wait_ge(w_loaded, 5 * 16)
                            split_weights(wqkv_hi, wqkv_lo, wqkv_st)
                        elif m == 1:
                            split_weights(wh_hi, wh_lo, wh_st)
                        elif m == 3:
                            dve.wait_ge(const_made, CONST_MADE)
                            dve.wait_ge(c_loaded, C_LOADED * 16)
                        if 3 <= m < 7:
                            fir_weights(m - 3)
                        elif m == 7:
                            small_weights()
                            assert setup == SETUP_LARGE, ("SETUP_LARGE", setup)
                if at.front:
                    dve.wait_ge(bias1_added, j + 1)
                    if at.back:
                        dve.wait_ge(x2_begun, i + 1)
                    residual("outa", x1_tok, x_in, x1_made)
                    stats(1, x1_tok)
                if at.back:
                    dve.tensor_reduce(mx_tok[:, us, 2:4], dv_tok[:, us, :, :], AX.X, ALU.max)
                    for k in range(len(SUM_BEHIND), 2 * TILES):
                        stat_sum(k)
                    dve.wait_ge(stat_used, 2 * TILES * i + 2 * TILES)
                    dve.sem_inc(max_made, 1)

                def hidden(h):
                    bank, read = arrive(dve, at, "gate", h)
                    if h >= 2:
                        dve.wait_ge(hm_made, HEADS * i + h - 1)
                    link(dve.tensor_tensor(pre[:, h % 2, :], bank, hid_fm[:, :], ALU.add))
                    dve.sem_inc(read, 1)
                    dve.sem_inc(pre_made, 1)

                def k_q_rows():
                    bank, read = arrive(dve, at, "rows_t")
                    for r in range(3):
                        ins = dve.tensor_copy(rows_tok[:, r, :].rearrange("p (t h) -> p t h", t=TILES),
                                              bank[:, 0:TILES * 96].rearrange("p (t r h) -> p t r h", t=TILES, r=3)[:, :, r, 0:HEADS])
                    link(ins)
                    dve.sem_inc(read, 1)
                    dve.tensor_scalar(nrm[:, :, :], rows_tok[:, 0:2, :], 1e-6, None, ALU.add).then_inc(nrm_made, 1)
                    dve.wait_ge(kqroot_made, j + 1)
                    link(dve.reciprocal(inv[:, :, :], nrm[:, :, :]))
                    link(dve.tensor_tensor(c1[:, :], rows_tok[:, 2, :], inv[:, 0, :], ALU.mult))
                    link(dve.scalar_tensor_tensor(out=c2n[:, :], in0=c1[:, :], scalar=-1.0, in1=inv[:, 0, :],
                                                  op0=ALU.mult, op1=ALU.mult))
                    for b in range(2):
                        bank, read = arrive(dve, at, "gram", b)
                        g = bank.rearrange("p (u a j) -> p u a j", u=UNITS // 2, a=2)
                        shape = [P, UNITS // 2, CHUNK]
                        link(dve.tensor_tensor(l_tok[:, b::2, :], g[:, :, 0, :], c2n[:, b::2].unsqueeze(2).broadcast_to(shape),
                                               ALU.mult))
                        dve.tensor_tensor(at_tok[:, b::2, :], g[:, :, 1, :], up_incl[:, :].unsqueeze(1).broadcast_to(shape),
                                          ALU.mult).then_inc(read, 1)
                    dve.tensor_tensor(l_tok[:, :, :], l_tok[:, :, :],
                                      low_strict[:, :].unsqueeze(1).broadcast_to([P, UNITS, CHUNK]), ALU.mult).then_inc(l_made, 1)

                if at.front:
                    normalise(1, j, x1_tok)
                if at.back:
                    bank, read = arrive(dve, at, "stat")
                    dve.tensor_copy(stat_fm[32:64, :], bank[32:64, :])
                    link(dve.tensor_scalar(stat_fm[0:32, :], bank[0:32, :], 1.0 / D, 1e-8, ALU.mult, ALU.max))
                    dve.sem_inc(read, 1)
                    dve.sem_inc(mean_made, 1)
                if at.front:
                    low(1, j, "ln2")
                    if not at.back:
                        gate_weights(at)
                        assert setup == SETUP_DVE, ("SETUP_DVE", setup)
                if at.front:
                    for m in range(4):
                        conv(m)
                if at.back:
                    hidden(0)
                    hidden(1)
                if at.front:
                    conv(4)
                    conv(5)
                    k_q_rows()
                if at.back:
                    hidden(2)
                    hidden(3)
                    bank, read = arrive(dve, at, "logit_t")
                    link(dve.tensor_copy(lg[:, :, :].rearrange("p (t h) b -> p t h b", t=TILES),
                                         bank.rearrange("p (t h b) -> p t h b", t=TILES, h=HEADS)[:, :, :, 0:BR]))
                    dve.sem_inc(read, 1)
                    link(dve.tensor_reduce(lmax[:, :], lg[:, :, :], AX.X, ALU.max))
                    dve.tensor_tensor(lg[:, :, :], lg[:, :, :], per_row(lmax[:, :], BR), ALU.subtract).then_inc(lshift_made, 1)
                    dve.wait_ge(exp_made, i + 1)
                    link(dve.tensor_reduce(lsum[:, :], lg[:, :, :], AX.X, ALU.add))
                    link(dve.reciprocal(linv[:, :], lsum[:, :]))
                    link(dve.tensor_tensor(lg[:, :, :], lg[:, :, :], per_row(linv[:, :], BR), ALU.mult))
                    rows = lg[:, :, :].rearrange("p (t h) b -> p t (h b)", t=TILES)
                    link(dve.tensor_tensor(rows, rows, floor_b[:, :, :].rearrange("p h b -> p (h b)").unsqueeze(1)
                                           .broadcast_to([P, TILES, HEADS * BR]), ALU.max))
                    link(dve.tensor_reduce(lsum[:, :], lg[:, :, :], AX.X, ALU.add))
                    link(dve.reciprocal(linv[:, :], lsum[:, :]))
                    link(dve.tensor_tensor(mix_w[:, :, :], lg[:, :, :], per_row(linv[:, :], BR), ALU.mult))
                    for src, s in ((f_tok, 0), (dv_tok, 2)):
                        link(dve.tensor_tensor(src[:, :, :, :], src[:, :, :, :],
                                               mix_w[:, :, s:s + 2].unsqueeze(3).broadcast_to([P, UNITS, 2, D]), ALU.mult))
                    link(dve.tensor_tensor(f_tok[:, :, :, :], f_tok[:, :, :, :], dv_tok[:, :, :, :], ALU.add))
                    dve.tensor_tensor(f_tok[:, :, 0, :], f_tok[:, :, 0, :], f_tok[:, :, 1, :], ALU.add).then_inc(mix_made, 1)
                if at.next:
                    dve.wait_ge(x_loaded, 16 * j + 32)
                    stats(0, x_in)
                if at.back:
                    dve.wait_ge(mix_squared, i + 1)
                    link(dve.tensor_reduce(oss[:, :], sq_u, AX.X, ALU.add))
                    dve.tensor_scalar(onrm[:, :], oss[:, :], 1.0 / D, 1e-5, ALU.mult, ALU.add).then_inc(onrm_made, 1)
                    dve.wait_ge(oroot_made, i + 1)
                    link(dve.reciprocal(oinv[:, :], onrm[:, :]))
                    dve.tensor_tensor(xn_u, f_tok[:, :, 0, :], per_row(oinv[:, :], D), ALU.mult).then_inc(norm_made, 1)
                    low(3, i, "mix_t")
                    dve.wait_ge(x2_begun, i + 1)
                    for b in range(2):
                        bank, read = arrive(dve, at, "wo", b)
                        two = slice(2 * b, 2 * b + 2)
                        link(dve.tensor_tensor(x2_tok[:, two, :], bank.rearrange("p (t c) -> p t c", t=2), x2_tok[:, two, :],
                                               ALU.add))
                        dve.sem_inc(read, 1)
                    stats(2, x2_tok)
                    normalise(2, i, x2_tok)
                    low(2, i, "ln3")
                if at.next:
                    normalise(0, j + 1, x_in)
                if at.back:
                    for m in range(3):
                        split(1, i, m)
                if at.front:
                    dve.wait_ge(t_loaded, 64 * j + 64)
                    link(dve.transpose(u_t[:, :, :].rearrange("p u j -> p (u j)"), t_tok[:, :, :].rearrange("p u j -> p (u j)")))
                    link(dve.tensor_tensor(u_t[:, :, :], u_t[:, :, :], eye32[:, :].unsqueeze(1).broadcast_to([P, UNITS, CHUNK]),
                                           ALU.add))
                    dve.tensor_tensor(u1[:, :, :], u_t[:, :, :], per_row(c1[:, :], CHUNK), ALU.mult)
                    dve.tensor_tensor(u2n[:, :, :], u_t[:, :, :], per_row(c2n[:, :], CHUNK), ALU.mult).then_inc(u_made, 1)
                if at.back:
                    for m in range(3, 5):
                        split(1, i, m)
                if at.front:
                    for c in range(CPT):
                        bank, read = arrive(dve, at, "w", c)
                        for p in range(2):
                            part = slice(D * p, D * p + D)
                            ins = dve.tensor_copy(
                                w_fm.rearrange("p h (t c j) -> p h t c j", t=TILES, c=CPT)[part, :, :, c, :],
                                bank[part, :].rearrange("p (t h q j) -> p h t q j", t=TILES, h=HALVES, q=2)[:, :, :, p, :])
                        ins.then_inc(read, 1)
                if at.back:
                    for m in range(5, KT):
                        split(1, i, m)
                if at.next:
                    low(0, j + 1, "next")
                if at.back:
                    dve.wait_ge(bias2_added, i + 1)
                    residual("outc", x2_tok, x2_tok, y_made)
                assert n == DVE_STEPS[at.mode], ("DVE_STEPS", at.mode, n)

            every_pass(dve, one_pass)


_INS = ["x", "Wq", "Wk", "Wv", "Wb", "qc_w", "kc_w", "vc_w", "fir_s", "fir_l", "gW1", "gb1", "gW2", "gb2", "temp",
        "eps_floor", "onorm_w", "Wo"]
_FFN = ["w1", "b1", "w2", "b2"]


def kernel(**inputs):
    import numpy as _np
    import concourse.bacc as _bacc
    from concourse import mybir as _mybir
    from concourse.bass_utils import run_bass_kernel_spmd as _run

    nc = _bacc.Bacc("TRN2", target_bir_lowering=False, num_devices=1)
    arrays, args = {}, []
    for name in [f"L0_attn_{n}" for n in _INS] + [f"L0_ffn_{n}" for n in _FFN]:
        a = _np.ascontiguousarray(inputs[name])
        arrays[f"in_{name}"] = a
        args.append(nc.dram_tensor(f"in_{name}", a.shape, _mybir.dt.from_np(a.dtype), kind="ExternalInput").ap())
    args.append(nc.dram_tensor("out_0", (SEQS, T, C), _mybir.dt.float32, kind="ExternalOutput").ap())
    macaron_kernel(nc, *args)
    r = _run(nc, [arrays], core_ids=[0])
    return r.results[0]["out_0"]
```
